# Optimizing a Trainium2 kernel written in Bass

```python
import numpy as np
import jax
import jax.numpy as jnp

def _softmax(x, axis=-1):
    return jax.nn.softmax(x, axis=axis)

def _gelu(x):
    return jax.nn.gelu(x, approximate=True)

def _silu(x):
    return jax.nn.silu(x)

def _sigmoid(x):
    return jax.nn.sigmoid(x)

def _layernorm(x, axis=-1, eps=1e-05):
    m = jnp.mean(x, axis=axis, keepdims=True)
    v = jnp.var(x, axis=axis, keepdims=True)
    return (x - m) / jnp.sqrt(v + eps)

def _scatter_add(tgt, idx, src, axis=0):
    return tgt.at[idx].add(src)

def _segment_sum(src, seg, n):
    return jax.ops.segment_sum(src, seg, n)
kernel_name = 'mk_seq_preln_d1_jaxref_r8_32d78f'

def setup_inputs(seed: int=0):
    np.random.seed(seed)
    _w = jnp.asarray

    def _L0_attn_setup():
        import jax, jax.numpy as jnp
        import numpy as np
        B, S, D, H, NB = (2, 256, 128, 16, 32)
        DH = D // H
        MLP = 512
        CLUSTER_SCORE = 0.1
        LN_EPS = 1e-06

        def _layernorm(x, g, b):
            mu = jnp.mean(x, axis=-1, keepdims=True)
            var = jnp.mean(jnp.square(x - mu), axis=-1, keepdims=True)
            return (x - mu) * jax.lax.rsqrt(var + LN_EPS) * g + b

        def _lha_attention(x, Wq, Wk, Wv, Whq, Whk, Wo):
            q = jnp.einsum('bsd,dhf->bshf', x, Wq)
            k = jnp.einsum('bsd,dhf->bshf', x, Wk)
            v = jnp.einsum('bsd,dhf->bshf', x, Wv)
            qb = jax.nn.softmax(jnp.einsum('bshf,hfn->bshn', q, Whq), axis=-1)
            kb = jax.nn.softmax(jnp.einsum('bshf,hfn->bshn', k, Whk), axis=-1)
            logits = jnp.einsum('bqhf,bkhf->bhqk', q, k) / jnp.sqrt(jnp.float32(DH))
            aff = jnp.einsum('bqhn,bkhn->bhqk', qb, kb)
            logits = logits + CLUSTER_SCORE * aff
            attn = jax.nn.softmax(logits, axis=-1)
            out = jnp.einsum('bhqk,bkhf->bqhf', attn, v)
            out = jnp.einsum('bqhf,hfd->bqd', out, Wo)
            mq = jnp.mean(qb, axis=(0, 1))
            mk = jnp.mean(kb, axis=(0, 1))
            extra_loss = 0.5 * NB * (jnp.mean(jnp.sum(mq * mq, -1)) + jnp.mean(jnp.sum(mk * mk, -1)))
            return (out, extra_loss)

        def _reference_tuple_inner(inputs, ln1_g, ln1_b, Wq, Wk, Wv, Whq, Whk, Wo, ln2_g, ln2_b, W1, b1, W2, b2):
            x = _layernorm(inputs, ln1_g, ln1_b)
            attn_out, extra_loss = _lha_attention(x, Wq, Wk, Wv, Whq, Whk, Wo)
            x = attn_out + inputs
            y = _layernorm(x, ln2_g, ln2_b)
            y = jax.nn.relu(jnp.einsum('bsd,dm->bsm', y, W1) + b1)
            y = jnp.einsum('bsm,md->bsd', y, W2) + b2
            return (x + y, extra_loss)
        key = jax.random.key(seed)
        ks = jax.random.split(key, 10)
        std = 0.02
        return {'inputs': jax.random.normal(ks[0], (B, S, D), jnp.float32), 'ln1_g': jnp.ones((D,), jnp.float32), 'ln1_b': jnp.zeros((D,), jnp.float32), 'Wq': jax.random.normal(ks[1], (D, H, DH), jnp.float32) * std, 'Wk': jax.random.normal(ks[2], (D, H, DH), jnp.float32) * std, 'Wv': jax.random.normal(ks[3], (D, H, DH), jnp.float32) * std, 'Whq': jax.random.normal(ks[4], (H, DH, NB), jnp.float32) * std, 'Whk': jax.random.normal(ks[5], (H, DH, NB), jnp.float32) * std, 'Wo': jax.random.normal(ks[6], (H, DH, D), jnp.float32) * std, 'ln2_g': jnp.ones((D,), jnp.float32), 'ln2_b': jnp.zeros((D,), jnp.float32), 'W1': jax.random.normal(ks[7], (D, MLP), jnp.float32) * std, 'b1': jnp.zeros((MLP,), jnp.float32), 'W2': jax.random.normal(ks[8], (MLP, D), jnp.float32) * std, 'b2': jnp.zeros((D,), jnp.float32)}
    _L0_attn_in = _L0_attn_setup()

    def _L0_ffn_setup():
        import jax, jax.numpy as jnp
        import numpy as np
        DIM = 128
        DEPTH = 2
        HEADS = 8
        DIM_HEAD = 64
        WINDOW = 64
        INNER = HEADS * DIM_HEAD
        HID = int(DIM * 4 * 2 / 3)
        B, N = (2, 1024)
        QK_SCALE = 8.0

        def shift_token(t):
            t1, t2 = jnp.split(t, 2, axis=-1)
            t2 = jnp.pad(t2, ((0, 0), (1, 0), (0, 0)))[:, :-1]
            return jnp.concatenate([t1, t2], axis=-1)

        def l2norm(t):
            return t / jnp.clip(jnp.linalg.norm(t, axis=-1, keepdims=True), 1e-12)

        def rotate_half(x):
            x1, x2 = jnp.split(x, 2, axis=-1)
            return jnp.concatenate([-x2, x1], axis=-1)

        def rotary_xpos(q, k):
            n = q.shape[-2]
            half_idx = jnp.arange(0, DIM_HEAD, 2, dtype=jnp.float32)
            inv_freq = 1.0 / 10000.0 ** (half_idx / DIM_HEAD)
            t = jnp.arange(n, dtype=jnp.float32)
            freqs = t[:, None] * inv_freq[None, :]
            freqs = jnp.concatenate([freqs, freqs], axis=-1)
            base = (half_idx + 0.4 * DIM_HEAD) / (1.4 * DIM_HEAD)
            power = (t - n // 2) / float(WINDOW // 2)
            scale = base[None, :] ** power[:, None]
            scale = jnp.concatenate([scale, scale], axis=-1)
            cos, sin = (jnp.cos(freqs), jnp.sin(freqs))
            q = q * cos * scale + rotate_half(q) * sin * scale
            k = k * cos / scale + rotate_half(k) * sin / scale
            return (q, k)

        def local_attention(q, k, v):
            b, h, n, d = q.shape
            w = n // WINDOW
            bq = q.reshape(b, h, w, WINDOW, d) * QK_SCALE
            bk = k.reshape(b, h, w, WINDOW, d)
            bv = v.reshape(b, h, w, WINDOW, d)

            def look_around(t):
                p = jnp.pad(t, ((0, 0), (0, 0), (1, 0), (0, 0), (0, 0)))
                return jnp.concatenate([p[:, :, :w], p[:, :, 1:]], axis=3)
            bk, bv = (look_around(bk), look_around(bv))
            bt = jnp.arange(n).reshape(w, WINDOW)
            btp = jnp.pad(bt, ((1, 0), (0, 0)), constant_values=-1)
            btk = jnp.concatenate([btp[:w], btp[1:]], axis=1)
            sim = jnp.einsum('bhwid,bhwjd->bhwij', bq, bk)
            i = bt[:, :, None]
            j = btk[:, None, :]
            mask = (i < j) | (i > j + WINDOW) | (j == -1)
            sim = jnp.where(mask, -jnp.finfo(sim.dtype).max, sim)
            attn = jax.nn.softmax(sim, axis=-1)
            out = jnp.einsum('bhwij,bhwjd->bhwid', attn, bv)
            return out.reshape(b, h, n, d)

        def _layer(x, wqkv, qs, ksc, wo, lg, lb, w1, b1, w2, b2):
            b, n, _ = x.shape
            h = shift_token(x)
            qkv = h @ wqkv
            q, k, v = jnp.split(qkv, 3, axis=-1)
            to_heads = lambda t: t.reshape(b, n, HEADS, DIM_HEAD).transpose(0, 2, 1, 3)
            q, k, v = (to_heads(q), to_heads(k), to_heads(v))
            q = l2norm(q) * qs
            k = l2norm(k) * ksc
            q, k = rotary_xpos(q, k)
            o = local_attention(q, k, v)
            o = o.transpose(0, 2, 1, 3).reshape(b, n, INNER)
            x = x + o @ wo
            h = shift_token(x)
            mu = h.mean(-1, keepdims=True)
            var = h.var(-1, keepdims=True)
            h = (h - mu) / jnp.sqrt(var + 1e-05) * lg + lb
            h = h @ w1 + b1
            a, g = jnp.split(h, 2, axis=-1)
            h = a * jax.nn.gelu(g, approximate=False)
            x = x + h @ w2 + b2
            return x
        key = jax.random.key(seed)
        ks = jax.random.split(key, 6)
        return {'x': jax.random.normal(ks[0], (B, N, DIM), jnp.float32), 'wqkv': jax.random.normal(ks[1], (DEPTH, DIM, 3 * INNER), jnp.float32) * 0.02, 'q_scale': jnp.ones((DEPTH, DIM_HEAD), jnp.float32), 'k_scale': jnp.ones((DEPTH, DIM_HEAD), jnp.float32), 'wo': jax.random.normal(ks[2], (DEPTH, INNER, DIM), jnp.float32) * 0.02, 'ln_g': jnp.ones((DEPTH, DIM), jnp.float32), 'ln_b': jnp.zeros((DEPTH, DIM), jnp.float32), 'w1': jax.random.normal(ks[3], (DEPTH, DIM, 2 * HID), jnp.float32) * 0.02, 'b1': jnp.zeros((DEPTH, 2 * HID), jnp.float32), 'w2': jax.random.normal(ks[4], (DEPTH, HID, DIM), jnp.float32) * 0.02, 'b2': jnp.zeros((DEPTH, DIM), jnp.float32)}
    _L0_ffn_in = _L0_ffn_setup()
    _d = {'L0_attn_inputs': _L0_attn_in['inputs'], 'L0_attn_ln1_g': _L0_attn_in['ln1_g'], 'L0_attn_ln1_b': _L0_attn_in['ln1_b'], 'L0_attn_Wq': _L0_attn_in['Wq'], 'L0_attn_Wk': _L0_attn_in['Wk'], 'L0_attn_Wv': _L0_attn_in['Wv'], 'L0_attn_Whq': _L0_attn_in['Whq'], 'L0_attn_Whk': _L0_attn_in['Whk'], 'L0_attn_Wo': _L0_attn_in['Wo'], 'L0_attn_ln2_g': _L0_attn_in['ln2_g'], 'L0_attn_ln2_b': _L0_attn_in['ln2_b'], 'L0_attn_W1': _L0_attn_in['W1'], 'L0_attn_b1': _L0_attn_in['b1'], 'L0_attn_W2': _L0_attn_in['W2'], 'L0_attn_b2': _L0_attn_in['b2'], 'L0_ffn_wqkv': _L0_ffn_in['wqkv'], 'L0_ffn_q_scale': _L0_ffn_in['q_scale'], 'L0_ffn_k_scale': _L0_ffn_in['k_scale'], 'L0_ffn_wo': _L0_ffn_in['wo'], 'L0_ffn_ln_g': _L0_ffn_in['ln_g'], 'L0_ffn_ln_b': _L0_ffn_in['ln_b'], 'L0_ffn_w1': _L0_ffn_in['w1'], 'L0_ffn_b1': _L0_ffn_in['b1'], 'L0_ffn_w2': _L0_ffn_in['w2'], 'L0_ffn_b2': _L0_ffn_in['b2']}
    _x0 = _d['L0_attn_inputs']
    _d['L0_attn_inputs'] = jax.random.normal(jax.random.fold_in(jax.random.key(seed), 1), (8, 512, 128), dtype=_x0.dtype)
    del _x0
    return _d

def reference(L0_attn_inputs, L0_attn_ln1_g, L0_attn_ln1_b, L0_attn_Wq, L0_attn_Wk, L0_attn_Wv, L0_attn_Whq, L0_attn_Whk, L0_attn_Wo, L0_attn_ln2_g, L0_attn_ln2_b, L0_attn_W1, L0_attn_b1, L0_attn_W2, L0_attn_b2, L0_ffn_wqkv, L0_ffn_q_scale, L0_ffn_k_scale, L0_ffn_wo, L0_ffn_ln_g, L0_ffn_ln_b, L0_ffn_w1, L0_ffn_b1, L0_ffn_w2, L0_ffn_b2):

    def _L0_attn_ref(inputs, ln1_g, ln1_b, Wq, Wk, Wv, Whq, Whk, Wo, ln2_g, ln2_b, W1, b1, W2, b2):
        import jax, jax.numpy as jnp
        import numpy as np
        B, S, D, H, NB = (2, 256, 128, 16, 32)
        DH = D // H
        MLP = 512
        CLUSTER_SCORE = 0.1
        LN_EPS = 1e-06

        def _layernorm(x, g, b):
            mu = jnp.mean(x, axis=-1, keepdims=True)
            var = jnp.mean(jnp.square(x - mu), axis=-1, keepdims=True)
            return (x - mu) * jax.lax.rsqrt(var + LN_EPS) * g + b

        def _lha_attention(x, Wq, Wk, Wv, Whq, Whk, Wo):
            q = jnp.einsum('bsd,dhf->bshf', x, Wq)
            k = jnp.einsum('bsd,dhf->bshf', x, Wk)
            v = jnp.einsum('bsd,dhf->bshf', x, Wv)
            qb = jax.nn.softmax(jnp.einsum('bshf,hfn->bshn', q, Whq), axis=-1)
            kb = jax.nn.softmax(jnp.einsum('bshf,hfn->bshn', k, Whk), axis=-1)
            logits = jnp.einsum('bqhf,bkhf->bhqk', q, k) / jnp.sqrt(jnp.float32(DH))
            aff = jnp.einsum('bqhn,bkhn->bhqk', qb, kb)
            logits = logits + CLUSTER_SCORE * aff
            attn = jax.nn.softmax(logits, axis=-1)
            out = jnp.einsum('bhqk,bkhf->bqhf', attn, v)
            out = jnp.einsum('bqhf,hfd->bqd', out, Wo)
            mq = jnp.mean(qb, axis=(0, 1))
            mk = jnp.mean(kb, axis=(0, 1))
            extra_loss = 0.5 * NB * (jnp.mean(jnp.sum(mq * mq, -1)) + jnp.mean(jnp.sum(mk * mk, -1)))
            return (out, extra_loss)

        def _reference_tuple_inner(inputs, ln1_g, ln1_b, Wq, Wk, Wv, Whq, Whk, Wo, ln2_g, ln2_b, W1, b1, W2, b2):
            x = _layernorm(inputs, ln1_g, ln1_b)
            attn_out, extra_loss = _lha_attention(x, Wq, Wk, Wv, Whq, Whk, Wo)
            x = attn_out + inputs
            y = _layernorm(x, ln2_g, ln2_b)
            y = jax.nn.relu(jnp.einsum('bsd,dm->bsm', y, W1) + b1)
            y = jnp.einsum('bsm,md->bsd', y, W2) + b2
            return (x + y, extra_loss)
        return _reference_tuple_inner(inputs, ln1_g, ln1_b, Wq, Wk, Wv, Whq, Whk, Wo, ln2_g, ln2_b, W1, b1, W2, b2)[0]

    def _L0_ffn_ref(x, wqkv, q_scale, k_scale, wo, ln_g, ln_b, w1, b1, w2, b2):
        import jax, jax.numpy as jnp
        import numpy as np
        DIM = 128
        DEPTH = 2
        HEADS = 8
        DIM_HEAD = 64
        WINDOW = 64
        INNER = HEADS * DIM_HEAD
        HID = int(DIM * 4 * 2 / 3)
        B, N = (2, 1024)
        QK_SCALE = 8.0

        def shift_token(t):
            t1, t2 = jnp.split(t, 2, axis=-1)
            t2 = jnp.pad(t2, ((0, 0), (1, 0), (0, 0)))[:, :-1]
            return jnp.concatenate([t1, t2], axis=-1)

        def l2norm(t):
            return t / jnp.clip(jnp.linalg.norm(t, axis=-1, keepdims=True), 1e-12)

        def rotate_half(x):
            x1, x2 = jnp.split(x, 2, axis=-1)
            return jnp.concatenate([-x2, x1], axis=-1)

        def rotary_xpos(q, k):
            n = q.shape[-2]
            half_idx = jnp.arange(0, DIM_HEAD, 2, dtype=jnp.float32)
            inv_freq = 1.0 / 10000.0 ** (half_idx / DIM_HEAD)
            t = jnp.arange(n, dtype=jnp.float32)
            freqs = t[:, None] * inv_freq[None, :]
            freqs = jnp.concatenate([freqs, freqs], axis=-1)
            base = (half_idx + 0.4 * DIM_HEAD) / (1.4 * DIM_HEAD)
            power = (t - n // 2) / float(WINDOW // 2)
            scale = base[None, :] ** power[:, None]
            scale = jnp.concatenate([scale, scale], axis=-1)
            cos, sin = (jnp.cos(freqs), jnp.sin(freqs))
            q = q * cos * scale + rotate_half(q) * sin * scale
            k = k * cos / scale + rotate_half(k) * sin / scale
            return (q, k)

        def local_attention(q, k, v):
            b, h, n, d = q.shape
            w = n // WINDOW
            bq = q.reshape(b, h, w, WINDOW, d) * QK_SCALE
            bk = k.reshape(b, h, w, WINDOW, d)
            bv = v.reshape(b, h, w, WINDOW, d)

            def look_around(t):
                p = jnp.pad(t, ((0, 0), (0, 0), (1, 0), (0, 0), (0, 0)))
                return jnp.concatenate([p[:, :, :w], p[:, :, 1:]], axis=3)
            bk, bv = (look_around(bk), look_around(bv))
            bt = jnp.arange(n).reshape(w, WINDOW)
            btp = jnp.pad(bt, ((1, 0), (0, 0)), constant_values=-1)
            btk = jnp.concatenate([btp[:w], btp[1:]], axis=1)
            sim = jnp.einsum('bhwid,bhwjd->bhwij', bq, bk)
            i = bt[:, :, None]
            j = btk[:, None, :]
            mask = (i < j) | (i > j + WINDOW) | (j == -1)
            sim = jnp.where(mask, -jnp.finfo(sim.dtype).max, sim)
            attn = jax.nn.softmax(sim, axis=-1)
            out = jnp.einsum('bhwij,bhwjd->bhwid', attn, bv)
            return out.reshape(b, h, n, d)

        def _layer(x, wqkv, qs, ksc, wo, lg, lb, w1, b1, w2, b2):
            b, n, _ = x.shape
            h = shift_token(x)
            qkv = h @ wqkv
            q, k, v = jnp.split(qkv, 3, axis=-1)
            to_heads = lambda t: t.reshape(b, n, HEADS, DIM_HEAD).transpose(0, 2, 1, 3)
            q, k, v = (to_heads(q), to_heads(k), to_heads(v))
            q = l2norm(q) * qs
            k = l2norm(k) * ksc
            q, k = rotary_xpos(q, k)
            o = local_attention(q, k, v)
            o = o.transpose(0, 2, 1, 3).reshape(b, n, INNER)
            x = x + o @ wo
            h = shift_token(x)
            mu = h.mean(-1, keepdims=True)
            var = h.var(-1, keepdims=True)
            h = (h - mu) / jnp.sqrt(var + 1e-05) * lg + lb
            h = h @ w1 + b1
            a, g = jnp.split(h, 2, axis=-1)
            h = a * jax.nn.gelu(g, approximate=False)
            x = x + h @ w2 + b2
            return x
        for l in range(DEPTH):
            x = _layer(x, wqkv[l], q_scale[l], k_scale[l], wo[l], ln_g[l], ln_b[l], w1[l], b1[l], w2[l], b2[l])
        return x
    x = L0_attn_inputs
    x = x + _L0_attn_ref(_layernorm(x, axis=-1), L0_attn_ln1_g, L0_attn_ln1_b, L0_attn_Wq, L0_attn_Wk, L0_attn_Wv, L0_attn_Whq, L0_attn_Whk, L0_attn_Wo, L0_attn_ln2_g, L0_attn_ln2_b, L0_attn_W1, L0_attn_b1, L0_attn_W2, L0_attn_b2)
    x = x + _L0_ffn_ref(_layernorm(x, axis=-1), L0_ffn_wqkv, L0_ffn_q_scale, L0_ffn_k_scale, L0_ffn_wo, L0_ffn_ln_g, L0_ffn_ln_b, L0_ffn_w1, L0_ffn_b1, L0_ffn_w2, L0_ffn_b2)
    return x

_drawn_inputs = setup_inputs


def setup_inputs(seed=0):
    import zlib

    import numpy as np

    out = dict(_drawn_inputs(seed))
    spreads = {'L0_attn_ln1_g': (1.0, 0.6),
     'L0_attn_ln1_b': (0.0, 0.8),
     'L0_attn_ln2_g': (1.0, 0.6),
     'L0_attn_ln2_b': (0.0, 2.0),
     'L0_attn_b1': (0.0, 0.519),
     'L0_attn_b2': (0.0, 0.1),
     'L0_ffn_q_scale': (1.0, 0.6),
     'L0_ffn_k_scale': (1.0, 0.6),
     'L0_ffn_ln_g': (1.0, 0.6),
     'L0_ffn_ln_b': (0.0, 0.8),
     'L0_ffn_b1': (0.0, 0.8),
     'L0_ffn_b2': (0.0, 0.8)}
    factors = {'L0_attn_Wq': 8.0,
     'L0_attn_Wk': 8.0,
     'L0_attn_Wv': 8.0,
     'L0_attn_Whq': 64.0,
     'L0_attn_Whk': 64.0,
     'L0_attn_Wo': 8.0,
     'L0_ffn_wqkv': 5.492,
     'L0_ffn_wo': 5.439,
     'L0_ffn_w1': 8.0,
     'L0_ffn_w2': 8.0}
    for name, (base, spread) in spreads.items():
        noise = np.random.default_rng([zlib.crc32(name.encode()), seed]).standard_normal(out[name].shape)
        drawn = base * np.exp(spread * noise) if base else spread * noise
        out[name] = jnp.asarray(drawn.astype(out[name].dtype))
    for name, factor in factors.items():
        out[name] = (out[name] * factor).astype(out[name].dtype)
    return out
```

```python
from contextlib import ExitStack

import numpy as np

import concourse.bass as bass
from concourse import mybir

ALU = mybir.AluOpType
ACT = mybir.ActivationFunctionType
AX = mybir.AxisListType
F32 = mybir.dt.float32
F16 = mybir.dt.float16
BF16 = mybir.dt.bfloat16

P = 128
B, S, D = 8, 512, 128
DEPTH = 2
TPB = S // P
NT = B * TPB

H, DH, NB = 16, 8, 32
MLP = 512
SHIFT = 64.0

UNITS = 8
SLOTS = 4 * UNITS
PAIR = 2 * SLOTS
LEAD_SCORES = 2
LEAD_MAX = 13
LEAD_PREP = 40
FIRST_SLOT = -LEAD_PREP
LAST_SLOT = B * SLOTS + 6
LOOP_FROM = 8
LOOP_TURNS = 3
LOOP_TO = LOOP_FROM + LOOP_TURNS * PAIR
TILE_SLOTS = 5


def streams(n):
    s = {}
    x = n + LEAD_SCORES
    s["scores"] = x if 0 <= x < B * SLOTS else None
    x = n + LEAD_MAX
    s["max"] = x if 0 <= x < B * SLOTS else None
    s["exp"] = n if 0 <= n < B * SLOTS else None
    s["pv"] = n // 2 - 1 if n % 2 == 0 and 2 <= n <= B * SLOTS else None
    s["out"] = n // UNITS - 1 if n % UNITS == 0 and UNITS <= n <= B * SLOTS else None
    prep, k = (n + LEAD_PREP) // SLOTS, (n + LEAD_PREP) % SLOTS
    s["prep"] = [] if not 0 <= prep < B else [
        (prep * TPB + t, k - TILE_SLOTS * t) for t in range(TPB) if 0 <= k - TILE_SLOTS * t <= 11]
    return s


def bench_uses(n):
    s = streams(n)
    uses = []
    for step, at in (("stack_q0", 8), ("stack_q1", 9), ("stack_k0", 10), ("stack_k1", 11),
                     ("xn", 0), ("qkv", 1), ("clq", 2), ("clk", 3)):
        uses += [(step, tile) for tile, k in s["prep"] if k == at]
    x = n - UNITS - 1
    if x % UNITS == 0 and 0 <= x // UNITS < B * 4:
        uses.append(("heads_out", x // UNITS))
    x = n - SLOTS - 3
    if x % SLOTS == 0 and 0 <= x // SLOTS < B:
        uses.append(("att_t", x // SLOTS))
    x = n - SLOTS - 5
    if x % SLOTS == 0 and 0 <= x // SLOTS < B:
        uses.append(("proj", x // SLOTS))
    x = n + 5
    if x % UNITS == 0 and 0 <= x // UNITS < B * 4:
        uses.append(("shift", x // UNITS))
    return uses


STACKS = ("stack_q0", "stack_q1", "stack_k0", "stack_k1")
BENCH_ORDER = {}
for _n in range(FIRST_SLOT, LAST_SLOT):
    for _u in bench_uses(_n):
        BENCH_ORDER[(_n, _u)] = len(BENCH_ORDER)
BENCH_LIST = list(BENCH_ORDER)
BENCH_PER_PAIR = sum(len(bench_uses(n)) for n in range(LOOP_FROM, LOOP_FROM + PAIR))


def over_slots(eng, slot):
    for n in range(FIRST_SLOT, LOOP_FROM):
        slot(n, 0)
    with eng.Fori(0, LOOP_TURNS) as turn:
        for n in range(LOOP_FROM, LOOP_FROM + PAIR):
            slot(n, turn)
    for n in range(LOOP_TO, LAST_SLOT):
        slot(n, 0)


def before(n, use):
    order = BENCH_ORDER[(n, use)]
    return BENCH_LIST[order - 1][1] if order else None


def wait(eng, sem, count, turn=0, per_pair=0):
    if isinstance(turn, int):
        if count > 0:
            eng.wait_ge(sem, count)
    else:
        assert count >= 0
        eng.wait_ge(sem, turn * per_pair + count)


def tile_at(turn, tile):
    return tile if isinstance(turn, int) else turn * (2 * TPB) + tile


def build(nc, a, debug=None):
    with ExitStack() as ctx:
        a["semaphores"] = ctx

        def sb(name, shape, dt=F32, c=ctx):
            return c.enter_context(nc.sbuf_tensor(name, shape, dt))

        X = sb("X", [P, NT, D])
        Z = sb("Z", [P, NT, D])
        R1 = sb("R1", [P, NT])
        normalise_input(nc, a, X, Z, R1)
        clustered_attention(nc, a, Z, R1)
        if debug == "A":
            store_tokens(nc, a, Z)
            return
        mean = sb("mean", [P, NT])
        inv_dev = sb("inv_dev", [P, NT])
        token_moments(nc, a, Z, mean, inv_dev, 1e-6, "m2_")
        attention_mlp(nc, a, X, Z, mean, inv_dev)
        if debug == "M":
            store_tokens(nc, a, X)
            return
        token_moments(nc, a, X, mean, inv_dev, 1e-5, "m3_")
        XT = sb("XT", [P, B, S])
        VAR = sb("VAR", [P, B, S])
        turn_tokens(nc, a, X, mean, inv_dev, XT)
        for layer in range(DEPTH):
            taken = []

            def take(name):
                taken.append(nc.alloc_semaphore(name=name))
                return taken[-1]

            a["layer_semaphores"] = take
            local_attention(nc, a, layer, XT, Z[:].rearrange("p (b t) d -> p b (t d)", b=B), VAR)
            gated_ffn(nc, a, layer, XT, Z[:].rearrange("p (b t) d -> p b (t d)", b=B), VAR)
            clear(nc, taken)
            if debug == "L%d" % layer:
                break
        add_and_store(nc, a, X, XT)


def _np_of(dtype):
    return mybir.dt.np(dtype)


def layouts(inputs):
    i = {k: np.ascontiguousarray(v) for k, v in inputs.items()}
    eye = np.zeros((P, P), np.float32)
    eye[np.arange(P), np.arange(P)] = 1

    def hash_blocks(w):
        out = np.zeros((H, DH, H, NB), np.float32)
        for h in range(H):
            out[h, :, h, :] = w[h]
        return out.reshape(P, H * NB)

    a = {
        "x": i["L0_attn_inputs"], "ident": eye, "ident16": eye.astype(np.float16),
        "wq": i["L0_attn_Wq"].reshape(P, P), "wk": i["L0_attn_Wk"].reshape(P, P),
        "wv": i["L0_attn_Wv"].reshape(P, P),
        "wqT": np.ascontiguousarray(i["L0_attn_Wq"].reshape(P, P).T),
        "wkT": np.ascontiguousarray(i["L0_attn_Wk"].reshape(P, P).T),
        "whq": hash_blocks(i["L0_attn_Whq"]), "whk": hash_blocks(i["L0_attn_Whk"]),
        "wo": i["L0_attn_Wo"].reshape(P, P),
        "ln1_g": i["L0_attn_ln1_g"].reshape(P, 1), "ln1_b": i["L0_attn_ln1_b"].reshape(P, 1),
    }
    swap = np.r_[LD // 2:LD, 0:LD // 2]
    gains = np.stack([np.stack([g, g[:, swap]], 1) for g in (i["L0_ffn_q_scale"], i["L0_ffn_k_scale"])], 1)

    def chunks(v):
        out = np.zeros((DEPTH, P, 2, len(HC)), np.float32)
        for side in range(2):
            for n, (c, m) in enumerate(HC):
                out[:, :m, side, n] = v[:, side * HID + c:side * HID + c + m]
        return out.reshape(DEPTH, P, -1)

    a |= {
        "mlp_w1": i["L0_attn_W1"], "mlp_w2": i["L0_attn_W2"],
        "mlp_b1": np.ascontiguousarray(i["L0_attn_b1"].reshape(MLP // P, P).T),
        "ln2_g": i["L0_attn_ln2_g"].reshape(P, 1), "ln2_b": i["L0_attn_ln2_b"].reshape(P, 1),
        "mlp_b2_rows": np.ascontiguousarray(np.broadcast_to(i["L0_attn_b2"], (P, D))),
        "identb": eye.astype(_np_of(BF16)), "band": band_mask().astype(_np_of(BF16)),
        "mean_of": np.full((P, P), 1.0 / D, np.float32),
        "wqkv": i["L0_ffn_wqkv"], "lwo": i["L0_ffn_wo"], "rot": rotary_tables(),
        "gains": np.ascontiguousarray(np.broadcast_to(gains.reshape(DEPTH, 1, -1), (DEPTH, P, 4 * LD))),
        "fw1": i["L0_ffn_w1"], "fb1": chunks(i["L0_ffn_b1"]),
        "fln": np.ascontiguousarray(np.stack([i["L0_ffn_ln_g"], i["L0_ffn_ln_b"]], 2)),
        "fb2": i["L0_ffn_b2"].reshape(DEPTH, P, 1), "fw2": i["L0_ffn_w2"],
    }
    return a


def store_tokens(nc, a, src):
    with nc.semaphore("stored") as stored, nc.Block() as block:
        @block.sync
        def _(sp):
            sp.dma_start(a["out"].rearrange("b (t p) d -> p (b t) d", p=P), src[:]).then_inc(stored, 16)
            sp.wait_ge(stored, 16)


def normalise_input(nc, a, X, Z, R1):
    x_tiles = a["x"].rearrange("b (t p) d -> p b t d", p=P)
    with ExitStack() as ctx:
        def sb(name, shape, dt=F32):
            return ctx.enter_context(nc.sbuf_tensor(name, shape, dt))

        def sem(name):
            return a["semaphores"].enter_context(nc.semaphore(name))

        stats = sb("in_stats", [P, NT, 6])
        moments = sb("in_moments", [P, NT, 2])
        dev = sb("in_dev", [P, NT])
        r0 = sb("in_r0", [P, NT])
        var1 = sb("in_var1", [P, NT])
        dev1 = sb("in_dev1", [P, NT])
        eps = sb("in_eps", [P, 2])
        loaded = [sem(f"in_loaded{b}") for b in range(B)]
        stats_done = sem("in_stats_done")
        moments_done = sem("in_moments_done")
        eps_set = sem("in_eps_set")
        dev_done = sem("in_dev_done")
        r0_done = sem("in_r0_done")
        r0_sq_done = sem("in_r0_sq_done")
        var1_done = sem("in_var1_done")
        block = ctx.enter_context(nc.Block())

        @block.sync
        def _(sp):
            for b in range(B):
                sp.dma_start(X[:, b * TPB:(b + 1) * TPB, :], x_tiles[:, b]).then_inc(loaded[b], 16)

        @block.vector
        def _(dve):
            nc.vector.memset(eps[:, 0:1], 1e-5)
            nc.vector.memset(eps[:, 1:2], 1e-6).then_inc(eps_set, 1)
            for b in range(B):
                dve.wait_ge(loaded[b], 16)
                for t in range(b * TPB, (b + 1) * TPB):
                    nc.vector.bn_stats(stats[:, t, :], X[:, t, :]).then_inc(stats_done, 1)
                    if t:
                        dve.wait_ge(stats_done, t)
                        nc.vector.bn_aggr(moments[:, t - 1, :], stats[:, t - 1, :])
            dve.wait_ge(stats_done, NT)
            nc.vector.bn_aggr(moments[:, NT - 1, :], stats[:, NT - 1, :]).then_inc(moments_done, 1)
            dve.wait_ge(moments_done, 1)
            dve.wait_ge(dev_done, 1)
            nc.vector.reciprocal(r0[:], dev[:]).then_inc(r0_done, 1)
            dve.wait_ge(r0_done, 1)
            nc.vector.tensor_tensor(var1[:], r0[:], r0[:], ALU.mult).then_inc(r0_sq_done, 1)
            dve.wait_ge(r0_sq_done, 1)
            nc.vector.tensor_tensor(var1[:], var1[:], moments[:, :, 1], ALU.mult).then_inc(var1_done, 1)
            with dve.Fori(0, NT) as t:
                nc.vector.tensor_scalar(Z[:, bass.ds(t, 1), :].rearrange("p t d -> p (t d)"),
                                        X[:, bass.ds(t, 1), :].rearrange("p t d -> p (t d)"),
                                        moments[:, bass.ds(t, 1), 0], r0[:, bass.ds(t, 1)],
                                        ALU.subtract, ALU.mult)
            dve.wait_ge(dev_done, 2)
            nc.vector.reciprocal(R1[:], dev1[:])

        @block.scalar
        def _(act):
            act.wait_ge(eps_set, 1)
            act.wait_ge(moments_done, 1)
            nc.scalar.activation(dev[:], moments[:, :, 1], ACT.Sqrt, bias=eps[:, 0:1]).then_inc(dev_done, 1)
            act.wait_ge(var1_done, 1)
            nc.scalar.activation(dev1[:], var1[:], ACT.Sqrt, bias=eps[:, 1:2]).then_inc(dev_done, 1)


def clustered_attention(nc, a, Z, R1):
    with ExitStack() as ctx:
        def sb(name, shape, dt=F32):
            return ctx.enter_context(nc.sbuf_tensor(name, shape, dt))

        def ps(name, shape, dt=F32):
            return ctx.enter_context(nc.psum_tensor(name, shape, dt))

        def sem(name):
            return a["semaphores"].enter_context(nc.semaphore(name))

        ident = sb("ident", [P, P])
        ident16 = sb("ident16", [P, P], F16)
        w_qkv = sb("w_qkv", [P, 3, D])
        w_qT = sb("w_qT", [P, 2, D])
        w_hash = sb("w_hash", [P, 2, H * NB])
        w_cl = sb("w_cl", [P, 2, H * NB])
        w_o = sb("w_o", [P, D])
        ln1 = sb("ln1", [P, 2])
        xn = sb("xn", [P, 2, D])
        xnT = sb("xnT", [P, 2, P])
        qkv = sb("qkv", [P, 2, 3, D])
        cl = sb("cl", [P, 2, 2, H * NB])
        cl_max = sb("cl_max", [P, 2, 2, H])
        cl_sum = sb("cl_sum", [P, 2, 2, H])
        cl_inv = sb("cl_inv", [P, 2, 2, H])
        stack_tok = sb("stack_tok", [P, 2, H, P], F16)
        stack = sb("stack", [P, 2, 2, H, S], F16)
        v_pad = sb("v_pad", [P, 2, TPB, H, 32])
        row_max = sb("row_max", [P, 2, TPB, 4])
        shift_tok = sb("shift_tok", [P, TPB, 2, 4], F16)
        shift_row = sb("shift_row", [8, S], F16)
        prob = sb("prob", [P, 4, 4, S])
        heads_raw = sb("heads_raw", [P, S])
        inv_sum = sb("inv_sum", [P, TPB, 4])
        att_tok = sb("att_tok", [P, TPB, H, DH])
        att_T = sb("att_T", [P, S])

        scores_ps = ps("scores_ps", [P, 2, 2, S])
        max_ps = ps("max_ps", [P, 2, S])
        heads_ps = ps("heads_ps", [P, S])
        bench = ps("bench", [P, S])
        bench16 = bench[:].bitcast(F16)

        with ExitStack() as setup:
            w_loaded = a["semaphores"].enter_context(nc.semaphore("w_loaded"))
            folded = a["semaphores"].enter_context(nc.semaphore("folded"))
            block = setup.enter_context(nc.Block())
            loads = [(ident[:], a["ident"]), (ident16[:], a["ident16"]),
                     (w_qkv[:, 0, :], a["wq"]), (w_qkv[:, 1, :], a["wk"]), (w_qkv[:, 2, :], a["wv"]),
                     (w_qT[:, 0, :], a["wqT"]), (w_qT[:, 1, :], a["wkT"]),
                     (w_hash[:, 0, :], a["whq"]), (w_hash[:, 1, :], a["whk"]),
                     (w_o[:], a["wo"]), (ln1[:, 0:1], a["ln1_g"]), (ln1[:, 1:2], a["ln1_b"])]

            @block.sync
            def _(sp):
                for dst, src in loads:
                    sp.dma_start(dst, src).then_inc(w_loaded, 16)

            @block.tensor
            def _(pe):
                pe.wait_ge(w_loaded, 16 * len(loads))
                for i in range(2):
                    nc.tensor.matmul(max_ps[:, i, :], w_qT[:, i, :], w_hash[:, i, :],
                                     start=True, stop=True).then_inc(folded, 1)

            @block.vector
            def _(dve):
                nc.vector.memset(stack_tok[:], 0.0).then_inc(folded, 1)
                nc.vector.memset(v_pad[:], 0.0).then_inc(folded, 1)
                dve.wait_ge(folded, 4)
                nc.vector.memset(stack_tok[:, 1, :, 120:122], -SHIFT)
                nc.vector.memset(v_pad[:, :, :, :, DH:DH + 1], 1.0)
                for i in range(2):
                    nc.vector.tensor_copy(w_cl[:, i, :], max_ps[:, i, :])
                dve.wait_ge(w_loaded, 16 * len(loads))
                nc.vector.tensor_scalar(w_qkv[:, 0, :], w_qkv[:, 0, :], float(DH) ** -0.5, None, ALU.mult)

        bench_filled = sem("bench_filled")
        proj_added = sem("proj_added")
        xn_made = sem("xn_made")
        xnT_made = sem("xnT_made")
        qkv_made = sem("qkv_made")
        cl_max_made = sem("cl_max_made")
        cl_sub_made = sem("cl_sub_made")
        cl_exp_made = sem("cl_exp_made")
        cl_sum_made = sem("cl_sum_made")
        cl_inv_made = sem("cl_inv_made")
        cl_scaled = sem("cl_scaled")
        cl_share_made = sem("cl_share_made")
        hi_made = sem("hi_made")
        lo_made = sem("lo_made")
        v_made = sem("v_made")
        stack_made = sem("stack_made")
        max_scored = sem("max_scored")
        max_made = sem("max_made")
        shift_hi_made = sem("shift_hi_made")
        shift_made = sem("shift_made")
        shift_row_made = sem("shift_row_made")
        shift_placed = sem("shift_placed")
        scored = sem("scored")
        exp_made = sem("exp_made")
        pv_made = sem("pv_made")
        heads_moved = sem("heads_moved")
        inv_made = sem("inv_made")
        att_made = sem("att_made")
        att_T_made = sem("att_T_made")
        block = ctx.enter_context(nc.Block())

        def filled(eng, n, turn, use):
            wait(eng, bench_filled, BENCH_ORDER[(n, use)] + 1, turn, BENCH_PER_PAIR)

        @block.tensor
        def _(pe):
            def bench_is_free(n, turn, use):
                if before(n, use) is None:
                    return
                step, x = before(n, use)
                if step == "xn":
                    wait(pe, xnT_made, x + 1, turn, 2 * TPB)
                elif step == "qkv":
                    wait(pe, qkv_made, x + 1, turn, 2 * TPB)
                elif step in ("clq", "clk"):
                    wait(pe, cl_sub_made, 2 * x + (step == "clk") + 1, turn, 4 * TPB)
                elif step[:5] == "stack":
                    wait(pe, stack_made, 4 * x + STACKS.index(step) + 1, turn, 8 * TPB)
                elif step == "heads_out":
                    wait(pe, att_made, x + 1, turn, 8)
                elif step == "att_t":
                    wait(pe, att_T_made, x + 1, turn, 2)
                elif step == "proj":
                    wait(pe, proj_added, x + 1, turn, 2)
                elif step == "shift":
                    wait(pe, shift_row_made, x + 1, turn, 8)

            def slot(n, turn):
                s = streams(n)
                if s["scores"] is not None:
                    u = s["scores"]
                    par, g, kt, pr = u // SLOTS % 2, u // UNITS % 4, u % UNITS // 2, u % 2
                    if u % UNITS == 0:
                        wait(pe, shift_placed, 32 * (u // UNITS + 1), turn, 32 * 8)
                    wait(pe, exp_made, u - 1, turn, PAIR)
                    for i in range(2):
                        h = 4 * g + 2 * pr + i
                        mm = nc.tensor.matmul(scores_ps[:, u % 2, i, :],
                                              stack[:, par, 1, h, kt * P:(kt + 1) * P],
                                              stack[:, par, 0, h, :], start=True, stop=True)
                    mm.then_inc(scored, 1)
                if s["max"] is not None:
                    u = s["max"]
                    par, g, w = u // SLOTS % 2, u // UNITS % 4, u % UNITS
                    h = 4 * g + w // 2
                    if u % SLOTS == 0:
                        wait(pe, stack_made, 16 * (u // SLOTS + 1), turn, 16 * 2)
                    for i in range(2):
                        qt = 2 * (w % 2) + i
                        wait(pe, max_made, 2 * u + i - 1, turn, 2 * PAIR)
                        nc.tensor.matmul(max_ps[:, i, :], stack[:, par, 0, h, qt * P:(qt + 1) * P],
                                         stack[:, par, 1, h, :], start=True, stop=True).then_inc(max_scored, 1)
                if s["pv"] is not None:
                    c = s["pv"]
                    par, g, kt = c // 16 % 2, c // 4 % 4, c % 4
                    wait(pe, exp_made, 2 * c + 2, turn, PAIR)
                    if kt == 0:
                        wait(pe, heads_moved, c // 4, turn, 8)
                        if g == 0:
                            wait(pe, v_made, TPB * (c // 16 + 1), turn, 2 * TPB)
                    for j in range(4):
                        mm = nc.tensor.matmul(heads_ps[32 * j:32 * j + 32, :],
                                              v_pad[:, par, kt, 4 * g + j, :],
                                              prob[:, c % 4, j, :],
                                              start=(kt == 0), stop=(kt == 3))
                    mm.then_inc(pv_made, 1)
                for use in bench_uses(n):
                    bench_is_free(n, turn, use)
                    step, x = use
                    if step == "xn":
                        wait(pe, xn_made, x + 1, turn, 2 * TPB)
                        mm = nc.tensor.transpose(bench[:, 0:P], xn[:, x % 2, :], ident[:])
                    elif step == "qkv":
                        wait(pe, xnT_made, x + 1, turn, 2 * TPB)
                        mm = nc.tensor.matmul(bench[:, 0:3 * D], xnT[:, x % 2, :],
                                              w_qkv[:].rearrange("p a b -> p (a b)"), start=True, stop=True)
                    elif step in ("clq", "clk"):
                        mm = nc.tensor.matmul(bench[:], xnT[:, x % 2, :], w_cl[:, step == "clk", :],
                                              start=True, stop=True)
                    elif step[:5] == "stack":
                        side, half = int(step[6] == "k"), int(step[7])
                        wait(pe, hi_made, 2 * x + side + 1, turn, 4 * TPB)
                        wait(pe, lo_made, 2 * x + side + 1, turn, 4 * TPB)
                        for i in range(8):
                            mm = nc.tensor.transpose(bench16[:, i * P:(i + 1) * P],
                                                     stack_tok[:, side, 8 * half + i, :], ident16[:])
                    elif step == "heads_out":
                        wait(pe, heads_moved, x + 1, turn, 8)
                        for qt in range(TPB):
                            mm = nc.tensor.transpose(bench[:, qt * P:(qt + 1) * P],
                                                     heads_raw[:, qt * P:(qt + 1) * P], ident[:])
                    elif step == "att_t":
                        wait(pe, att_made, 4 * (x + 1), turn, 8)
                        for qt in range(TPB):
                            mm = nc.tensor.transpose(bench[:, qt * P:(qt + 1) * P],
                                                     att_tok[:, qt].rearrange("p h f -> p (h f)"), ident[:])
                    elif step == "proj":
                        wait(pe, att_T_made, x + 1, turn, 2)
                        for qt in range(TPB):
                            mm = nc.tensor.matmul(bench[:, qt * D:(qt + 1) * D],
                                                  att_T[:, qt * P:(qt + 1) * P], w_o[:],
                                                  start=True, stop=True)
                    elif step == "shift":
                        wait(pe, shift_made, x + 1, turn, 8)
                        for qt in range(TPB):
                            mm = nc.tensor.transpose(bench16[0:8, qt * P:(qt + 1) * P],
                                                     shift_tok[:, qt].rearrange("p s j -> p (s j)"), ident16[:])
                    mm.then_inc(bench_filled, 1)

            over_slots(pe, slot)

        @block.vector
        def _(dve):
            def slot(n, turn):
                s = streams(n)
                for tile, k in s["prep"]:
                    if k == 0:
                        wait(dve, xnT_made, tile - 1, turn, 2 * TPB)
                        T = tile_at(turn, tile)
                        nc.vector.tensor_scalar(xn[:, tile % 2, :],
                                                Z[:, bass.ds(T, 1), :].rearrange("p t d -> p (t d)"),
                                                R1[:, bass.ds(T, 1)], None, ALU.mult).then_inc(xn_made, 1)
                if s["max"] is not None:
                    u = s["max"]
                    w, grp = u % UNITS, u // UNITS
                    for i in range(2):
                        wait(dve, max_scored, 2 * u + i + 1, turn, 2 * PAIR)
                        qt = 2 * (w % 2) + i
                        nc.vector.tensor_reduce(row_max[:, grp % 2, qt, w // 2:w // 2 + 1],
                                                max_ps[:, i, :], AX.X, ALU.max).then_inc(max_made, 1)
                    if w == UNITS - 1:
                        wait(dve, max_made, 16 * (grp + 1), turn, 16 * 8)
                        wait(dve, shift_row_made, grp, turn, 8)
                        nc.vector.tensor_scalar(shift_tok[:, :, 0, :], row_max[:, grp % 2], 1.0 / SHIFT,
                                                None, ALU.mult).then_inc(shift_hi_made, 1)
                        wait(dve, shift_hi_made, grp + 1, turn, 8)
                        nc.vector.scalar_tensor_tensor(out=shift_tok[:, :, 1, :], in0=row_max[:, grp % 2],
                                                       scalar=1.0 / SHIFT, in1=shift_tok[:, :, 0, :],
                                                       op0=ALU.mult, op1=ALU.subtract).then_inc(shift_made, 1)
                for use in bench_uses(n):
                    step, x = use
                    if step in ("clq", "clk"):
                        side = int(step == "clk")
                        c = 2 * x + side
                        filled(dve, n, turn, use)
                        scores = bench[:].rearrange("p (h n) -> p h n", n=NB)
                        nc.vector.tensor_reduce(cl_max[:, x % 2, side, :], scores, AX.X,
                                                ALU.max).then_inc(cl_max_made, 1)
                        wait(dve, cl_max_made, c + 1, turn, 4 * TPB)
                        wait(dve, lo_made, c - 3, turn, 4 * TPB)
                        nc.vector.tensor_tensor(
                            cl[:, x % 2, side].rearrange("p (h n) -> p h n", n=NB), scores,
                            cl_max[:, x % 2, side, :].unsqueeze(2).to_broadcast([P, H, NB]),
                            ALU.subtract).then_inc(cl_sub_made, 1)
                    elif step[:5] == "stack":
                        side, half = int(step[6] == "k"), int(step[7])
                        filled(dve, n, turn, use)
                        if x % TPB == 0 and side == 0 and half == 0:
                            wait(dve, scored, SLOTS * (x // TPB - 1), turn, PAIR)
                        nc.vector.tensor_copy(
                            stack[:, x // TPB % 2, side, 8 * half:8 * half + 8, x % TPB * P:(x % TPB + 1) * P],
                            bench16.rearrange("p (h t) -> p h t", h=8)).then_inc(stack_made, 1)
                    elif step == "heads_out":
                        filled(dve, n, turn, use)
                        v = bench[:].rearrange("p (q j f) -> p q j f", q=TPB, j=4)
                        nc.vector.reciprocal(inv_sum[:], v[:, :, :, DH]).then_inc(inv_made, 1)
                        wait(dve, inv_made, x + 1, turn, 8)
                        if x % 4 == 0:
                            wait(dve, att_T_made, x // 4, turn, 2)
                        nc.vector.tensor_tensor(att_tok[:, :, 4 * (x % 4):4 * (x % 4) + 4, :],
                                                v[:, :, :, 0:DH],
                                                inv_sum[:].unsqueeze(3).to_broadcast([P, TPB, 4, DH]),
                                                ALU.mult).then_inc(att_made, 1)
                    elif step == "proj":
                        filled(dve, n, turn, use)
                        first = x * TPB if isinstance(turn, int) else turn * (2 * TPB) + x * TPB
                        zz = Z[:, bass.ds(first, TPB), :]
                        nc.vector.tensor_tensor(zz, bench[:].rearrange("p (t d) -> p t d", d=D), zz,
                                                ALU.add).then_inc(proj_added, 1)
                    elif step == "shift":
                        filled(dve, n, turn, use)
                        wait(dve, shift_placed, 32 * x, turn, 32 * 8)
                        nc.vector.tensor_copy(shift_row[:], bench16[0:8, 0:S]).then_inc(shift_row_made, 1)
                for tile, k in s["prep"]:
                    par = tile % 2
                    for side in range(2):
                        c = 2 * tile + side
                        if k == 4 + side:
                            wait(dve, cl_exp_made, c + 1, turn, 4 * TPB)
                            nc.vector.tensor_reduce(cl_sum[:, par, side, :],
                                                    cl[:, par, side].rearrange("p (h n) -> p h n", n=NB),
                                                    AX.X, ALU.add).then_inc(cl_sum_made, 1)
                            wait(dve, cl_sum_made, c + 1, turn, 4 * TPB)
                            nc.vector.reciprocal(cl_inv[:, par, side, :],
                                                 cl_sum[:, par, side, :]).then_inc(cl_inv_made, 1)
                            wait(dve, cl_inv_made, c + 1, turn, 4 * TPB)
                            nc.vector.tensor_scalar(cl_inv[:, par, side, :], cl_inv[:, par, side, :],
                                                    0.1 if side == 0 else 1.0, None,
                                                    ALU.mult).then_inc(cl_scaled, 1)
                        if k == 6 + side:
                            at = 4 * tile + side
                            wait(dve, cl_share_made, c + 1, turn, 4 * TPB)
                            wait(dve, stack_made, 4 * (tile - 1) + 2 * side + 2, turn, 8 * TPB)
                            share = cl[:, par, side].rearrange("p (h n) -> p h n", n=NB)
                            for dst in ((0, 2 * NB) if side == 0 else (0, NB)):
                                nc.vector.tensor_copy(stack_tok[:, side, :, dst:dst + NB], share)
                            feat = qkv[:, par, side].rearrange("p (h f) -> p h f", f=DH)
                            for dst in ((96, 112) if side == 0 else (96, 104)):
                                ins = nc.vector.tensor_copy(stack_tok[:, side, :, dst:dst + DH], feat)
                            ins.then_inc(hi_made, 1)

            over_slots(dve, slot)

        @block.scalar
        def _(act):
            def slot(n, turn):
                s = streams(n)
                if s["exp"] is not None:
                    u = s["exp"]
                    kt_all, pr = u // 2, u % 2
                    wait(act, scored, u + 1, turn, PAIR)
                    wait(act, pv_made, kt_all - 3, turn, PAIR // 2)
                    nc.scalar.activation(prob[:, kt_all % 4, 2 * pr:2 * pr + 2, :], scores_ps[:, u % 2],
                                         ACT.Exp).then_inc(exp_made, 1)
                if s["out"] is not None:
                    g = s["out"]
                    wait(act, pv_made, 4 * (g + 1), turn, PAIR // 2)
                    wait(act, att_made, g, turn, 8)
                    nc.scalar.activation(heads_raw[:], heads_ps[:], ACT.Copy).then_inc(heads_moved, 1)
                for use in bench_uses(n):
                    step, x = use
                    if step == "xn":
                        filled(act, n, turn, use)
                        nc.scalar.activation(xnT[:, x % 2, :], bench[:, 0:P], ACT.Identity,
                                             bias=ln1[:, 1:2], scale=ln1[:, 0:1]).then_inc(xnT_made, 1)
                    elif step == "qkv":
                        filled(act, n, turn, use)
                        wait(act, v_made, x - 1, turn, 2 * TPB)
                        wait(act, lo_made, 2 * x - 2, turn, 4 * TPB)
                        nc.scalar.activation(qkv[:, x % 2].rearrange("p a b -> p (a b)"), bench[:, 0:3 * D],
                                             ACT.Copy).then_inc(qkv_made, 1)
                    elif step == "att_t":
                        filled(act, n, turn, use)
                        nc.scalar.activation(att_T[:], bench[:], ACT.Copy).then_inc(att_T_made, 1)
                for tile, k in s["prep"]:
                    for side in range(2):
                        if k == 3 + side:
                            wait(act, cl_sub_made, 2 * tile + side + 1, turn, 4 * TPB)
                            e = cl[:, tile % 2, side]
                            nc.scalar.activation(e, e, ACT.Exp).then_inc(cl_exp_made, 1)
                    if k == 9:
                        wait(act, qkv_made, tile + 1, turn, 2 * TPB)
                        wait(act, pv_made, 16 * (tile // TPB - 1), turn, PAIR // 2)
                        nc.scalar.activation(v_pad[:, tile // TPB % 2, tile % TPB, :, 0:DH],
                                             qkv[:, tile % 2, 2].rearrange("p (h f) -> p h f", f=DH),
                                             ACT.Copy).then_inc(v_made, 1)

            over_slots(act, slot)

        @block.gpsimd
        def _(pool):
            def slot(n, turn):
                for tile, k in streams(n)["prep"]:
                    par = tile % 2
                    for side in range(2):
                        c = 2 * tile + side
                        share = cl[:, par, side].rearrange("p (h n) -> p h n", n=NB)
                        feat = qkv[:, par, side].rearrange("p (h f) -> p h f", f=DH)
                        if k == 4 + side:
                            wait(pool, cl_scaled, c + 1, turn, 4 * TPB)
                            nc.gpsimd.tensor_tensor(
                                share, share, cl_inv[:, par, side, :].unsqueeze(2).to_broadcast([P, H, NB]),
                                ALU.mult).then_inc(cl_share_made, 1)
                        if k == 6 + side:
                            wait(pool, hi_made, c + 1, turn, 4 * TPB)
                            lo = NB if side == 0 else 2 * NB
                            nc.gpsimd.tensor_tensor(stack_tok[:, side, :, lo:lo + NB], share,
                                                    stack_tok[:, side, :, 0:NB], ALU.subtract)
                            lo = 104 if side == 0 else 112
                            nc.gpsimd.tensor_tensor(stack_tok[:, side, :, lo:lo + DH], feat,
                                                    stack_tok[:, side, :, 96:96 + DH],
                                                    ALU.subtract).then_inc(lo_made, 1)

            over_slots(pool, slot)

        @block.sync
        def _(sp):
            def slot(n, turn):
                for step, g in bench_uses(n):
                    if step == "shift":
                        wait(sp, shift_row_made, g + 1, turn, 8)
                        heads = slice(4 * (g % 4), 4 * (g % 4) + 4)
                        for part in range(2):
                            sp.dma_start(stack[120 + part:121 + part, g // 4 % 2, 0, heads, :],
                                         shift_row[4 * part:4 * part + 4, :]).then_inc(shift_placed, 16)

            over_slots(sp, slot)


def over(eng, slot, first, loop_from, turns, period, last):
    for n in range(first, loop_from):
        slot(n, 0)
    with eng.Fori(0, turns) as turn:
        for n in range(loop_from, loop_from + period):
            slot(n, turn)
    for n in range(loop_from + turns * period, last):
        slot(n, 0)


def flat(ap):
    return ap.rearrange("p a b -> p (a b)")


def clear(nc, semaphores):
    with nc.Block() as block:
        @block.gpsimd
        def _(pool):
            for s in semaphores:
                pool.sem_clear(s)
    for s in semaphores:
        nc.release_semaphore(s)


def token_moments(nc, a, src, mean, inv_dev, eps, tag):
    with ExitStack() as ctx:
        def sb(name, shape, dt=F32):
            return ctx.enter_context(nc.sbuf_tensor(tag + name, shape, dt))

        def sem(name):
            return a["semaphores"].enter_context(nc.semaphore(tag + name))

        stats = sb("stats", [P, NT, 6])
        moments = sb("moments", [P, NT, 2])
        dev = sb("dev", [P, NT])
        eps_col = sb("eps", [P, 1])
        stats_done = sem("stats_done")
        moments_done = sem("moments_done")
        dev_done = sem("dev_done")
        block = ctx.enter_context(nc.Block())

        @block.vector
        def _(dve):
            nc.vector.memset(eps_col[:], eps)
            with dve.Fori(0, NT) as t:
                nc.vector.bn_stats(stats[:, bass.ds(t, 1), :].rearrange("p a b -> p (a b)"),
                                   flat(src[:, bass.ds(t, 1), :])).then_inc(stats_done, 1)
            dve.wait_ge(stats_done, NT)
            for t in range(NT):
                nc.vector.bn_aggr(moments[:, t, :], stats[:, t, :]).then_inc(moments_done, 1)
            dve.wait_ge(moments_done, NT)
            nc.vector.tensor_copy(mean[:], moments[:, :, 0])
            dve.wait_ge(dev_done, 1)
            nc.vector.reciprocal(inv_dev[:], dev[:])

        @block.scalar
        def _(act):
            act.wait_ge(moments_done, NT)
            nc.scalar.activation(dev[:], moments[:, :, 1], ACT.Sqrt, bias=eps_col[:]).then_inc(dev_done, 1)


def attention_mlp(nc, a, X, Z, mean, inv_dev):
    MC = MLP // P
    with ExitStack() as ctx:
        def sb(name, shape, dt=F32):
            return ctx.enter_context(nc.sbuf_tensor("mlp_" + name, shape, dt))

        def ps(name, shape, dt=F32):
            return ctx.enter_context(nc.psum_tensor("mlp_" + name, shape, dt))

        def sem(name):
            return a["semaphores"].enter_context(nc.semaphore("mlp_" + name))

        ident = sb("ident", [P, P])
        w1 = sb("w1", [P, MLP])
        w2 = sb("w2", [P, MC, D])
        b1 = sb("b1", [P, MC])
        ln2 = sb("ln2", [P, 2])
        b2_rows = sb("b2_rows", [P, D])
        y = sb("y", [P, 2, TPB, D])
        yT = sb("yT", [P, 2, S])
        hid = sb("hid", [P, 2, MC, S])
        base = sb("base", [P, 2, TPB, D])
        t_ps = ps("t_ps", [P, S])
        h_ps = ps("h_ps", [P, MC, S])
        o_ps = ps("o_ps", [P, S])
        loaded = sem("loaded")
        y_made = sem("y_made")
        turned = sem("turned")
        yT_made = sem("yT_made")
        h_filled = sem("h_filled")
        h_act = sem("h_act")
        h_dve = sem("h_dve")
        o_filled = sem("o_filled")
        added = sem("added")
        base_half = sem("base_half")
        base_made = sem("base_made")
        loads = [(ident[:], a["ident"]), (w1[:], a["mlp_w1"]),
                 (w2[:], a["mlp_w2"].rearrange("(c p) d -> p c d", p=P)), (b1[:], a["mlp_b1"]),
                 (ln2[:, 0:1], a["ln2_g"]), (ln2[:, 1:2], a["ln2_b"]), (b2_rows[:], a["mlp_b2_rows"])]
        all_loaded = 16 * len(loads)
        block = ctx.enter_context(nc.Block())

        def tiles(buf, b, turn):
            first = b * TPB if isinstance(turn, int) else turn * (2 * TPB) + b * TPB
            return buf[:, bass.ds(first, TPB), :]

        def run(eng, slot):
            over(eng, slot, 0, 2, 3, 2, B + 2)

        @block.sync
        def _(sp):
            for dst, src in loads:
                sp.dma_start(dst, src).then_inc(loaded, 16)

        @block.vector
        def _(dve):
            dve.wait_ge(loaded, all_loaded)

            def slot(n, turn):
                b = n
                if b < B:
                    wait(dve, turned, b - 1, turn, 2)
                    for t in range(TPB):
                        T = b * TPB + t if isinstance(turn, int) else turn * (2 * TPB) + b * TPB + t
                        ins = nc.vector.tensor_scalar(y[:, b % 2, t, :], flat(Z[:, bass.ds(T, 1), :]),
                                                      mean[:, bass.ds(T, 1)], inv_dev[:, bass.ds(T, 1)],
                                                      ALU.subtract, ALU.mult)
                    ins.then_inc(y_made, 1)
                b = n - 1
                if 0 <= b < B:
                    for c in (1, 3):
                        wait(dve, h_filled, MC * b + c + 1, turn, 2 * MC)
                        wait(dve, o_filled, b - 1, turn, 2)
                        nc.vector.tensor_scalar(hid[:, b % 2, c, :], h_ps[:, c, :], b1[:, c:c + 1], 0.0,
                                                ALU.add, ALU.max).then_inc(h_dve, 1)
                b = n - 2
                if 0 <= b < B:
                    wait(dve, o_filled, b + 1, turn, 2)
                    wait(dve, base_made, b + 1, turn, 2)
                    nc.vector.tensor_tensor(tiles(X, b, turn), o_ps[:].rearrange("p (t d) -> p t d", d=D),
                                            base[:, b % 2], ALU.add).then_inc(added, 1)

            run(dve, slot)

        @block.gpsimd
        def _(pool):
            pool.wait_ge(loaded, all_loaded)

            def slot(n, turn):
                b = n - 1
                if 0 <= b < B:
                    wait(pool, added, b - 1, turn, 2)
                    nc.gpsimd.tensor_tensor(base[:, b % 2], tiles(X, b, turn), tiles(Z, b, turn),
                                            ALU.add).then_inc(base_half, 1)
                    wait(pool, base_half, b + 1, turn, 2)
                    nc.gpsimd.tensor_tensor(base[:, b % 2], base[:, b % 2],
                                            b2_rows[:].unsqueeze(1).to_broadcast([P, TPB, D]),
                                            ALU.add).then_inc(base_made, 1)

            run(pool, slot)

        @block.scalar
        def _(act):
            act.wait_ge(loaded, all_loaded)

            def slot(n, turn):
                b = n
                if b < B:
                    wait(act, turned, b + 1, turn, 2)
                    wait(act, h_filled, MC * (b - 1), turn, 2 * MC)
                    nc.scalar.activation(yT[:, b % 2, :], t_ps[:], ACT.Identity, bias=ln2[:, 1:2],
                                         scale=ln2[:, 0:1]).then_inc(yT_made, 1)
                b = n - 1
                if 0 <= b < B:
                    for c in (0, 2):
                        wait(act, h_filled, MC * b + c + 1, turn, 2 * MC)
                        wait(act, o_filled, b - 1, turn, 2)
                        nc.scalar.activation(hid[:, b % 2, c, :], h_ps[:, c, :], ACT.Relu,
                                             bias=b1[:, c:c + 1]).then_inc(h_act, 1)

            run(act, slot)

        @block.tensor
        def _(pe):
            pe.wait_ge(loaded, all_loaded)

            def slot(n, turn):
                b = n
                if b < B:
                    wait(pe, y_made, b + 1, turn, 2)
                    wait(pe, yT_made, b, turn, 2)
                    for t in range(TPB):
                        mm = nc.tensor.transpose(t_ps[:, t * P:(t + 1) * P], y[:, b % 2, t, :], ident[:])
                    mm.then_inc(turned, 1)
                b = n - 1
                if 0 <= b < B:
                    wait(pe, yT_made, b + 1, turn, 2)
                    for c in range(MC):
                        wait(pe, (h_act, h_dve)[c % 2], 2 * (b - 1) + c // 2 + 1, turn, 4)
                        nc.tensor.matmul(h_ps[:, c, :], w1[:, c * P:(c + 1) * P], yT[:, b % 2, :],
                                         start=True, stop=True).then_inc(h_filled, 1)
                b = n - 2
                if 0 <= b < B:
                    wait(pe, h_act, 2 * (b + 1), turn, 4)
                    wait(pe, h_dve, 2 * (b + 1), turn, 4)
                    wait(pe, added, b, turn, 2)
                    for t in range(TPB):
                        for c in range(MC):
                            mm = nc.tensor.matmul(o_ps[:, t * D:(t + 1) * D],
                                                  hid[:, b % 2, c, t * P:(t + 1) * P], w2[:, c, :],
                                                  start=(c == 0), stop=(c == MC - 1))
                    mm.then_inc(o_filled, 1)

            run(pe, slot)


def turn_tokens(nc, a, X, mean, inv_dev, XT):
    with ExitStack() as ctx:
        def sem(name):
            return a["semaphores"].enter_context(nc.semaphore("turn_" + name))

        ident = ctx.enter_context(nc.sbuf_tensor("turn_ident", [P, P], F32))
        w = ctx.enter_context(nc.sbuf_tensor("turn_w", [P, 2, TPB, D], F32))
        t_ps = ctx.enter_context(nc.psum_tensor("turn_ps", [P, 2, S], F32))
        loaded, made, turned, moved = sem("loaded"), sem("made"), sem("turned"), sem("moved")
        block = ctx.enter_context(nc.Block())

        def run(eng, slot):
            over(eng, slot, 0, 2, 3, 2, B)

        @block.sync
        def _(sp):
            sp.dma_start(ident[:], a["ident"]).then_inc(loaded, 16)

        @block.vector
        def _(dve):
            def slot(n, turn):
                wait(dve, turned, n - 1, turn, 2)
                for t in range(TPB):
                    T = n * TPB + t if isinstance(turn, int) else turn * (2 * TPB) + n * TPB + t
                    ins = nc.vector.tensor_scalar(w[:, n % 2, t, :], flat(X[:, bass.ds(T, 1), :]),
                                                  mean[:, bass.ds(T, 1)], inv_dev[:, bass.ds(T, 1)],
                                                  ALU.subtract, ALU.mult)
                ins.then_inc(made, 1)

            run(dve, slot)

        @block.tensor
        def _(pe):
            pe.wait_ge(loaded, 16)

            def slot(n, turn):
                wait(pe, made, n + 1, turn, 2)
                wait(pe, moved, n - 1, turn, 2)
                for t in range(TPB):
                    mm = nc.tensor.transpose(t_ps[:, n % 2, t * P:(t + 1) * P], w[:, n % 2, t, :], ident[:])
                mm.then_inc(turned, 1)

            run(pe, slot)

        @block.scalar
        def _(act):
            def slot(n, turn):
                wait(act, turned, n + 1, turn, 2)
                b = n if isinstance(turn, int) else turn * 2 + n
                nc.scalar.activation(flat(XT[:, bass.ds(b, 1), :]), t_ps[:, n % 2, :], ACT.Copy).then_inc(moved, 1)

            run(act, slot)


LH, LD, WIN = 8, 64, 64
INNER = LH * LD
KEYS = P + WIN
NEG = -1e30
LN_SCALE = 2.0 ** 20


def local_attention(nc, a, layer, XT, C, VAR):
    tag = f"la{layer}_"
    with ExitStack() as ctx:
        def sb(name, shape, dt=F32):
            return ctx.enter_context(nc.sbuf_tensor(tag + name, shape, dt))

        def ps(name, shape, dt=F32):
            return ctx.enter_context(nc.psum_tensor(tag + name, shape, dt))

        def sem(name):
            return a["layer_semaphores"](tag + name)

        ident = sb("ident", [P, P])
        identb = sb("identb", [P, P], BF16)
        band = sb("band", [P, KEYS], BF16)
        mean_of = sb("mean_of", [P, P])
        wqkv = sb("wqkv", [P, 3 * INNER])
        wo = sb("wo", [P, INNER // P, D])
        rot = sb("rot", [P, TPB, 2, 2, LD])
        gains = sb("gains", [P, 2, 2, LD])
        hT = sb("hT", [P, 2, S])
        raw = sb("raw", [P, 2, INNER])
        plain = sb("plain", [P, 2, INNER])
        swapped = sb("swapped", [P, 2, INNER])
        turned = sb("turned", [P, 2, 2, INNER])
        squares = sb("squares", [P, 2, INNER])
        sumsq = sb("sumsq", [P, 2, 2 * LH])
        lnsq = sb("lnsq", [P, 2, 2 * LH])
        inv = sb("inv", [P, 2, 2 * LH])
        newton = sb("newton", [P, 2 * LH])
        q_gain = sb("q_gain", [P, 4, LH])
        half_ln = sb("half_ln", [P, 1])
        qT = sb("qT", [P, 2, 4, P])
        kT = sb("kT", [P, 2, 4, S])
        v1 = sb("v1", [P, 2, TPB, LH, LD + 1])
        s_max = sb("s_max", [P, 2, 4])
        s_bias = sb("s_bias", [P, 2, 4])
        prob = sb("prob", [P, 2, 4, 2 * P])
        probT = sb("probT", [P, 2, 8, P])
        o_inv = sb("o_inv", [P, 4])
        o_tok = sb("o_tok", [P, 2, INNER])
        oT = sb("oT", [P, 2, 4, S])
        shifted = sb("shifted", [P, S])
        csq = sb("csq", [P, S])
        ring_ps = ps("ring", [P, 2, S])
        s_ps = ps("s", [P, 4, 2 * P])
        pT_ps = ps("pT", [P, 8, P])
        o_ps = ps("o", [P, 4, P])
        m_ps = ps("m", [P, S])
        loaded = sem("loaded")
        ready = sem("ready")
        gained = sem("gained")
        h_made = sem("h_made")
        ring_filled = sem("ring_filled")
        raw_made = sem("raw_made")
        rot_read = sem("rot_read")
        sq_made = sem("sq_made")
        v_made = sem("v_made")
        qT_made = sem("qT_made")
        kT_made = sem("kT_made")
        added_rot = sem("added_rot")
        k_scaled = sem("k_scaled")
        sum_made = sem("sum_made")
        clip_made = sem("clip_made")
        ln_made = sem("ln_made")
        seed_made = sem("seed_made")
        nt1, nt2, nt3, inv_made = sem("newton1"), sem("newton2"), sem("newton3"), sem("inv_made")
        q_gain_made = sem("q_gain_made")
        s_filled = sem("s_filled")
        max_made = sem("max_made")
        bias_made = sem("bias_made")
        exp_made = sem("exp_made")
        pT_filled = sem("pT_filled")
        pT_made = sem("pT_made")
        o_filled = sem("o_filled")
        o_inv_made = sem("o_inv_made")
        o_made = sem("o_made")
        m_filled = sem("m_filled")
        oT_made = sem("oT_made")
        x_added = sem("x_added")
        sh_made = sem("sh_made")
        c_made = sem("c_made")
        csq_made = sem("csq_made")
        var_made = sem("var_made")

        loads = [(ident[:], a["ident"]), (identb[:], a["identb"]), (band[:], a["band"]),
                 (mean_of[:], a["mean_of"]), (wqkv[:], a["wqkv"][layer]),
                 (wo[:], a["lwo"][layer].rearrange("(c p) d -> p c d", p=P)),
                 (rot[:].rearrange("p t s w f -> p t (s w f)"), a["rot"].rearrange("(t p) s w f -> p t (s w f)", p=P)),
                 (gains[:].rearrange("p s w f -> p (s w f)"), a["gains"][layer])]
        all_loaded = 16 * len(loads)
        T_LAST = NT + 3
        block = ctx.enter_context(nc.Block())

        def batch_at(buf, b, turn):
            return flat(buf[:, bass.ds(b if isinstance(turn, int) else turn * 2 + b, 1), :])

        def run(eng, slot):
            over(eng, slot, 0, 8, 3, 8, T_LAST)

        def ring_index(T, use):
            return 5 * T + use if use < 3 else 5 * (T + 1) + use
        RING = 5 * 8

        def missing(r):
            return (2 if r >= 5 else 0) + (3 if r >= 5 * NT else 0)

        def m_count(T):
            return T + 1 + 3 * (T // TPB) if T >= 0 else 0

        def place(j):
            return 2 * (j % 2) + j // 2

        def attn_tile(n):
            return n - 2 if 0 <= n - 2 < NT else None

        @block.sync
        def _(sp):
            for dst, src in loads:
                sp.dma_start(dst, src).then_inc(loaded, 16)

        @block.tensor
        def _(pe):
            pe.wait_ge(loaded, all_loaded)
            pe.wait_ge(ready, 1)

            def ring_free(r, turn):
                p = r - 2
                while p >= 0 and not 0 <= p // 5 - (p % 5 >= 3) < NT:
                    p -= 2
                if p < 0:
                    return
                T, use = p // 5 - (p % 5 >= 3), p % 5
                if use < 2:
                    wait(pe, raw_made, 2 * T + use + 1, turn, 16)
                else:
                    wait(pe, (v_made, qT_made, kT_made)[use - 2], T + 1, turn, 8)

            def project(T, use, turn):
                b, t = T // TPB, T % TPB
                if t == 0 and use == 0:
                    wait(pe, h_made, 2 * (b + 1), turn, 4)
                r = ring_index(T, use)
                ring_free(r, turn)
                nc.tensor.matmul(ring_ps[:, r % 2, :], hT[:, b % 2, t * P:(t + 1) * P],
                                 wqkv[:, use * INNER:(use + 1) * INNER], start=True, stop=True
                                 ).then_inc(ring_filled, 1)

            def transpose(T, use, turn):
                r = ring_index(T, use)
                ring_free(r, turn)
                if use == 3:
                    wait(pe, added_rot, 2 * T + 1, turn, 16)
                else:
                    wait(pe, k_scaled, T + 1, turn, 8)
                for c in range(4):
                    mm = nc.tensor.transpose(ring_ps[:, r % 2, c * P:(c + 1) * P],
                                             turned[:, T % 2, use - 3, c * P:(c + 1) * P], ident[:])
                mm.then_inc(ring_filled, 1)

            def scores(T, half, turn):
                b, t = T // TPB, T % TPB
                if half == 0:
                    wait(pe, qT_made, T + 1, turn, 8)
                    wait(pe, kT_made, T + 1, turn, 8)
                wait(pe, exp_made, 2 * T + half, turn, 16)
                lo = WIN if t == 0 else 0
                for j in range(4):
                    h = 4 * half + j
                    e = 64 * (h % 2)
                    nc.tensor.matmul(s_ps[:, place(j), lo:KEYS], qT[e:e + 64, T % 2, h // 2, :],
                                     kT[e:e + 64, b % 2, h // 2, t * P - WIN + lo:(t + 1) * P],
                                     start=(j < 2), stop=False, skip_group_check=True)
                for j in range(4):
                    mm = nc.tensor.matmul(s_ps[:, place(j), lo:KEYS], identb[:], band[:, lo:KEYS],
                                          start=False, stop=True, skip_group_check=True)
                mm.then_inc(s_filled, 1)

            def prob_turn(T, half, turn):
                t = T % TPB
                wait(pe, exp_made, 2 * T + half + 1, turn, 16)
                wait(pe, pT_made, 2 * T + half, turn, 16)
                for j in range(4):
                    for blk in range(t == 0, 2):
                        mm = nc.tensor.transpose(pT_ps[:, 2 * j + blk, :],
                                                 prob[:, half, j, blk * P:(blk + 1) * P], ident[:])
                mm.then_inc(pT_filled, 1)

            def weigh(T, half, turn):
                b, t = T // TPB, T % TPB
                wait(pe, pT_made, 2 * T + half + 1, turn, 16)
                wait(pe, o_made, 2 * T + half, turn, 16)
                for j in range(4):
                    for blk in range(t == 0, 2):
                        mm = nc.tensor.matmul(o_ps[:, j, 0:LD + 1], probT[:, half, 2 * j + blk, :],
                                              v1[:, b % 2, t - 1 + blk, 4 * half + j, :],
                                              start=(blk == (t == 0)), stop=(blk == 1))
                mm.then_inc(o_filled, 1)

            def slot(n, turn):
                T = n if n < NT else None
                U = attn_tile(n)
                if U is not None:
                    scores(U, 0, turn)
                if T is not None:
                    project(T, 0, turn)
                    project(T, 1, turn)
                if U is not None:
                    prob_turn(U, 0, turn)
                    scores(U, 1, turn)
                if T is not None:
                    project(T, 2, turn)
                if U is not None:
                    weigh(U, 0, turn)
                if 0 <= n - 1 < NT:
                    transpose(n - 1, 3, turn)
                    transpose(n - 1, 4, turn)
                if U is not None:
                    prob_turn(U, 1, turn)
                    weigh(U, 1, turn)
                T = n - 3
                if 0 <= T < NT:
                    t, b = T % TPB, T // TPB
                    wait(pe, o_made, 2 * (T + 1), turn, 16)
                    if t == 0:
                        wait(pe, var_made, b, turn, 2)
                    else:
                        wait(pe, oT_made, T, turn, 8)
                    for c in range(4):
                        mm = nc.tensor.transpose(m_ps[:, c * P:(c + 1) * P],
                                                 o_tok[:, T % 2, c * P:(c + 1) * P], ident[:])
                    mm.then_inc(m_filled, 1)
                    if t == TPB - 1:
                        wait(pe, oT_made, T + 1, turn, 8)
                        for c in range(4):
                            mm = nc.tensor.matmul(m_ps[:], wo[:, c, :], oT[:, b % 2, c, :],
                                                  start=(c == 0), stop=(c == 3))
                        mm.then_inc(m_filled, 1)
                        wait(pe, sh_made, 2 * (b + 1), turn, 4)
                        nc.tensor.matmul(m_ps[:], mean_of[:], shifted[:], start=True, stop=True
                                         ).then_inc(m_filled, 1)
                        wait(pe, csq_made, b + 1, turn, 2)
                        nc.tensor.matmul(m_ps[:], mean_of[:], csq[:], start=True, stop=True
                                         ).then_inc(m_filled, 1)

            run(pe, slot)

        def shift(dve, dst, src, done):
            nc.vector.tensor_scalar(dst[0:64, :], src[0:64, :], 1.0, None, ALU.mult).then_inc(done, 1)
            nc.vector.tensor_scalar(dst[64:P, 1:S], src[64:P, 0:S - 1], 1.0, None, ALU.mult).then_inc(done, 1)

        @block.vector
        def _(dve):
            nc.vector.memset(half_ln[:], 0.5 * float(np.log(LN_SCALE)))
            nc.vector.memset(hT[64:P, :, 0:1], 0.0)
            nc.vector.memset(shifted[64:P, 0:1], 0.0)
            nc.vector.memset(prob[:, :, :, 0:WIN], 0.0)
            nc.vector.memset(v1[:, :, :, :, LD:LD + 1], 1.0).then_inc(ready, 1)
            dve.wait_ge(loaded, all_loaded)
            for t in range(TPB):
                nc.vector.tensor_tensor(rot[:, t], rot[:, t], gains[:], ALU.mult).then_inc(gained, 1)
            dve.wait_ge(gained, TPB)

            def halves(ap):
                return ap.rearrange("p (h w f) -> p h w f", w=2, f=LD // 2)

            def rotate(T, side, turn):
                t = T % TPB
                wait(dve, raw_made, 2 * T + side + 1, turn, 16)
                if side == 0:
                    wait(dve, added_rot, 2 * T - 1, turn, 16)
                else:
                    wait(dve, added_rot, 2 * T, turn, 16)
                src = raw[:, side]
                nc.vector.tensor_tensor(plain[:, side].rearrange("p (h f) -> p h f", f=LD),
                                        src.rearrange("p (h f) -> p h f", f=LD),
                                        rot[:, t, side, 0, :].unsqueeze(1).to_broadcast([P, LH, LD]), ALU.mult)
                for w in range(2):
                    ins = nc.vector.tensor_tensor(
                        halves(swapped[:, side])[:, :, w, :], halves(src)[:, :, 1 - w, :],
                        rot[:, t, side, 1, w * 32:(w + 1) * 32].unsqueeze(1).to_broadcast([P, LH, 32]), ALU.mult)
                ins.then_inc(rot_read, 1)

            def norms(T, turn):
                par = T % 2
                for side in range(2):
                    wait(dve, sq_made, 2 * T + side + 1, turn, 16)
                    nc.vector.tensor_reduce(sumsq[:, par, side * LH:(side + 1) * LH],
                                            squares[:, side].rearrange("p (h f) -> p h f", f=LD),
                                            AX.X, ALU.add).then_inc(sum_made, 1)
                wait(dve, sum_made, 2 * T + 2, turn, 16)
                nc.vector.tensor_scalar(sumsq[:, par], sumsq[:, par], 1e-24, None, ALU.max).then_inc(clip_made, 1)

            def polish(T, turn):
                par = T % 2
                wait(dve, seed_made, T + 1, turn, 8)
                nc.vector.tensor_tensor(newton[:], inv[:, par], inv[:, par], ALU.mult).then_inc(nt1, 1)
                wait(dve, nt1, T + 1, turn, 8)
                nc.vector.tensor_tensor(newton[:], newton[:], sumsq[:, par], ALU.mult).then_inc(nt2, 1)
                wait(dve, nt2, T + 1, turn, 8)
                nc.vector.tensor_scalar(newton[:], newton[:], -0.5, 1.5, ALU.mult, ALU.add).then_inc(nt3, 1)
                wait(dve, nt3, T + 1, turn, 8)
                nc.vector.tensor_tensor(inv[:, par], inv[:, par], newton[:], ALU.mult).then_inc(inv_made, 1)
                wait(dve, inv_made, T + 1, turn, 8)
                nc.vector.tensor_scalar(q_gain[:, T % 4], inv[:, par, 0:LH], 8.0, None,
                                        ALU.mult).then_inc(q_gain_made, 1)

            def maxima(T, half, turn):
                lo = WIN if T % TPB == 0 else 0
                wait(dve, s_filled, 2 * T + half + 1, turn, 16)
                wait(dve, exp_made, 2 * T + half - 1, turn, 16)
                nc.vector.tensor_reduce(s_max[:, half], s_ps[:, :, lo:KEYS], AX.X, ALU.max).then_inc(max_made, 1)
                wait(dve, max_made, 2 * T + half + 1, turn, 16)
                if half == 0:
                    wait(dve, q_gain_made, T + 1, turn, 8)
                by_place = q_gain[:, T % 4, 4 * half:4 * half + 4].rearrange("p (b a) -> p a b", a=2)
                nc.vector.scalar_tensor_tensor(out=s_bias[:, half].rearrange("p (a b) -> p a b", a=2),
                                               in0=s_max[:, half].rearrange("p (a b) -> p a b", a=2),
                                               scalar=-1.0, in1=by_place,
                                               op0=ALU.mult, op1=ALU.mult).then_inc(bias_made, 1)

            def take_probT(T, half, turn):
                wait(dve, pT_filled, 2 * T + half + 1, turn, 16)
                wait(dve, o_filled, 2 * T + half - 1, turn, 16)
                first = T % TPB == 0
                v = pT_ps[:].rearrange("p (j s) q -> p j s q", s=2)
                o = probT[:, half].rearrange("p (j s) q -> p j s q", s=2)
                nc.vector.tensor_copy(o[:, :, first:2, :], v[:, :, first:2, :]).then_inc(pT_made, 1)

            def take_out(T, half, turn):
                wait(dve, o_filled, 2 * T + half + 1, turn, 16)
                nc.vector.reciprocal(o_inv[:], o_ps[:, :, LD]).then_inc(o_inv_made, 1)
                wait(dve, o_inv_made, 2 * T + half + 1, turn, 16)
                if half == 0:
                    wait(dve, m_filled, m_count(T - 2), turn, 14)
                nc.vector.tensor_tensor(
                    o_tok[:, T % 2, half * 256:(half + 1) * 256].rearrange("p (j f) -> p j f", f=LD),
                    o_ps[:, :, 0:LD], o_inv[:].unsqueeze(2).to_broadcast([P, 4, LD]),
                    ALU.mult).then_inc(o_made, 1)

            def slot(n, turn):
                T = n if n < NT else None
                U = attn_tile(n)
                if T is not None and T % TPB == 0:
                    b = T // TPB
                    if b >= 2:
                        r = ring_index(T - TPB - 1, 2)
                        wait(dve, ring_filled, r + 1 - missing(r), turn, RING)
                    shift(dve, hT[:, b % 2, :], batch_at(XT, b, turn), h_made)
                if U is not None:
                    maxima(U, 0, turn)
                if T is not None:
                    rotate(T, 0, turn)
                    rotate(T, 1, turn)
                if U is not None:
                    take_probT(U, 0, turn)
                if T is not None:
                    norms(T, turn)
                if U is not None:
                    maxima(U, 1, turn)
                    take_out(U, 0, turn)
                if T is not None:
                    polish(T, turn)
                if 0 <= n - 1 < NT:
                    T = n - 1
                    r = ring_index(T, 3)
                    wait(dve, ring_filled, r + 1 - missing(r), turn, RING)
                    wait(dve, s_filled, 2 * T - 2, turn, 16)
                    nc.vector.tensor_copy(qT[:, T % 2].rearrange("p c q -> p (c q)"),
                                          ring_ps[:, r % 2, :]).then_inc(qT_made, 1)
                if U is not None:
                    take_probT(U, 1, turn)
                    take_out(U, 1, turn)
                T = n - 3
                if 0 <= T < NT and T % TPB == TPB - 1:
                    b = T // TPB
                    x = batch_at(XT, b, turn)
                    wait(dve, m_filled, m_count(T) + 1, turn, 14)
                    nc.vector.tensor_tensor(x, m_ps[:], x, ALU.add).then_inc(x_added, 1)
                    wait(dve, x_added, b + 1, turn, 2)
                    shift(dve, shifted, x, sh_made)
                    wait(dve, sh_made, 2 * (b + 1), turn, 4)
                    wait(dve, m_filled, m_count(T) + 2, turn, 14)
                    nc.vector.tensor_tensor(batch_at(C, b, turn), shifted[:], m_ps[:],
                                            ALU.subtract).then_inc(c_made, 1)

            run(dve, slot)

        @block.scalar
        def _(act):
            act.wait_ge(ready, 1)

            def exps(T, half, turn):
                lo = WIN if T % TPB == 0 else 0
                wait(act, bias_made, 2 * T + half + 1, turn, 16)
                wait(act, pT_filled, 2 * T + half - 1, turn, 16)
                for j in range(4):
                    ins = nc.scalar.activation(prob[:, half, j, WIN + lo:WIN + KEYS],
                                               s_ps[:, place(j), lo:KEYS], ACT.Exp,
                                               bias=s_bias[:, half, place(j):place(j) + 1],
                                               scale=q_gain[:, T % 4, 4 * half + j:4 * half + j + 1])
                ins.then_inc(exp_made, 1)

            def slot(n, turn):
                T = n if n < NT else None
                U = attn_tile(n)
                if U is not None:
                    exps(U, 0, turn)
                if T is not None:
                    for side in range(2):
                        r = ring_index(T, side)
                        wait(act, ring_filled, r + 1 - missing(r), turn, RING)
                        wait(act, sum_made, 2 * T + side - 1, turn, 16)
                        wait(act, rot_read, 2 * T + side - 1, turn, 16)
                        nc.scalar.activation(raw[:, side], ring_ps[:, r % 2, :], ACT.Copy).then_inc(raw_made, 1)
                        wait(act, raw_made, 2 * T + side + 1, turn, 16)
                        nc.scalar.activation(squares[:, side], raw[:, side], ACT.Square).then_inc(sq_made, 1)
                if U is not None:
                    exps(U, 1, turn)
                if T is not None:
                    b, t = T // TPB, T % TPB
                    r = ring_index(T, 2)
                    wait(act, ring_filled, r + 1 - missing(r), turn, RING)
                    wait(act, o_filled, 8 * (b - 1), turn, 16)
                    nc.scalar.activation(v1[:, b % 2, t, :, 0:LD],
                                         ring_ps[:, r % 2, :].rearrange("p (h f) -> p h f", f=LD),
                                         ACT.Copy).then_inc(v_made, 1)
                    wait(act, clip_made, T + 1, turn, 8)
                    wait(act, q_gain_made, T - 1, turn, 8)
                    wait(act, k_scaled, T - 1, turn, 8)
                    nc.scalar.activation(lnsq[:, T % 2], sumsq[:, T % 2], ACT.Ln, scale=LN_SCALE
                                         ).then_inc(ln_made, 1)
                    wait(act, ln_made, T + 1, turn, 8)
                    nc.scalar.activation(inv[:, T % 2], lnsq[:, T % 2], ACT.Exp, bias=half_ln[:],
                                         scale=-0.5).then_inc(seed_made, 1)
                if 0 <= n - 1 < NT:
                    T = n - 1
                    b, t = T // TPB, T % TPB
                    r = ring_index(T, 4)
                    wait(act, ring_filled, r + 1 - missing(r), turn, RING)
                    wait(act, s_filled, 8 * (b - 1), turn, 16)
                    nc.scalar.activation(kT[:, b % 2, :, t * P:(t + 1) * P],
                                         ring_ps[:, r % 2, :].rearrange("p (c q) -> p c q", q=P),
                                         ACT.Copy).then_inc(kT_made, 1)
                T = n - 3
                if 0 <= T < NT:
                    b, t = T // TPB, T % TPB
                    wait(act, m_filled, m_count(T), turn, 14)
                    nc.scalar.activation(oT[:, b % 2, :, t * P:(t + 1) * P],
                                         m_ps[:].rearrange("p (c q) -> p c q", q=P),
                                         ACT.Copy).then_inc(oT_made, 1)
                    if t == TPB - 1:
                        wait(act, c_made, b + 1, turn, 2)
                        nc.scalar.activation(csq[:], batch_at(C, b, turn), ACT.Square).then_inc(csq_made, 1)
                        wait(act, m_filled, m_count(T) + 3, turn, 14)
                        nc.scalar.activation(batch_at(VAR, b, turn), m_ps[:], ACT.Copy).then_inc(var_made, 1)

            run(act, slot)

        @block.gpsimd
        def _(pool):
            def slot(n, turn):
                T = n if n < NT else None
                if T is not None:
                    for side in range(2):
                        wait(pool, rot_read, 2 * T + side + 1, turn, 16)
                        r = ring_index(T - 2, 3 + side)
                        if T >= 2:
                            wait(pool, ring_filled, r + 1 - missing(r), turn, RING)
                        nc.gpsimd.tensor_tensor(turned[:, T % 2, side], plain[:, side], swapped[:, side],
                                                ALU.add).then_inc(added_rot, 1)
                    wait(pool, inv_made, T + 1, turn, 8)
                    wait(pool, added_rot, 2 * T + 2, turn, 16)
                    k = turned[:, T % 2, 1].rearrange("p (h f) -> p h f", f=LD)
                    nc.gpsimd.tensor_tensor(k, k, inv[:, T % 2, LH:2 * LH].unsqueeze(2).to_broadcast([P, LH, LD]),
                                            ALU.mult).then_inc(k_scaled, 1)

            over(pool, slot, 0, 8, 3, 8, NT)


HID = D * 4 * 2 // 3
HC = [(c, min(P, HID - c)) for c in range(0, HID, P)]


def gated_ffn(nc, a, layer, XT, C, VAR):
    tag = f"ff{layer}_"
    NC = len(HC)
    with ExitStack() as ctx:
        def sb(name, shape, dt=F32):
            return ctx.enter_context(nc.sbuf_tensor(tag + name, shape, dt))

        def ps(name, shape, dt=F32):
            return ctx.enter_context(nc.psum_tensor(tag + name, shape, dt))

        def sem(name):
            return a["layer_semaphores"](tag + name)

        w1 = sb("w1", [P, 2 * HID])
        w2 = sb("w2", [P, NC, D])
        b1 = sb("b1", [P, 2, NC])
        ln = sb("ln", [P, 2])
        b2 = sb("b2", [P, 1])
        eps = sb("eps", [P, 1])
        hn = sb("hn", [P, 2, S])
        gate = sb("gate", [P, 2, NC, S])
        prod = sb("prod", [P, 2, NC, S])
        a_ps = ps("a", [P, NC, S])
        g_ps = ps("g", [P, NC, S])
        o_ps = ps("o", [P, S])
        loaded, eps_set = sem("loaded"), sem("eps_set")
        dev_made, inv_made, div_made, hn_made = sem("dev"), sem("inv"), sem("div"), sem("hn")
        a_filled, g_filled = sem("a_filled"), sem("g_filled")
        gate_made, prod_made = sem("gate_made"), sem("prod_made")
        o_filled, x_added = sem("o_filled"), sem("x_added")
        loads = [(w1[:], a["fw1"][layer]), (b1[:].rearrange("p s c -> p (s c)"), a["fb1"][layer]),
                 (ln[:], a["fln"][layer]), (b2[:], a["fb2"][layer])]
        loads += [(w2[0:m, i, :], a["fw2"][layer][c:c + m, :]) for i, (c, m) in enumerate(HC)]
        all_loaded = 16 * len(loads)
        block = ctx.enter_context(nc.Block())

        def batch_at(buf, b, turn):
            return flat(buf[:, bass.ds(b if isinstance(turn, int) else turn * 2 + b, 1), :])

        def run(eng, slot):
            over(eng, slot, 0, 2, 3, 2, B + 1)

        @block.sync
        def _(sp):
            for dst, src in loads:
                sp.dma_start(dst, src).then_inc(loaded, 16)

        @block.vector
        def _(dve):
            nc.vector.memset(eps[:], 1e-5).then_inc(eps_set, 1)
            with dve.Fori(0, B) as b:
                dve.wait_ge(dev_made, b + 1)
                v = flat(VAR[:, bass.ds(b, 1), :])
                nc.vector.reciprocal(v, v).then_inc(inv_made, 1)
            dve.wait_ge(inv_made, B)
            dve.wait_ge(loaded, all_loaded)

            def slot(n, turn):
                b = n
                if b < B:
                    wait(dve, hn_made, b - 1, turn, 2)
                    c = batch_at(C, b, turn)
                    nc.vector.tensor_tensor(c, c, batch_at(VAR, b, turn), ALU.mult).then_inc(div_made, 1)
                    wait(dve, div_made, b + 1, turn, 2)
                    wait(dve, g_filled, NC * (b - 1), turn, 2 * NC)
                    nc.vector.tensor_scalar(hn[:, b % 2, :], c, ln[:, 0:1], ln[:, 1:2],
                                            ALU.mult, ALU.add).then_inc(hn_made, 1)
                    for i, (_, m) in enumerate(HC):
                        wait(dve, a_filled, NC * b + i + 1, turn, 2 * NC)
                        wait(dve, gate_made, NC * b + i + 1, turn, 2 * NC)
                        wait(dve, o_filled, b - 1, turn, 2)
                        nc.vector.scalar_tensor_tensor(out=prod[0:m, b % 2, i, :], in0=a_ps[0:m, i, :],
                                                       scalar=b1[0:m, 0, i:i + 1], in1=gate[0:m, b % 2, i, :],
                                                       op0=ALU.add, op1=ALU.mult).then_inc(prod_made, 1)
                b = n - 1
                if 0 <= b < B:
                    wait(dve, o_filled, b + 1, turn, 2)
                    x = batch_at(XT, b, turn)
                    nc.vector.scalar_tensor_tensor(out=x, in0=o_ps[:], scalar=b2[:, 0:1], in1=x,
                                                   op0=ALU.add, op1=ALU.add).then_inc(x_added, 1)

            run(dve, slot)

        @block.scalar
        def _(act):
            act.wait_ge(eps_set, 1)
            with act.Fori(0, B) as b:
                v = flat(VAR[:, bass.ds(b, 1), :])
                nc.scalar.activation(v, v, ACT.Sqrt, bias=eps[:]).then_inc(dev_made, 1)
            act.wait_ge(loaded, all_loaded)

            def slot(n, turn):
                b = n
                if b < B:
                    for i, (_, m) in enumerate(HC):
                        wait(act, g_filled, NC * b + i + 1, turn, 2 * NC)
                        wait(act, prod_made, NC * (b - 1), turn, 2 * NC)
                        nc.scalar.activation(gate[0:m, b % 2, i, :], g_ps[0:m, i, :], ACT.Gelu,
                                             bias=b1[0:m, 1, i:i + 1]).then_inc(gate_made, 1)

            run(act, slot)

        @block.tensor
        def _(pe):
            pe.wait_ge(loaded, all_loaded)

            def slot(n, turn):
                b = n
                if b < B:
                    wait(pe, hn_made, b + 1, turn, 2)
                    for i, (c, m) in enumerate(HC):
                        wait(pe, prod_made, NC * (b - 1) + i + 1, turn, 2 * NC)
                        nc.tensor.matmul(g_ps[0:m, i, :], w1[:, HID + c:HID + c + m], hn[:, b % 2, :],
                                         start=True, stop=True).then_inc(g_filled, 1)
                        nc.tensor.matmul(a_ps[0:m, i, :], w1[:, c:c + m], hn[:, b % 2, :],
                                         start=True, stop=True).then_inc(a_filled, 1)
                b = n - 1
                if 0 <= b < B:
                    wait(pe, prod_made, NC * (b + 1), turn, 2 * NC)
                    wait(pe, x_added, b, turn, 2)
                    for i, (_, m) in enumerate(HC):
                        mm = nc.tensor.matmul(o_ps[:], w2[0:m, i, :], prod[0:m, b % 2, i, :],
                                              start=(i == 0), stop=(i == NC - 1))
                    mm.then_inc(o_filled, 1)

            run(pe, slot)


def add_and_store(nc, a, X, XT):
    out_tiles = a["out"].rearrange("b (t p) d -> p b t d", p=P)
    with ExitStack() as ctx:
        def sem(name):
            return a["semaphores"].enter_context(nc.semaphore("end_" + name))

        ident = ctx.enter_context(nc.sbuf_tensor("end_ident", [P, P], F32))
        t_ps = ctx.enter_context(nc.psum_tensor("end_ps", [P, 2, S], F32))
        xt = ctx.enter_context(nc.sbuf_tensor("end_xt", [P, 2, S], F32))
        loaded, copied, turned, added, stored = (sem(x) for x in ("loaded", "copied", "turned", "added", "stored"))
        block = ctx.enter_context(nc.Block())

        def run(eng, slot):
            over(eng, slot, 0, 2, 3, 2, B)

        @block.sync
        def _(sp):
            sp.dma_start(ident[:], a["ident"]).then_inc(loaded, 16)
            for b in range(B):
                sp.wait_ge(added, b + 1)
                sp.dma_start(out_tiles[:, b], X[:, b * TPB:(b + 1) * TPB, :]).then_inc(stored, 16)
            sp.wait_ge(stored, 16 * B)

        @block.scalar
        def _(act):
            def slot(n, turn):
                wait(act, turned, n - 1, turn, 2)
                b = n if isinstance(turn, int) else turn * 2 + n
                nc.scalar.activation(xt[:, n % 2, :], flat(XT[:, bass.ds(b, 1), :]), ACT.Copy).then_inc(copied, 1)

            run(act, slot)

        @block.tensor
        def _(pe):
            pe.wait_ge(loaded, 16)

            def slot(n, turn):
                wait(pe, copied, n + 1, turn, 2)
                wait(pe, added, n - 1, turn, 2)
                for t in range(TPB):
                    mm = nc.tensor.transpose(t_ps[:, n % 2, t * P:(t + 1) * P],
                                             xt[:, n % 2, t * P:(t + 1) * P], ident[:])
                mm.then_inc(turned, 1)

            run(pe, slot)

        @block.vector
        def _(dve):
            def slot(n, turn):
                wait(dve, turned, n + 1, turn, 2)
                first = n * TPB if isinstance(turn, int) else turn * (2 * TPB) + n * TPB
                x = X[:, bass.ds(first, TPB), :]
                nc.vector.tensor_tensor(x, t_ps[:, n % 2, :].rearrange("p (t d) -> p t d", d=D), x,
                                        ALU.add).then_inc(added, 1)

            run(dve, slot)


def rotary_tables():
    half = np.arange(0, LD, 2, dtype=np.float32)
    inv_freq = (1.0 / 10000.0 ** (half / LD)).astype(np.float32)
    t = np.arange(S, dtype=np.float32)
    freqs = (t[:, None] * inv_freq[None, :]).astype(np.float32)
    base = ((half + 0.4 * LD) / (1.4 * LD)).astype(np.float32)
    power = ((t - S // 2) / float(WIN // 2)).astype(np.float32)
    scale = (base[None, :] ** power[:, None]).astype(np.float32)
    cos, sin = np.cos(freqs), np.sin(freqs)
    sides = []
    for c, s in ((cos * scale, sin * scale), (cos / scale, sin / scale)):
        sides.append(np.stack([np.concatenate([c, c], 1), np.concatenate([-s, s], 1)], 1))
    return np.ascontiguousarray(np.stack(sides, 1).astype(np.float32))


def band_mask():
    i, j = np.arange(P)[:, None], np.arange(KEYS)[None, :]
    return np.where((j <= i + WIN) & (j >= i), 0.0, NEG).astype(np.float32)




def kernel(**inputs):
    import numpy as _np
    import concourse.bacc as _bacc
    from concourse.bass_utils import run_bass_kernel_spmd as _run

    nc = _bacc.Bacc("TRN2", target_bir_lowering=False, num_devices=1)
    arrays = layouts(inputs)
    aps = {name: nc.dram_tensor(f"in_{name}", v.shape, mybir.dt.from_np(v.dtype), kind="ExternalInput").ap()
           for name, v in arrays.items()}
    aps["out"] = nc.dram_tensor("out", (B, S, D), F32, kind="ExternalOutput").ap()
    build(nc, aps)
    r = _run(nc, [{f"in_{k}": v for k, v in arrays.items()}], core_ids=[0])
    return r.results[0]["out"]
```

```python
from contextlib import ExitStack

import numpy as np

import concourse.bass as bass
from concourse import mybir

ALU = mybir.AluOpType
ACT = mybir.ActivationFunctionType
AX = mybir.AxisListType
F32 = mybir.dt.float32
F16 = mybir.dt.float16
BF16 = mybir.dt.bfloat16

P = 128
B, S, D = 8, 512, 128
DEPTH = 2
TPB = S // P
NT = B * TPB

H, DH, NB = 16, 8, 32
MLP = 512
SHIFT = 64.0

UNITS = 8
SLOTS = 4 * UNITS
PAIR = 2 * SLOTS
LEAD_SCORES = 1
LEAD_MAX = 13
LEAD_PREP = 42
FIRST_SLOT = -LEAD_PREP
LAST_SLOT = B * SLOTS + 6
LOOP_FROM = 22
LOOP_TURNS = 3
LOOP_TO = LOOP_FROM + LOOP_TURNS * PAIR
TILE_SLOTS = 5


def streams(n):
    s = {}
    x = n + LEAD_SCORES
    s["scores"] = x if 0 <= x < B * SLOTS else None
    x = n + LEAD_MAX
    s["max"] = x if 0 <= x < B * SLOTS else None
    s["exp"] = n if 0 <= n < B * SLOTS else None
    s["pv"] = n // 2 - 1 if n % 2 == 0 and 2 <= n <= B * SLOTS else None
    s["out"] = n // UNITS - 1 if n % UNITS == 0 and UNITS <= n <= B * SLOTS else None
    prep, k = (n + LEAD_PREP) // SLOTS, (n + LEAD_PREP) % SLOTS
    s["prep"] = [] if not 0 <= prep < B else [
        (prep * TPB + t, k - TILE_SLOTS * t) for t in range(TPB) if 0 <= k - TILE_SLOTS * t <= 13]
    return s


def bench_uses(n):
    s = streams(n)
    uses = []
    for step, at in (("stack_q0", 10), ("stack_q1", 11), ("stack_k0", 12), ("stack_k1", 13),
                     ("xn", 1), ("qkv", 2), ("clq", 3), ("clk", 4)):
        uses += [(step, tile) for tile, k in s["prep"] if k == at]
    x = n - UNITS - 1
    if x % UNITS == 0 and 0 <= x // UNITS < B * 4:
        uses.append(("heads_out", x // UNITS))
    x = n - SLOTS - 3
    if x % SLOTS == 0 and 0 <= x // SLOTS < B:
        uses.append(("att_t", x // SLOTS))
    x = n - SLOTS - 5
    if x % SLOTS == 0 and 0 <= x // SLOTS < B:
        uses.append(("proj", x // SLOTS))
    x = n + 5
    if x % UNITS == 0 and 0 <= x // UNITS < B * 4:
        uses.append(("shift", x // UNITS))
    return uses


STACKS = ("stack_q0", "stack_q1", "stack_k0", "stack_k1")
VECTOR_EMPTIES = ("clq", "clk", "heads_out", "proj", "shift")
BENCH_ORDER = {}
for _n in range(FIRST_SLOT, LAST_SLOT):
    for _u in bench_uses(_n):
        BENCH_ORDER[(_n, _u)] = len(BENCH_ORDER)
BENCH_LIST = list(BENCH_ORDER)
BENCH_BANKS = 3
BENCH_PER_PAIR = sum(len(bench_uses(n)) for n in range(LOOP_FROM, LOOP_FROM + PAIR))


def over_slots(eng, slot):
    for n in range(FIRST_SLOT, LOOP_FROM):
        slot(n, 0)
    with eng.Fori(0, LOOP_TURNS) as turn:
        for n in range(LOOP_FROM, LOOP_FROM + PAIR):
            slot(n, turn)
    for n in range(LOOP_TO, LAST_SLOT):
        slot(n, 0)


def before(n, use):
    order = BENCH_ORDER[(n, use)] - BENCH_BANKS
    return BENCH_LIST[order][1] if order >= 0 else None


def bank_of(n, use):
    return BENCH_ORDER[(n, use)] % BENCH_BANKS


def wait(eng, sem, count, turn=0, per_pair=0):
    if isinstance(turn, int):
        if count > 0:
            eng.wait_ge(sem, count)
    else:
        assert count > 0
        eng.wait_ge(sem, turn * per_pair + count)


def tile_at(turn, tile):
    return tile if isinstance(turn, int) else turn * (2 * TPB) + tile


def build(nc, a, debug=None):
    with ExitStack() as ctx:
        a["semaphores"] = ctx

        def sb(name, shape, dt=F32, c=ctx):
            return c.enter_context(nc.sbuf_tensor(name, shape, dt))

        X = sb("X", [P, NT, D])
        Z = sb("Z", [P, NT, D])
        R1 = sb("R1", [P, NT])
        normalise_input(nc, a, X, Z, R1)
        clustered_attention(nc, a, Z, R1)
        if debug == "A":
            store_tokens(nc, a, Z)
            return
        mean = sb("mean", [P, NT])
        inv_dev = sb("inv_dev", [P, NT])
        token_moments(nc, a, Z, mean, inv_dev, 1e-6, "m2_")
        attention_mlp(nc, a, X, Z, mean, inv_dev)
        if debug == "M":
            store_tokens(nc, a, X)
            return
        token_moments(nc, a, X, mean, inv_dev, 1e-5, "m3_")
        XT = sb("XT", [P, B, S])
        VAR = sb("VAR", [P, B, S])
        turn_tokens(nc, a, X, mean, inv_dev, XT)
        for layer in range(DEPTH):
            taken = []

            def take(name):
                taken.append(nc.alloc_semaphore(name=name))
                return taken[-1]

            a["layer_semaphores"] = take
            local_attention(nc, a, layer, XT, Z[:].rearrange("p (b t) d -> p b (t d)", b=B), VAR)
            gated_ffn(nc, a, layer, XT, Z[:].rearrange("p (b t) d -> p b (t d)", b=B), VAR)
            clear(nc, taken)
            if debug == "L%d" % layer:
                break
        add_and_store(nc, a, X, XT)


def _np_of(dtype):
    return mybir.dt.np(dtype)


def layouts(inputs):
    i = {k: np.ascontiguousarray(v) for k, v in inputs.items()}
    eye = np.zeros((P, P), np.float32)
    eye[np.arange(P), np.arange(P)] = 1

    def hash_blocks(w):
        out = np.zeros((H, DH, H, NB), np.float32)
        for h in range(H):
            out[h, :, h, :] = w[h]
        return out.reshape(P, H * NB)

    a = {
        "x": i["L0_attn_inputs"], "ident": eye, "ident16": eye.astype(np.float16),
        "wq": i["L0_attn_Wq"].reshape(P, P), "wk": i["L0_attn_Wk"].reshape(P, P),
        "wv": i["L0_attn_Wv"].reshape(P, P),
        "wqT": np.ascontiguousarray(i["L0_attn_Wq"].reshape(P, P).T),
        "wkT": np.ascontiguousarray(i["L0_attn_Wk"].reshape(P, P).T),
        "whq": hash_blocks(i["L0_attn_Whq"]), "whk": hash_blocks(i["L0_attn_Whk"]),
        "wo": i["L0_attn_Wo"].reshape(P, P),
        "ln1_g": i["L0_attn_ln1_g"].reshape(P, 1), "ln1_b": i["L0_attn_ln1_b"].reshape(P, 1),
    }
    swap = np.r_[LD // 2:LD, 0:LD // 2]
    gains = np.stack([np.stack([g, g[:, swap]], 1) for g in (i["L0_ffn_q_scale"], i["L0_ffn_k_scale"])], 1)

    def chunks(v):
        out = np.zeros((DEPTH, P, 2, len(HC)), np.float32)
        for side in range(2):
            for n, (c, m) in enumerate(HC):
                out[:, :m, side, n] = v[:, side * HID + c:side * HID + c + m]
        return out.reshape(DEPTH, P, -1)

    a |= {
        "mlp_w1": i["L0_attn_W1"], "mlp_w2": i["L0_attn_W2"],
        "mlp_b1": np.ascontiguousarray(i["L0_attn_b1"].reshape(MLP // P, P).T),
        "ln2_g": i["L0_attn_ln2_g"].reshape(P, 1), "ln2_b": i["L0_attn_ln2_b"].reshape(P, 1),
        "mlp_b2_rows": np.ascontiguousarray(np.broadcast_to(i["L0_attn_b2"], (P, D))),
        "identb": eye.astype(_np_of(BF16)), "band": band_mask().astype(_np_of(BF16)),
        "mean_of": np.full((P, P), 1.0 / D, np.float32),
        "wqkv": i["L0_ffn_wqkv"], "lwo": i["L0_ffn_wo"], "rot": rotary_tables(),
        "gains": np.ascontiguousarray(np.broadcast_to(gains.reshape(DEPTH, 1, -1), (DEPTH, P, 4 * LD))),
        "fw1": i["L0_ffn_w1"], "fb1": chunks(i["L0_ffn_b1"]),
        "fln": np.ascontiguousarray(np.stack([i["L0_ffn_ln_g"], i["L0_ffn_ln_b"]], 2)),
        "fb2": i["L0_ffn_b2"].reshape(DEPTH, P, 1), "fw2": i["L0_ffn_w2"],
    }
    return a


def store_tokens(nc, a, src):
    with nc.semaphore("stored") as stored, nc.Block() as block:
        @block.sync
        def _(sp):
            sp.dma_start(a["out"].rearrange("b (t p) d -> p (b t) d", p=P), src[:]).then_inc(stored, 16)
            sp.wait_ge(stored, 16)


def normalise_input(nc, a, X, Z, R1):
    x_tiles = a["x"].rearrange("b (t p) d -> p b t d", p=P)
    with ExitStack() as ctx:
        def sb(name, shape, dt=F32):
            return ctx.enter_context(nc.sbuf_tensor(name, shape, dt))

        def sem(name):
            return a["semaphores"].enter_context(nc.semaphore(name))

        stats = sb("in_stats", [P, NT, 6])
        moments = sb("in_moments", [P, NT, 2])
        dev = sb("in_dev", [P, NT])
        r0 = sb("in_r0", [P, NT])
        var1 = sb("in_var1", [P, NT])
        dev1 = sb("in_dev1", [P, NT])
        eps = sb("in_eps", [P, 2])
        loaded = [sem(f"in_loaded{b}") for b in range(B)]
        stats_done = sem("in_stats_done")
        moments_done = sem("in_moments_done")
        eps_set = sem("in_eps_set")
        dev_done = sem("in_dev_done")
        r0_done = sem("in_r0_done")
        r0_sq_done = sem("in_r0_sq_done")
        var1_done = sem("in_var1_done")
        block = ctx.enter_context(nc.Block())

        @block.sync
        def _(sp):
            for b in range(B):
                sp.dma_start(X[:, b * TPB:(b + 1) * TPB, :], x_tiles[:, b]).then_inc(loaded[b], 16)

        @block.vector
        def _(dve):
            nc.vector.memset(eps[:, 0:1], 1e-5)
            nc.vector.memset(eps[:, 1:2], 1e-6).then_inc(eps_set, 1)
            for b in range(B):
                dve.wait_ge(loaded[b], 16)
                for t in range(b * TPB, (b + 1) * TPB):
                    nc.vector.bn_stats(stats[:, t, :], X[:, t, :]).then_inc(stats_done, 1)
                    if t:
                        dve.wait_ge(stats_done, t)
                        nc.vector.bn_aggr(moments[:, t - 1, :], stats[:, t - 1, :])
            dve.wait_ge(stats_done, NT)
            nc.vector.bn_aggr(moments[:, NT - 1, :], stats[:, NT - 1, :]).then_inc(moments_done, 1)
            dve.wait_ge(moments_done, 1)
            dve.wait_ge(dev_done, 1)
            nc.vector.reciprocal(r0[:], dev[:]).then_inc(r0_done, 1)
            dve.wait_ge(r0_done, 1)
            nc.vector.tensor_tensor(var1[:], r0[:], r0[:], ALU.mult).then_inc(r0_sq_done, 1)
            dve.wait_ge(r0_sq_done, 1)
            nc.vector.tensor_tensor(var1[:], var1[:], moments[:, :, 1], ALU.mult).then_inc(var1_done, 1)
            with dve.Fori(0, NT) as t:
                nc.vector.tensor_scalar(Z[:, bass.ds(t, 1), :].rearrange("p t d -> p (t d)"),
                                        X[:, bass.ds(t, 1), :].rearrange("p t d -> p (t d)"),
                                        moments[:, bass.ds(t, 1), 0], r0[:, bass.ds(t, 1)],
                                        ALU.subtract, ALU.mult)
            dve.wait_ge(dev_done, 2)
            nc.vector.reciprocal(R1[:], dev1[:])

        @block.scalar
        def _(act):
            act.wait_ge(eps_set, 1)
            act.wait_ge(moments_done, 1)
            nc.scalar.activation(dev[:], moments[:, :, 1], ACT.Sqrt, bias=eps[:, 0:1]).then_inc(dev_done, 1)
            act.wait_ge(var1_done, 1)
            nc.scalar.activation(dev1[:], var1[:], ACT.Sqrt, bias=eps[:, 1:2]).then_inc(dev_done, 1)


def clustered_attention(nc, a, Z, R1):
    with ExitStack() as ctx:
        def sb(name, shape, dt=F32):
            return ctx.enter_context(nc.sbuf_tensor(name, shape, dt))

        def ps(name, shape, dt=F32):
            return ctx.enter_context(nc.psum_tensor(name, shape, dt))

        def sem(name):
            return a["semaphores"].enter_context(nc.semaphore(name))

        ident = sb("ident", [P, P])
        ident16 = sb("ident16", [P, P], F16)
        w_qkv = sb("w_qkv", [P, 3, D])
        w_qT = sb("w_qT", [P, 2, D])
        w_hash = sb("w_hash", [P, 2, H * NB])
        w_cl = sb("w_cl", [P, 2, H * NB])
        w_o = sb("w_o", [P, D])
        ln1 = sb("ln1", [P, 2])
        xn = sb("xn", [P, 2, D])
        xnT = sb("xnT", [P, 2, P])
        qkv = sb("qkv", [P, 2, 3, D])
        cl = sb("cl", [P, 2, 2, H * NB])
        cl_max = sb("cl_max", [P, 2, 2, H])
        cl_sum = sb("cl_sum", [P, 2, 2, H])
        cl_inv = sb("cl_inv", [P, 2, 2, H])
        stack_tok = sb("stack_tok", [P, 2, H, P], F16)
        stack = sb("stack", [P, 2, 2, H, S], F16)
        v_pad = sb("v_pad", [P, 2, TPB, H, 32])
        row_max = sb("row_max", [P, 2, TPB, 4])
        shift_tok = sb("shift_tok", [P, TPB, 2, 4], F16)
        shift_row = sb("shift_row", [8, S], F16)
        prob = sb("prob", [P, 4, 4, S])
        heads_raw = sb("heads_raw", [P, S])
        inv_sum = sb("inv_sum", [P, TPB, 4])
        att_tok = sb("att_tok", [P, TPB, H, DH])
        att_T = sb("att_T", [P, S])

        scores_ps = ps("scores_ps", [P, 2, S])
        max_ps = ps("max_ps", [P, 2, S])
        heads_ps = ps("heads_ps", [P, S])
        bench_ps = ps("bench", [P, BENCH_BANKS, S])

        with ExitStack() as setup:
            w_loaded = a["semaphores"].enter_context(nc.semaphore("w_loaded"))
            folded = a["semaphores"].enter_context(nc.semaphore("folded"))
            block = setup.enter_context(nc.Block())
            loads = [(ident[:], a["ident"]), (ident16[:], a["ident16"]),
                     (w_qkv[:, 0, :], a["wq"]), (w_qkv[:, 1, :], a["wk"]), (w_qkv[:, 2, :], a["wv"]),
                     (w_qT[:, 0, :], a["wqT"]), (w_qT[:, 1, :], a["wkT"]),
                     (w_hash[:, 0, :], a["whq"]), (w_hash[:, 1, :], a["whk"]),
                     (w_o[:], a["wo"]), (ln1[:, 0:1], a["ln1_g"]), (ln1[:, 1:2], a["ln1_b"])]

            @block.sync
            def _(sp):
                for dst, src in loads:
                    sp.dma_start(dst, src).then_inc(w_loaded, 16)

            @block.tensor
            def _(pe):
                pe.wait_ge(w_loaded, 16 * len(loads))
                for i in range(2):
                    nc.tensor.matmul(max_ps[:, i, :], w_qT[:, i, :], w_hash[:, i, :],
                                     start=True, stop=True).then_inc(folded, 1)

            @block.vector
            def _(dve):
                nc.vector.memset(stack_tok[:], 0.0).then_inc(folded, 1)
                nc.vector.memset(v_pad[:], 0.0).then_inc(folded, 1)
                dve.wait_ge(folded, 4)
                nc.vector.memset(stack_tok[:, 1, :, 120:122], -SHIFT)
                nc.vector.memset(v_pad[:, :, :, :, DH:DH + 1], 1.0)
                for i in range(2):
                    nc.vector.tensor_copy(w_cl[:, i, :], max_ps[:, i, :])
                dve.wait_ge(w_loaded, 16 * len(loads))
                nc.vector.tensor_scalar(w_qkv[:, 0, :], w_qkv[:, 0, :], float(DH) ** -0.5, None, ALU.mult)

        bench_filled = sem("bench_filled")
        proj_added = sem("proj_added")
        xn_made = sem("xn_made")
        xnT_made = sem("xnT_made")
        qkv_made = sem("qkv_made")
        cl_max_made = sem("cl_max_made")
        cl_sub_made = sem("cl_sub_made")
        cl_exp_made = sem("cl_exp_made")
        cl_sum_made = sem("cl_sum_made")
        cl_inv_made = sem("cl_inv_made")
        cl_scaled = sem("cl_scaled")
        cl_share_made = sem("cl_share_made")
        hi_made = sem("hi_made")
        lo_made = sem("lo_made")
        v_made = sem("v_made")
        stack_made = sem("stack_made")
        max_scored = sem("max_scored")
        max_made = sem("max_made")
        shift_hi_made = sem("shift_hi_made")
        shift_made = sem("shift_made")
        shift_row_made = sem("shift_row_made")
        shift_placed = sem("shift_placed")
        scored = sem("scored")
        exp_made = sem("exp_made")
        pv_made = sem("pv_made")
        heads_moved = sem("heads_moved")
        inv_made = sem("inv_made")
        att_made = sem("att_made")
        att_T_made = sem("att_T_made")
        block = ctx.enter_context(nc.Block())

        def filled(eng, n, turn, use):
            wait(eng, bench_filled, BENCH_ORDER[(n, use)] + 1, turn, BENCH_PER_PAIR)

        @block.tensor
        def _(pe):
            def bench_is_free(n, turn, use):
                if before(n, use) is None:
                    return
                step, x = before(n, use)
                if step == "xn":
                    wait(pe, xnT_made, x + 1, turn, 2 * TPB)
                elif step == "qkv":
                    wait(pe, qkv_made, x + 1, turn, 2 * TPB)
                elif step in ("clq", "clk"):
                    wait(pe, cl_sub_made, 2 * x + (step == "clk") + 1, turn, 4 * TPB)
                elif step[:5] == "stack":
                    wait(pe, stack_made, 4 * x + STACKS.index(step) + 1, turn, 8 * TPB)
                elif step == "heads_out":
                    wait(pe, att_made, x + 1, turn, 8)
                elif step == "att_t":
                    wait(pe, att_T_made, x + 1, turn, 2)
                elif step == "proj":
                    wait(pe, proj_added, x + 1, turn, 2)
                elif step == "shift":
                    wait(pe, shift_row_made, x + 1, turn, 8)

            def make_scores(u, i, turn):
                par, g, kt, pr = u // SLOTS % 2, u // UNITS % 4, u % UNITS // 2, u % 2
                if u % UNITS == 0 and i == 0:
                    wait(pe, shift_placed, 32 * (u // UNITS + 1), turn, 32 * 8)
                wait(pe, exp_made, 2 * u + i - 1, turn, 2 * PAIR)
                h = 4 * g + 2 * pr + i
                nc.tensor.matmul(scores_ps[:, i, :], stack[:, par, 1, h, kt * P:(kt + 1) * P],
                                 stack[:, par, 0, h, :], start=True, stop=True).then_inc(scored, 1)

            def make_max_scores(u, i, turn):
                par, g, w = u // SLOTS % 2, u // UNITS % 4, u % UNITS
                h = 4 * g + w // 2
                if u % SLOTS == 0 and i == 0:
                    wait(pe, stack_made, 16 * (u // SLOTS + 1), turn, 16 * 2)
                qt = 2 * (w % 2) + i
                wait(pe, max_made, 2 * u + i - 1, turn, 2 * PAIR)
                nc.tensor.matmul(max_ps[:, i, :], stack[:, par, 0, h, qt * P:(qt + 1) * P],
                                 stack[:, par, 1, h, :], start=True, stop=True).then_inc(max_scored, 1)

            def weight_values(c, turn):
                par, g, kt = c // 16 % 2, c // 4 % 4, c % 4
                wait(pe, exp_made, 4 * c + 4, turn, 2 * PAIR)
                if kt == 0:
                    wait(pe, heads_moved, c // 4, turn, 8)
                    if g == 0:
                        wait(pe, v_made, TPB * (c // 16 + 1), turn, 2 * TPB)
                for j in range(4):
                    mm = nc.tensor.matmul(heads_ps[32 * j:32 * j + 32, :],
                                          v_pad[:, par, kt, 4 * g + j, :],
                                          prob[:, c % 4, j, :],
                                          start=(kt == 0), stop=(kt == 3))
                mm.then_inc(pv_made, 1)

            def fill_bench(n, turn, use):
                bench = bench_ps[:, bank_of(n, use), :]
                bench16 = bench.bitcast(F16)
                bench_is_free(n, turn, use)
                step, x = use
                if step == "xn":
                    wait(pe, xn_made, x + 1, turn, 2 * TPB)
                    mm = nc.tensor.transpose(bench[:, 0:P], xn[:, x % 2, :], ident[:])
                elif step == "qkv":
                    wait(pe, xnT_made, x + 1, turn, 2 * TPB)
                    mm = nc.tensor.matmul(bench[:, 0:3 * D], xnT[:, x % 2, :],
                                          w_qkv[:].rearrange("p a b -> p (a b)"), start=True, stop=True)
                elif step in ("clq", "clk"):
                    mm = nc.tensor.matmul(bench, xnT[:, x % 2, :], w_cl[:, step == "clk", :],
                                          start=True, stop=True)
                elif step[:5] == "stack":
                    side, half = int(step[6] == "k"), int(step[7])
                    wait(pe, hi_made, 2 * x + side + 1, turn, 4 * TPB)
                    wait(pe, lo_made, 2 * x + side + 1, turn, 4 * TPB)
                    for i in range(8):
                        mm = nc.tensor.transpose(bench16[:, i * P:(i + 1) * P],
                                                 stack_tok[:, side, 8 * half + i, :], ident16[:])
                elif step == "heads_out":
                    wait(pe, heads_moved, x + 1, turn, 8)
                    for qt in range(TPB):
                        mm = nc.tensor.transpose(bench[:, qt * P:(qt + 1) * P],
                                                 heads_raw[:, qt * P:(qt + 1) * P], ident[:])
                elif step == "att_t":
                    wait(pe, att_made, 4 * (x + 1), turn, 8)
                    for qt in range(TPB):
                        mm = nc.tensor.transpose(bench[:, qt * P:(qt + 1) * P],
                                                 att_tok[:, qt].rearrange("p h f -> p (h f)"), ident[:])
                elif step == "proj":
                    wait(pe, att_T_made, x + 1, turn, 2)
                    for qt in range(TPB):
                        mm = nc.tensor.matmul(bench[:, qt * D:(qt + 1) * D],
                                              att_T[:, qt * P:(qt + 1) * P], w_o[:],
                                              start=True, stop=True)
                elif step == "shift":
                    wait(pe, shift_made, x + 1, turn, 8)
                    for qt in range(TPB):
                        mm = nc.tensor.transpose(bench16[0:8, qt * P:(qt + 1) * P],
                                                 shift_tok[:, qt].rearrange("p s j -> p (s j)"), ident16[:])
                mm.then_inc(bench_filled, 1)

            def slot(n, turn):
                s, uses = streams(n), bench_uses(n)
                if s["max"] is not None:
                    make_max_scores(s["max"], 0, turn)
                for use in uses[0:1]:
                    fill_bench(n, turn, use)
                if s["scores"] is not None:
                    make_scores(s["scores"], 0, turn)
                if s["max"] is not None:
                    make_max_scores(s["max"], 1, turn)
                for use in uses[1:2]:
                    fill_bench(n, turn, use)
                if s["pv"] is not None:
                    weight_values(s["pv"], turn)
                if s["scores"] is not None:
                    make_scores(s["scores"], 1, turn)
                for use in uses[2:9]:
                    fill_bench(n, turn, use)

            over_slots(pe, slot)

        @block.vector
        def _(dve):
            def empty_bench(n, turn, use):
                step, x = use
                bench = bench_ps[:, bank_of(n, use), :]
                filled(dve, n, turn, use)
                if step in ("clq", "clk"):
                    side = int(step == "clk")
                    c = 2 * x + side
                    scores = bench.rearrange("p (h n) -> p h n", n=NB)
                    nc.vector.tensor_reduce(cl_max[:, x % 2, side, :], scores, AX.X,
                                            ALU.max).then_inc(cl_max_made, 1)
                    wait(dve, cl_max_made, c + 1, turn, 4 * TPB)
                    wait(dve, lo_made, c - 3, turn, 4 * TPB)
                    nc.vector.tensor_tensor(
                        cl[:, x % 2, side].rearrange("p (h n) -> p h n", n=NB), scores,
                        cl_max[:, x % 2, side, :].unsqueeze(2).to_broadcast([P, H, NB]),
                        ALU.subtract).then_inc(cl_sub_made, 1)
                elif step == "heads_out":
                    v = bench.rearrange("p (q j f) -> p q j f", q=TPB, j=4)
                    nc.vector.reciprocal(inv_sum[:], v[:, :, :, DH]).then_inc(inv_made, 1)
                    wait(dve, inv_made, x + 1, turn, 8)
                    if x % 4 == 0:
                        wait(dve, att_T_made, x // 4, turn, 2)
                    nc.vector.tensor_tensor(att_tok[:, :, 4 * (x % 4):4 * (x % 4) + 4, :],
                                            v[:, :, :, 0:DH],
                                            inv_sum[:].unsqueeze(3).to_broadcast([P, TPB, 4, DH]),
                                            ALU.mult).then_inc(att_made, 1)
                elif step == "proj":
                    first = x * TPB if isinstance(turn, int) else turn * (2 * TPB) + x * TPB
                    zz = Z[:, bass.ds(first, TPB), :]
                    nc.vector.tensor_tensor(zz, bench.rearrange("p (t d) -> p t d", d=D), zz,
                                            ALU.add).then_inc(proj_added, 1)
                elif step == "shift":
                    wait(dve, shift_placed, 32 * x, turn, 32 * 8)
                    nc.vector.tensor_copy(shift_row[:], bench.bitcast(F16)[0:8, 0:S]).then_inc(shift_row_made, 1)

            def slot(n, turn):
                s = streams(n)
                for tile, k in s["prep"]:
                    if k == 0:
                        wait(dve, xnT_made, tile - 1, turn, 2 * TPB)
                        T = tile_at(turn, tile)
                        nc.vector.tensor_scalar(xn[:, tile % 2, :],
                                                Z[:, bass.ds(T, 1), :].rearrange("p t d -> p (t d)"),
                                                R1[:, bass.ds(T, 1)], None, ALU.mult).then_inc(xn_made, 1)
                uses = [use for use in bench_uses(n) if use[0] in VECTOR_EMPTIES]
                summed = [(tile, k - 6) for tile, k in s["prep"] if k in (6, 7)]
                for tile, side in summed:
                    wait(dve, cl_exp_made, 2 * tile + side + 1, turn, 4 * TPB)
                    nc.vector.tensor_reduce(cl_sum[:, tile % 2, side, :],
                                            cl[:, tile % 2, side].rearrange("p (h n) -> p h n", n=NB),
                                            AX.X, ALU.add).then_inc(cl_sum_made, 1)
                for i in range(2):
                    if s["max"] is not None:
                        u = s["max"]
                        w, grp = u % UNITS, u // UNITS
                        wait(dve, max_scored, 2 * u + i + 1, turn, 2 * PAIR)
                        qt = 2 * (w % 2) + i
                        nc.vector.tensor_reduce(row_max[:, grp % 2, qt, w // 2:w // 2 + 1],
                                                max_ps[:, i, :], AX.X, ALU.max).then_inc(max_made, 1)
                    for tile, side in summed:
                        c, inv = 2 * tile + side, cl_inv[:, tile % 2, side, :]
                        if i == 0:
                            wait(dve, cl_sum_made, c + 1, turn, 4 * TPB)
                            nc.vector.reciprocal(inv, cl_sum[:, tile % 2, side, :]).then_inc(cl_inv_made, 1)
                        elif side == 0:
                            wait(dve, cl_inv_made, c + 1, turn, 4 * TPB)
                            nc.vector.tensor_scalar(inv, inv, 0.1, None, ALU.mult).then_inc(cl_scaled, 1)
                for use in uses:
                    empty_bench(n, turn, use)
                if s["max"] is not None and s["max"] % UNITS == UNITS - 1:
                    grp = s["max"] // UNITS
                    wait(dve, max_made, 16 * (grp + 1), turn, 16 * 8)
                    wait(dve, shift_row_made, grp, turn, 8)
                    nc.vector.tensor_scalar(shift_tok[:, :, 0, :], row_max[:, grp % 2], 1.0 / SHIFT,
                                            None, ALU.mult).then_inc(shift_hi_made, 1)
                    wait(dve, shift_hi_made, grp + 1, turn, 8)
                    nc.vector.scalar_tensor_tensor(out=shift_tok[:, :, 1, :], in0=row_max[:, grp % 2],
                                                   scalar=1.0 / SHIFT, in1=shift_tok[:, :, 0, :],
                                                   op0=ALU.mult, op1=ALU.subtract).then_inc(shift_made, 1)
                for tile, k in s["prep"]:
                    par = tile % 2
                    for side in range(2):
                        c = 2 * tile + side
                        if k == 8 + side:
                            wait(dve, cl_share_made, c + 1, turn, 4 * TPB)
                            wait(dve, stack_made, 4 * (tile - 1) + 2 * side + 2, turn, 8 * TPB)
                            share = cl[:, par, side].rearrange("p (h n) -> p h n", n=NB)
                            for dst in ((0, 2 * NB) if side == 0 else (0, NB)):
                                nc.vector.tensor_copy(stack_tok[:, side, :, dst:dst + NB], share)
                            feat = qkv[:, par, side].rearrange("p (h f) -> p h f", f=DH)
                            for dst in ((96, 112) if side == 0 else (96, 104)):
                                ins = nc.vector.tensor_copy(stack_tok[:, side, :, dst:dst + DH], feat)
                            ins.then_inc(hi_made, 1)

            over_slots(dve, slot)

        @block.scalar
        def _(act):
            def exponentiate(u, i, turn):
                kt_all, pr = u // 2, u % 2
                wait(act, scored, 2 * u + i + 1, turn, 2 * PAIR)
                wait(act, pv_made, kt_all - 3, turn, PAIR // 2)
                nc.scalar.activation(prob[:, kt_all % 4, 2 * pr + i, :], scores_ps[:, i, :],
                                     ACT.Exp).then_inc(exp_made, 1)

            def empty_bench(n, turn, use):
                step, x = use
                bench = bench_ps[:, bank_of(n, use), :]
                filled(act, n, turn, use)
                if step == "xn":
                    nc.scalar.activation(xnT[:, x % 2, :], bench[:, 0:P], ACT.Identity,
                                         bias=ln1[:, 1:2], scale=ln1[:, 0:1]).then_inc(xnT_made, 1)
                elif step == "qkv":
                    wait(act, v_made, x - 1, turn, 2 * TPB)
                    wait(act, lo_made, 2 * x - 2, turn, 4 * TPB)
                    nc.scalar.activation(qkv[:, x % 2].rearrange("p a b -> p (a b)"), bench[:, 0:3 * D],
                                         ACT.Copy).then_inc(qkv_made, 1)
                elif step == "att_t":
                    nc.scalar.activation(att_T[:], bench, ACT.Copy).then_inc(att_T_made, 1)
                else:
                    side, half = int(step[6] == "k"), int(step[7])
                    if x % TPB == 0 and side == 0 and half == 0:
                        wait(act, scored, 2 * SLOTS * (x // TPB - 1), turn, 2 * PAIR)
                    nc.scalar.activation(
                        stack[:, x // TPB % 2, side, 8 * half:8 * half + 8, x % TPB * P:(x % TPB + 1) * P],
                        bench.bitcast(F16).rearrange("p (h t) -> p h t", h=8),
                        ACT.Copy).then_inc(stack_made, 1)

            def slot(n, turn):
                s = streams(n)
                uses = [use for use in bench_uses(n) if use[0] not in VECTOR_EMPTIES]
                if s["exp"] is not None:
                    for i in range(2):
                        exponentiate(s["exp"], i, turn)
                for tile, k in s["prep"]:
                    if k == 10:
                        wait(act, qkv_made, tile + 1, turn, 2 * TPB)
                        wait(act, pv_made, 16 * (tile // TPB - 1), turn, PAIR // 2)
                        nc.scalar.activation(v_pad[:, tile // TPB % 2, tile % TPB, :, 0:DH],
                                             qkv[:, tile % 2, 2].rearrange("p (h f) -> p h f", f=DH),
                                             ACT.Copy).then_inc(v_made, 1)
                for use in uses:
                    empty_bench(n, turn, use)
                if s["out"] is not None:
                    g = s["out"]
                    wait(act, pv_made, 4 * (g + 1), turn, PAIR // 2)
                    wait(act, att_made, g, turn, 8)
                    nc.scalar.activation(heads_raw[:], heads_ps[:], ACT.Copy).then_inc(heads_moved, 1)
                for tile, k in s["prep"]:
                    for side in range(2):
                        if k == 4 + side:
                            wait(act, cl_sub_made, 2 * tile + side + 1, turn, 4 * TPB)
                            e = cl[:, tile % 2, side]
                            nc.scalar.activation(e, e, ACT.Exp).then_inc(cl_exp_made, 1)

            over_slots(act, slot)

        @block.gpsimd
        def _(pool):
            def slot(n, turn):
                for tile, k in streams(n)["prep"]:
                    par = tile % 2
                    for side in range(2):
                        c = 2 * tile + side
                        share = cl[:, par, side].rearrange("p (h n) -> p h n", n=NB)
                        feat = qkv[:, par, side].rearrange("p (h f) -> p h f", f=DH)
                        if k == 6 + side:
                            if side == 0:
                                wait(pool, cl_scaled, tile + 1, turn, 2 * TPB)
                            else:
                                wait(pool, cl_inv_made, c + 1, turn, 4 * TPB)
                            nc.gpsimd.tensor_tensor(
                                share, share, cl_inv[:, par, side, :].unsqueeze(2).to_broadcast([P, H, NB]),
                                ALU.mult).then_inc(cl_share_made, 1)
                        if k == 8 + side:
                            wait(pool, hi_made, c + 1, turn, 4 * TPB)
                            lo = NB if side == 0 else 2 * NB
                            nc.gpsimd.tensor_tensor(stack_tok[:, side, :, lo:lo + NB], share,
                                                    stack_tok[:, side, :, 0:NB], ALU.subtract)
                            lo = 104 if side == 0 else 112
                            nc.gpsimd.tensor_tensor(stack_tok[:, side, :, lo:lo + DH], feat,
                                                    stack_tok[:, side, :, 96:96 + DH],
                                                    ALU.subtract).then_inc(lo_made, 1)

            over_slots(pool, slot)

        @block.sync
        def _(sp):
            def slot(n, turn):
                for step, g in bench_uses(n):
                    if step == "shift":
                        wait(sp, shift_row_made, g + 1, turn, 8)
                        heads = slice(4 * (g % 4), 4 * (g % 4) + 4)
                        for part in range(2):
                            sp.dma_start(stack[120 + part:121 + part, g // 4 % 2, 0, heads, :],
                                         shift_row[4 * part:4 * part + 4, :]).then_inc(shift_placed, 16)

            over_slots(sp, slot)


def over(eng, slot, first, loop_from, turns, period, last):
    for n in range(first, loop_from):
        slot(n, 0)
    with eng.Fori(0, turns) as turn:
        for n in range(loop_from, loop_from + period):
            slot(n, turn)
    for n in range(loop_from + turns * period, last):
        slot(n, 0)


def flat(ap):
    return ap.rearrange("p a b -> p (a b)")


def clear(nc, semaphores):
    with nc.Block() as block:
        @block.gpsimd
        def _(pool):
            for s in semaphores:
                pool.sem_clear(s)
    for s in semaphores:
        nc.release_semaphore(s)


def token_moments(nc, a, src, mean, inv_dev, eps, tag):
    with ExitStack() as ctx:
        def sb(name, shape, dt=F32):
            return ctx.enter_context(nc.sbuf_tensor(tag + name, shape, dt))

        def sem(name):
            return a["semaphores"].enter_context(nc.semaphore(tag + name))

        stats = sb("stats", [P, NT, 6])
        moments = sb("moments", [P, NT, 2])
        dev = sb("dev", [P, NT])
        eps_col = sb("eps", [P, 1])
        stats_done = sem("stats_done")
        moments_done = sem("moments_done")
        dev_done = sem("dev_done")
        block = ctx.enter_context(nc.Block())

        @block.vector
        def _(dve):
            nc.vector.memset(eps_col[:], eps)
            with dve.Fori(0, NT) as t:
                nc.vector.bn_stats(stats[:, bass.ds(t, 1), :].rearrange("p a b -> p (a b)"),
                                   flat(src[:, bass.ds(t, 1), :])).then_inc(stats_done, 1)
            dve.wait_ge(stats_done, NT)
            for t in range(NT):
                nc.vector.bn_aggr(moments[:, t, :], stats[:, t, :]).then_inc(moments_done, 1)
            dve.wait_ge(moments_done, NT)
            nc.vector.tensor_copy(mean[:], moments[:, :, 0])
            dve.wait_ge(dev_done, 1)
            nc.vector.reciprocal(inv_dev[:], dev[:])

        @block.scalar
        def _(act):
            act.wait_ge(moments_done, NT)
            nc.scalar.activation(dev[:], moments[:, :, 1], ACT.Sqrt, bias=eps_col[:]).then_inc(dev_done, 1)


def attention_mlp(nc, a, X, Z, mean, inv_dev):
    MC = MLP // P
    with ExitStack() as ctx:
        def sb(name, shape, dt=F32):
            return ctx.enter_context(nc.sbuf_tensor("mlp_" + name, shape, dt))

        def ps(name, shape, dt=F32):
            return ctx.enter_context(nc.psum_tensor("mlp_" + name, shape, dt))

        def sem(name):
            return a["semaphores"].enter_context(nc.semaphore("mlp_" + name))

        ident = sb("ident", [P, P])
        w1 = sb("w1", [P, MLP])
        w2 = sb("w2", [P, MC, D])
        b1 = sb("b1", [P, MC])
        ln2 = sb("ln2", [P, 2])
        b2_rows = sb("b2_rows", [P, D])
        y = sb("y", [P, 2, TPB, D])
        yT = sb("yT", [P, 2, S])
        hid = sb("hid", [P, 2, MC, S])
        base = sb("base", [P, 2, TPB, D])
        t_ps = ps("t_ps", [P, S])
        h_ps = ps("h_ps", [P, MC, S])
        o_ps = ps("o_ps", [P, S])
        loaded = sem("loaded")
        y_made = sem("y_made")
        turned = sem("turned")
        yT_made = sem("yT_made")
        h_filled = sem("h_filled")
        h_act = sem("h_act")
        h_dve = sem("h_dve")
        o_filled = sem("o_filled")
        added = sem("added")
        base_half = sem("base_half")
        base_made = sem("base_made")
        loads = [(ident[:], a["ident"]), (w1[:], a["mlp_w1"]),
                 (w2[:], a["mlp_w2"].rearrange("(c p) d -> p c d", p=P)), (b1[:], a["mlp_b1"]),
                 (ln2[:, 0:1], a["ln2_g"]), (ln2[:, 1:2], a["ln2_b"]), (b2_rows[:], a["mlp_b2_rows"])]
        all_loaded = 16 * len(loads)
        block = ctx.enter_context(nc.Block())

        def tiles(buf, b, turn):
            first = b * TPB if isinstance(turn, int) else turn * (2 * TPB) + b * TPB
            return buf[:, bass.ds(first, TPB), :]

        def run(eng, slot):
            over(eng, slot, 0, 4, 2, 2, B + 2)

        @block.sync
        def _(sp):
            for dst, src in loads:
                sp.dma_start(dst, src).then_inc(loaded, 16)

        @block.vector
        def _(dve):
            dve.wait_ge(loaded, all_loaded)

            def slot(n, turn):
                b = n
                if b < B:
                    wait(dve, turned, b - 1, turn, 2)
                    for t in range(TPB):
                        T = b * TPB + t if isinstance(turn, int) else turn * (2 * TPB) + b * TPB + t
                        ins = nc.vector.tensor_scalar(y[:, b % 2, t, :], flat(Z[:, bass.ds(T, 1), :]),
                                                      mean[:, bass.ds(T, 1)], inv_dev[:, bass.ds(T, 1)],
                                                      ALU.subtract, ALU.mult)
                    ins.then_inc(y_made, 1)
                b = n - 1
                if 0 <= b < B:
                    for c in (1, 3):
                        wait(dve, h_filled, MC * b + c + 1, turn, 2 * MC)
                        wait(dve, o_filled, b - 1, turn, 2)
                        nc.vector.tensor_scalar(hid[:, b % 2, c, :], h_ps[:, c, :], b1[:, c:c + 1], 0.0,
                                                ALU.add, ALU.max).then_inc(h_dve, 1)
                b = n - 2
                if 0 <= b < B:
                    wait(dve, o_filled, b + 1, turn, 2)
                    wait(dve, base_made, b + 1, turn, 2)
                    nc.vector.tensor_tensor(tiles(X, b, turn), o_ps[:].rearrange("p (t d) -> p t d", d=D),
                                            base[:, b % 2], ALU.add).then_inc(added, 1)

            run(dve, slot)

        @block.gpsimd
        def _(pool):
            pool.wait_ge(loaded, all_loaded)

            def slot(n, turn):
                b = n - 1
                if 0 <= b < B:
                    wait(pool, added, b - 1, turn, 2)
                    nc.gpsimd.tensor_tensor(base[:, b % 2], tiles(X, b, turn), tiles(Z, b, turn),
                                            ALU.add).then_inc(base_half, 1)
                    wait(pool, base_half, b + 1, turn, 2)
                    nc.gpsimd.tensor_tensor(base[:, b % 2], base[:, b % 2],
                                            b2_rows[:].unsqueeze(1).to_broadcast([P, TPB, D]),
                                            ALU.add).then_inc(base_made, 1)

            run(pool, slot)

        @block.scalar
        def _(act):
            act.wait_ge(loaded, all_loaded)

            def slot(n, turn):
                b = n
                if b < B:
                    wait(act, turned, b + 1, turn, 2)
                    wait(act, h_filled, MC * (b - 1), turn, 2 * MC)
                    nc.scalar.activation(yT[:, b % 2, :], t_ps[:], ACT.Identity, bias=ln2[:, 1:2],
                                         scale=ln2[:, 0:1]).then_inc(yT_made, 1)
                b = n - 1
                if 0 <= b < B:
                    for c in (0, 2):
                        wait(act, h_filled, MC * b + c + 1, turn, 2 * MC)
                        wait(act, o_filled, b - 1, turn, 2)
                        nc.scalar.activation(hid[:, b % 2, c, :], h_ps[:, c, :], ACT.Relu,
                                             bias=b1[:, c:c + 1]).then_inc(h_act, 1)

            run(act, slot)

        @block.tensor
        def _(pe):
            pe.wait_ge(loaded, all_loaded)

            def slot(n, turn):
                b = n
                if b < B:
                    wait(pe, y_made, b + 1, turn, 2)
                    wait(pe, yT_made, b, turn, 2)
                    for t in range(TPB):
                        mm = nc.tensor.transpose(t_ps[:, t * P:(t + 1) * P], y[:, b % 2, t, :], ident[:])
                    mm.then_inc(turned, 1)
                b = n - 1
                if 0 <= b < B:
                    wait(pe, yT_made, b + 1, turn, 2)
                    for c in range(MC):
                        wait(pe, (h_act, h_dve)[c % 2], 2 * (b - 1) + c // 2 + 1, turn, 4)
                        nc.tensor.matmul(h_ps[:, c, :], w1[:, c * P:(c + 1) * P], yT[:, b % 2, :],
                                         start=True, stop=True).then_inc(h_filled, 1)
                b = n - 2
                if 0 <= b < B:
                    wait(pe, h_act, 2 * (b + 1), turn, 4)
                    wait(pe, h_dve, 2 * (b + 1), turn, 4)
                    wait(pe, added, b, turn, 2)
                    for t in range(TPB):
                        for c in range(MC):
                            mm = nc.tensor.matmul(o_ps[:, t * D:(t + 1) * D],
                                                  hid[:, b % 2, c, t * P:(t + 1) * P], w2[:, c, :],
                                                  start=(c == 0), stop=(c == MC - 1))
                    mm.then_inc(o_filled, 1)

            run(pe, slot)


def turn_tokens(nc, a, X, mean, inv_dev, XT):
    with ExitStack() as ctx:
        def sem(name):
            return a["semaphores"].enter_context(nc.semaphore("turn_" + name))

        ident = ctx.enter_context(nc.sbuf_tensor("turn_ident", [P, P], F32))
        w = ctx.enter_context(nc.sbuf_tensor("turn_w", [P, 2, TPB, D], F32))
        t_ps = ctx.enter_context(nc.psum_tensor("turn_ps", [P, 2, S], F32))
        loaded, made, turned, moved = sem("loaded"), sem("made"), sem("turned"), sem("moved")
        block = ctx.enter_context(nc.Block())

        def run(eng, slot):
            over(eng, slot, 0, 2, 3, 2, B)

        @block.sync
        def _(sp):
            sp.dma_start(ident[:], a["ident"]).then_inc(loaded, 16)

        @block.vector
        def _(dve):
            def slot(n, turn):
                wait(dve, turned, n - 1, turn, 2)
                for t in range(TPB):
                    T = n * TPB + t if isinstance(turn, int) else turn * (2 * TPB) + n * TPB + t
                    ins = nc.vector.tensor_scalar(w[:, n % 2, t, :], flat(X[:, bass.ds(T, 1), :]),
                                                  mean[:, bass.ds(T, 1)], inv_dev[:, bass.ds(T, 1)],
                                                  ALU.subtract, ALU.mult)
                ins.then_inc(made, 1)

            run(dve, slot)

        @block.tensor
        def _(pe):
            pe.wait_ge(loaded, 16)

            def slot(n, turn):
                wait(pe, made, n + 1, turn, 2)
                wait(pe, moved, n - 1, turn, 2)
                for t in range(TPB):
                    mm = nc.tensor.transpose(t_ps[:, n % 2, t * P:(t + 1) * P], w[:, n % 2, t, :], ident[:])
                mm.then_inc(turned, 1)

            run(pe, slot)

        @block.scalar
        def _(act):
            def slot(n, turn):
                wait(act, turned, n + 1, turn, 2)
                b = n if isinstance(turn, int) else turn * 2 + n
                nc.scalar.activation(flat(XT[:, bass.ds(b, 1), :]), t_ps[:, n % 2, :], ACT.Copy).then_inc(moved, 1)

            run(act, slot)


LH, LD, WIN = 8, 64, 64
INNER = LH * LD
KEYS = P + WIN
NEG = -1e30
LN_SCALE = 2.0 ** 20


def local_attention(nc, a, layer, XT, C, VAR):
    tag = f"la{layer}_"
    with ExitStack() as ctx:
        def sb(name, shape, dt=F32):
            return ctx.enter_context(nc.sbuf_tensor(tag + name, shape, dt))

        def ps(name, shape, dt=F32):
            return ctx.enter_context(nc.psum_tensor(tag + name, shape, dt))

        def sem(name):
            return a["layer_semaphores"](tag + name)

        ident = sb("ident", [P, P])
        identb = sb("identb", [P, P], BF16)
        band = sb("band", [P, KEYS], BF16)
        mean_of = sb("mean_of", [P, P])
        wqkv = sb("wqkv", [P, 3 * INNER])
        wo = sb("wo", [P, INNER // P, D])
        rot = sb("rot", [P, TPB, 2, 2, LD])
        gains = sb("gains", [P, 2, 2, LD])
        hT = sb("hT", [P, 2, S])
        raw = sb("raw", [P, 2, 2, INNER])
        plain = sb("plain", [P, 2, INNER])
        swapped = sb("swapped", [P, 2, INNER])
        turned = sb("turned", [P, 2, 2, INNER])
        squares = sb("squares", [P, 2, 2, INNER])
        sumsq = sb("sumsq", [P, 2, 2 * LH])
        lnsq = sb("lnsq", [P, 2, 2 * LH])
        inv = sb("inv", [P, 2, 2 * LH])
        newton = sb("newton", [P, 2 * LH])
        q_gain = sb("q_gain", [P, 4, LH])
        half_ln = sb("half_ln", [P, 1])
        three_halves = sb("three_halves", [P, 2 * LH])
        eight = sb("eight", [P, LH])
        qT = sb("qT", [P, 2, 4, P])
        kT = sb("kT", [P, 2, 4, S])
        v1 = sb("v1", [P, 2, TPB, LH, LD + 1])
        s_max = sb("s_max", [P, 2, 4])
        s_bias = sb("s_bias", [P, 2, 4])
        prob = sb("prob", [P, 2, 4, 2 * P])
        probT = sb("probT", [P, 2, 8, P])
        o_inv = sb("o_inv", [P, 4])
        o_tok = sb("o_tok", [P, 2, INNER])
        oT = sb("oT", [P, 2, 4, S])
        shifted = sb("shifted", [P, S])
        csq = sb("csq", [P, S])
        ring_ps = ps("ring", [P, 2, S])
        s_ps = ps("s", [P, 4, 2 * P])
        pT_ps = ps("pT", [P, 8, P])
        o_ps = ps("o", [P, 4, P])
        m_ps = ps("m", [P, S])
        loaded = sem("loaded")
        ready = sem("ready")
        gained = sem("gained")
        h_made = sem("h_made")
        ring_filled = sem("ring_filled")
        raw_made = sem("raw_made")
        rot_read = sem("rot_read")
        plain_made = sem("plain_made")
        sq_made = sem("sq_made")
        v_made = sem("v_made")
        qT_made = sem("qT_made")
        kT_made = sem("kT_made")
        added_rot = sem("added_rot")
        k_scaled = sem("k_scaled")
        sum_made = sem("sum_made")
        clip_made = sem("clip_made")
        ln_made = sem("ln_made")
        seed_made = sem("seed_made")
        nt1, nt2, nt3, inv_made = sem("newton1"), sem("newton2"), sem("newton3"), sem("inv_made")
        q_gain_made = sem("q_gain_made")
        s_filled = sem("s_filled")
        max_made = sem("max_made")
        bias_made = sem("bias_made")
        exp_made = sem("exp_made")
        pT_filled = sem("pT_filled")
        pT_made = sem("pT_made")
        o_filled = sem("o_filled")
        o_inv_made = sem("o_inv_made")
        o_made = sem("o_made")
        m_filled = sem("m_filled")
        oT_made = sem("oT_made")
        x_added = sem("x_added")
        sh_made = sem("sh_made")
        c_made = sem("c_made")
        csq_made = sem("csq_made")
        var_made = sem("var_made")

        loads = [(ident[:], a["ident"]), (identb[:], a["identb"]), (band[:], a["band"]),
                 (mean_of[:], a["mean_of"]), (wqkv[:], a["wqkv"][layer]),
                 (wo[:], a["lwo"][layer].rearrange("(c p) d -> p c d", p=P)),
                 (rot[:].rearrange("p t s w f -> p t (s w f)"), a["rot"].rearrange("(t p) s w f -> p t (s w f)", p=P)),
                 (gains[:].rearrange("p s w f -> p (s w f)"), a["gains"][layer])]
        all_loaded = 16 * len(loads)
        T_LAST = NT + 6
        block = ctx.enter_context(nc.Block())

        def batch_at(buf, b, turn):
            return flat(buf[:, bass.ds(b if isinstance(turn, int) else turn * 2 + b, 1), :])

        def run(eng, slot):
            over(eng, slot, 0, 15, 2, 8, T_LAST)

        RING = 5 * 8

        def ring_index(T, use):
            return 5 * T + use if use < 3 else 5 * (T + 2) + use

        def ring_used(r):
            return 0 <= r // 5 - 2 * (r % 5 >= 3) < NT

        def missing(r):
            return sum(not ring_used(x) for x in range(r))

        def m_count(T):
            if T < 0:
                return 0
            return T + 1 + 3 * (T // TPB) - (T % TPB == 0 and T > 0)

        def m_square_count(b):
            return m_count((b + 1) * TPB - 1) + (4 if b < B - 1 else 3)

        def ended(T):
            return T // TPB if 0 <= T < NT and T % TPB == TPB - 1 else None

        def place(j):
            return 2 * (j % 2) + j // 2

        def attn_tile(n):
            return n - 3 if 0 <= n - 3 < NT else None

        @block.sync
        def _(sp):
            for dst, src in loads:
                sp.dma_start(dst, src).then_inc(loaded, 16)

        @block.tensor
        def _(pe):
            pe.wait_ge(loaded, all_loaded)
            pe.wait_ge(ready, 1)

            def ring_free(r, turn):
                p = r - 2
                while p >= 0 and not ring_used(p):
                    p -= 2
                if p < 0:
                    return
                T, use = p // 5 - 2 * (p % 5 >= 3), p % 5
                if use < 2:
                    wait(pe, raw_made, 2 * T + use + 1, turn, 16)
                else:
                    wait(pe, (v_made, qT_made, kT_made)[use - 2], T + 1, turn, 8)

            def project(T, use, turn):
                b, t = T // TPB, T % TPB
                if t == 0 and use == 0:
                    wait(pe, h_made, 2 * (b + 1), turn, 4)
                r = ring_index(T, use)
                ring_free(r, turn)
                nc.tensor.matmul(ring_ps[:, r % 2, :], hT[:, b % 2, t * P:(t + 1) * P],
                                 wqkv[:, use * INNER:(use + 1) * INNER], start=True, stop=True
                                 ).then_inc(ring_filled, 1)

            def transpose(T, use, turn):
                r = ring_index(T, use)
                ring_free(r, turn)
                if use == 3:
                    wait(pe, added_rot, 2 * T + 1, turn, 16)
                else:
                    wait(pe, k_scaled, T + 1, turn, 8)
                for c in range(4):
                    mm = nc.tensor.transpose(ring_ps[:, r % 2, c * P:(c + 1) * P],
                                             turned[:, T % 2, use - 3, c * P:(c + 1) * P], ident[:])
                mm.then_inc(ring_filled, 1)

            def scores(T, half, turn):
                b, t = T // TPB, T % TPB
                if half == 0:
                    wait(pe, qT_made, T + 1, turn, 8)
                    wait(pe, kT_made, T + 1, turn, 8)
                wait(pe, exp_made, 2 * T + half, turn, 16)
                lo = WIN if t == 0 else 0
                for j in range(4):
                    h = 4 * half + j
                    e = 64 * (h % 2)
                    nc.tensor.matmul(s_ps[:, place(j), lo:KEYS], qT[e:e + 64, T % 2, h // 2, :],
                                     kT[e:e + 64, b % 2, h // 2, t * P - WIN + lo:(t + 1) * P],
                                     start=(j < 2), stop=False, skip_group_check=True)
                for j in range(4):
                    mm = nc.tensor.matmul(s_ps[:, place(j), lo:KEYS], identb[:], band[:, lo:KEYS],
                                          start=False, stop=True, skip_group_check=True)
                mm.then_inc(s_filled, 1)

            def prob_turn(T, half, turn):
                t = T % TPB
                wait(pe, exp_made, 2 * T + half + 1, turn, 16)
                wait(pe, pT_made, 2 * T + half, turn, 16)
                for j in range(4):
                    for blk in range(t == 0, 2):
                        mm = nc.tensor.transpose(pT_ps[:, 2 * j + blk, :],
                                                 prob[:, half, j, blk * P:(blk + 1) * P], ident[:])
                mm.then_inc(pT_filled, 1)

            def weigh(T, half, turn):
                b, t = T // TPB, T % TPB
                wait(pe, pT_made, 2 * T + half + 1, turn, 16)
                wait(pe, o_made, 2 * T + half, turn, 16)
                for j in range(4):
                    for blk in range(t == 0, 2):
                        mm = nc.tensor.matmul(o_ps[:, j, 0:LD + 1], probT[:, half, 2 * j + blk, :],
                                              v1[:, b % 2, t - 1 + blk, 4 * half + j, :],
                                              start=(blk == (t == 0)), stop=(blk == 1))
                mm.then_inc(o_filled, 1)

            def slot(n, turn):
                T = n if n < NT else None
                U, R, O = attn_tile(n), n - 2, n - 4
                if U is not None:
                    scores(U, 0, turn)
                if 0 <= O < NT:
                    prob_turn(O, 1, turn)
                if ended(n - 6) is not None:
                    b = ended(n - 6)
                    wait(pe, csq_made, b + 1, turn, 2)
                    if b < B - 1:
                        wait(pe, oT_made, (b + 1) * TPB + 1, turn, 8)
                    nc.tensor.matmul(m_ps[:], mean_of[:], csq[:], start=True, stop=True
                                     ).then_inc(m_filled, 1)
                if T is not None:
                    project(T, 0, turn)
                    project(T, 1, turn)
                if ended(n - 5) is not None:
                    b = ended(n - 5)
                    wait(pe, oT_made, (b + 1) * TPB, turn, 8)
                    for c in range(4):
                        mm = nc.tensor.matmul(m_ps[:], wo[:, c, :], oT[:, b % 2, c, :],
                                              start=(c == 0), stop=(c == 3))
                    mm.then_inc(m_filled, 1)
                if 0 <= O < NT:
                    weigh(O, 1, turn)
                if U is not None:
                    scores(U, 1, turn)
                    prob_turn(U, 0, turn)
                if T is not None:
                    project(T, 2, turn)
                if 0 <= R < NT:
                    transpose(R, 3, turn)
                if U is not None:
                    weigh(U, 0, turn)
                if 0 <= R < NT:
                    transpose(R, 4, turn)
                if ended(n - 5) is not None:
                    wait(pe, sh_made, 2 * (ended(n - 5) + 1), turn, 4)
                    nc.tensor.matmul(m_ps[:], mean_of[:], shifted[:], start=True, stop=True
                                     ).then_inc(m_filled, 1)
                if 0 <= O < NT:
                    t, b = O % TPB, O // TPB
                    wait(pe, o_made, 2 * (O + 1), turn, 16)
                    if t == 0:
                        wait(pe, c_made, b, turn, 2)
                    elif t == 1 and b > 0:
                        wait(pe, var_made, b, turn, 2)
                    else:
                        wait(pe, oT_made, O, turn, 8)
                    for c in range(4):
                        mm = nc.tensor.transpose(m_ps[:, c * P:(c + 1) * P],
                                                 o_tok[:, O % 2, c * P:(c + 1) * P], ident[:])
                    mm.then_inc(m_filled, 1)

            run(pe, slot)

        def shift(dve, dst, src, done):
            nc.vector.tensor_scalar(dst[0:64, :], src[0:64, :], 1.0, None, ALU.mult).then_inc(done, 1)
            nc.vector.tensor_scalar(dst[64:P, 1:S], src[64:P, 0:S - 1], 1.0, None, ALU.mult).then_inc(done, 1)

        @block.vector
        def _(dve):
            nc.vector.memset(three_halves[:], 1.5)
            nc.vector.memset(eight[:], 8.0)
            nc.vector.memset(half_ln[:], 0.5 * float(np.log(LN_SCALE)))
            nc.vector.memset(hT[64:P, :, 0:1], 0.0)
            nc.vector.memset(shifted[64:P, 0:1], 0.0)
            nc.vector.memset(prob[:, :, :, 0:WIN], 0.0)
            nc.vector.memset(v1[:, :, :, :, LD:LD + 1], 1.0).then_inc(ready, 1)
            dve.wait_ge(loaded, all_loaded)
            for t in range(TPB):
                nc.vector.tensor_tensor(rot[:, t], rot[:, t], gains[:], ALU.mult).then_inc(gained, 1)
            dve.wait_ge(gained, TPB)

            def halves(ap):
                return ap.rearrange("p (h w f) -> p h w f", w=2, f=LD // 2)

            def rotate(T, side, turn):
                t = T % TPB
                wait(dve, raw_made, 2 * T + side + 1, turn, 16)
                if side == 0:
                    wait(dve, added_rot, 2 * T - 1, turn, 16)
                else:
                    wait(dve, added_rot, 2 * T, turn, 16)
                src = raw[:, T % 2, side]
                for w in range(2):
                    ins = nc.vector.tensor_tensor(
                        halves(swapped[:, side])[:, :, w, :], halves(src)[:, :, 1 - w, :],
                        rot[:, t, side, 1, w * 32:(w + 1) * 32].unsqueeze(1).to_broadcast([P, LH, 32]), ALU.mult)
                ins.then_inc(rot_read, 1)

            def norms(T, turn):
                par = T % 2
                for side in range(2):
                    wait(dve, sq_made, 2 * T + side + 1, turn, 16)
                    nc.vector.tensor_reduce(sumsq[:, par, side * LH:(side + 1) * LH],
                                            squares[:, par, side].rearrange("p (h f) -> p h f", f=LD),
                                            AX.X, ALU.add).then_inc(sum_made, 1)
                wait(dve, sum_made, 2 * T + 2, turn, 16)
                nc.vector.tensor_scalar(sumsq[:, par], sumsq[:, par], 1e-24, -0.5, ALU.max,
                                        ALU.mult).then_inc(clip_made, 1)

            def maxima(T, half, turn):
                lo = WIN if T % TPB == 0 else 0
                wait(dve, s_filled, 2 * T + half + 1, turn, 16)
                wait(dve, exp_made, 2 * T + half - 1, turn, 16)
                nc.vector.tensor_reduce(s_max[:, half], s_ps[:, :, lo:KEYS], AX.X, ALU.max).then_inc(max_made, 1)
                wait(dve, max_made, 2 * T + half + 1, turn, 16)
                if half == 0:
                    wait(dve, q_gain_made, T + 1, turn, 8)
                by_place = q_gain[:, T % 4, 4 * half:4 * half + 4].rearrange("p (b a) -> p a b", a=2)
                nc.vector.scalar_tensor_tensor(out=s_bias[:, half].rearrange("p (a b) -> p a b", a=2),
                                               in0=s_max[:, half].rearrange("p (a b) -> p a b", a=2),
                                               scalar=-1.0, in1=by_place,
                                               op0=ALU.mult, op1=ALU.mult).then_inc(bias_made, 1)

            def take_probT(T, half, turn):
                wait(dve, pT_filled, 2 * T + half + 1, turn, 16)
                wait(dve, o_filled, 2 * T + half - 1, turn, 16)
                first = T % TPB == 0
                v = pT_ps[:].rearrange("p (j s) q -> p j s q", s=2)
                o = probT[:, half].rearrange("p (j s) q -> p j s q", s=2)
                nc.vector.tensor_copy(o[:, :, first:2, :], v[:, :, first:2, :]).then_inc(pT_made, 1)

            def take_out(T, half, turn):
                wait(dve, o_filled, 2 * T + half + 1, turn, 16)
                nc.vector.reciprocal(o_inv[:], o_ps[:, :, LD]).then_inc(o_inv_made, 1)
                wait(dve, o_inv_made, 2 * T + half + 1, turn, 16)
                if half == 0:
                    wait(dve, m_filled, m_count(T - 2), turn, 14)
                nc.vector.tensor_tensor(
                    o_tok[:, T % 2, half * 256:(half + 1) * 256].rearrange("p (j f) -> p j f", f=LD),
                    o_ps[:, :, 0:LD], o_inv[:].unsqueeze(2).to_broadcast([P, 4, LD]),
                    ALU.mult).then_inc(o_made, 1)

            def slot(n, turn):
                U, N, R, O = attn_tile(n), n - 1, n - 2, n - 4
                if n == 0:
                    shift(dve, hT[:, 0, :], batch_at(XT, 0, turn), h_made)
                if U is not None:
                    maxima(U, 0, turn)
                if 0 <= O < NT:
                    take_probT(O, 1, turn)
                if 0 <= N < NT:
                    rotate(N, 0, turn)
                if 0 <= O < NT:
                    take_out(O, 1, turn)
                if 0 <= N < NT:
                    rotate(N, 1, turn)
                if U is not None:
                    maxima(U, 1, turn)
                    take_probT(U, 0, turn)
                b = ended(n - 5)
                if b is not None:
                    x = batch_at(XT, b, turn)
                    wait(dve, m_filled, m_count(n - 5) + 1, turn, 14)
                    nc.vector.tensor_tensor(x, m_ps[:], x, ALU.add).then_inc(x_added, 1)
                if 0 <= N < NT:
                    norms(N, turn)
                if b is not None:
                    wait(dve, x_added, b + 1, turn, 2)
                    shift(dve, shifted, x, sh_made)
                if 0 <= R < NT:
                    r = ring_index(R, 3)
                    wait(dve, ring_filled, r + 1 - missing(r), turn, RING)
                    wait(dve, s_filled, 2 * R - 2, turn, 16)
                    nc.vector.tensor_copy(qT[:, R % 2].rearrange("p c q -> p (c q)"),
                                          ring_ps[:, r % 2, :]).then_inc(qT_made, 1)
                if U is not None:
                    take_out(U, 0, turn)
                if b is not None:
                    wait(dve, sh_made, 2 * (b + 1), turn, 4)
                    wait(dve, m_filled, m_count(n - 5) + 2, turn, 14)
                    nc.vector.tensor_tensor(batch_at(C, b, turn), shifted[:], m_ps[:],
                                            ALU.subtract).then_inc(c_made, 1)
                if n % TPB == TPB - 1 and n + 1 < NT:
                    b = (n + 1) // TPB
                    if b >= 2:
                        r = ring_index((b - 1) * TPB - 1, 2)
                        wait(dve, ring_filled, r + 1 - missing(r), turn, RING)
                    shift(dve, hT[:, b % 2, :], batch_at(XT, b, turn), h_made)

            run(dve, slot)

        @block.scalar
        def _(act):
            nc.scalar.preload_act_table_set("natural_log_exp_and_others")
            act.wait_ge(ready, 1)

            def exps(T, half, turn):
                lo = WIN if T % TPB == 0 else 0
                wait(act, bias_made, 2 * T + half + 1, turn, 16)
                wait(act, pT_filled, 2 * T + half - 1, turn, 16)
                for j in range(4):
                    ins = nc.scalar.activation(prob[:, half, j, WIN + lo:WIN + KEYS],
                                               s_ps[:, place(j), lo:KEYS], ACT.Exp,
                                               bias=s_bias[:, half, place(j):place(j) + 1],
                                               scale=q_gain[:, T % 4, 4 * half + j:4 * half + j + 1])
                ins.then_inc(exp_made, 1)

            def slot(n, turn):
                T = n if n < NT else None
                U = attn_tile(n)
                if U is not None:
                    exps(U, 0, turn)
                if T is not None:
                    for side in range(2):
                        r = ring_index(T, side)
                        wait(act, ring_filled, r + 1 - missing(r), turn, RING)
                        wait(act, sum_made, 2 * T + side - 3, turn, 16)
                        wait(act, rot_read, 2 * T + side - 3, turn, 16)
                        wait(act, added_rot, 2 * T + side - 3, turn, 16)
                        nc.scalar.activation(raw[:, T % 2, side], ring_ps[:, r % 2, :], ACT.Copy
                                             ).then_inc(raw_made, 1)
                        wait(act, raw_made, 2 * T + side + 1, turn, 16)
                        nc.scalar.activation(squares[:, T % 2, side], raw[:, T % 2, side], ACT.Square
                                             ).then_inc(sq_made, 1)
                if T is not None:
                    b, t = T // TPB, T % TPB
                    r = ring_index(T, 2)
                    wait(act, ring_filled, r + 1 - missing(r), turn, RING)
                    wait(act, o_filled, 8 * (b - 1), turn, 16)
                    nc.scalar.activation(v1[:, b % 2, t, :, 0:LD],
                                         ring_ps[:, r % 2, :].rearrange("p (h f) -> p h f", f=LD),
                                         ACT.Copy).then_inc(v_made, 1)
                if ended(n - 6) is not None:
                    b = ended(n - 6)
                    wait(act, m_filled, m_square_count(b), turn, 14)
                    nc.scalar.activation(batch_at(VAR, b, turn), m_ps[:], ACT.Copy).then_inc(var_made, 1)
                if U is not None:
                    exps(U, 1, turn)
                if 0 <= n - 1 < NT:
                    T = n - 1
                    wait(act, clip_made, T + 1, turn, 8)
                    wait(act, q_gain_made, T - 1, turn, 8)
                    wait(act, k_scaled, T - 1, turn, 8)
                    nc.scalar.activation(lnsq[:, T % 2], sumsq[:, T % 2], ACT.Ln, scale=-2.0 * LN_SCALE
                                         ).then_inc(ln_made, 1)
                    wait(act, ln_made, T + 1, turn, 8)
                    nc.scalar.activation(inv[:, T % 2], lnsq[:, T % 2], ACT.Exp, bias=half_ln[:],
                                         scale=-0.5).then_inc(seed_made, 1)
                if 0 <= n - 2 < NT:
                    T = n - 2
                    b, t = T // TPB, T % TPB
                    r = ring_index(T, 4)
                    wait(act, ring_filled, r + 1 - missing(r), turn, RING)
                    wait(act, s_filled, 8 * (b - 1), turn, 16)
                    nc.scalar.activation(kT[:, b % 2, :, t * P:(t + 1) * P],
                                         ring_ps[:, r % 2, :].rearrange("p (c q) -> p c q", q=P),
                                         ACT.Copy).then_inc(kT_made, 1)
                T = n - 4
                if 0 <= T < NT:
                    b, t = T // TPB, T % TPB
                    wait(act, m_filled, m_count(T), turn, 14)
                    nc.scalar.activation(oT[:, b % 2, :, t * P:(t + 1) * P],
                                         m_ps[:].rearrange("p (c q) -> p c q", q=P),
                                         ACT.Copy).then_inc(oT_made, 1)
                if ended(n - 5) is not None:
                    b = ended(n - 5)
                    wait(act, c_made, b + 1, turn, 2)
                    nc.scalar.activation(csq[:], batch_at(C, b, turn), ACT.Square).then_inc(csq_made, 1)

            run(act, slot)

        @block.gpsimd
        def _(pool):
            pool.wait_ge(ready, 1)
            pool.wait_ge(gained, TPB)

            def polish(T, turn):
                par = T % 2
                wait(pool, seed_made, T + 1, turn, 8)
                wait(pool, bias_made, 2 * T - 6, turn, 16)
                wait(pool, exp_made, 2 * T - 6, turn, 16)
                nc.gpsimd.tensor_tensor(newton[:], inv[:, par], inv[:, par], ALU.mult).then_inc(nt1, 1)
                wait(pool, nt1, T + 1, turn, 8)
                nc.gpsimd.tensor_tensor(newton[:], newton[:], sumsq[:, par], ALU.mult).then_inc(nt2, 1)
                wait(pool, nt2, T + 1, turn, 8)
                nc.gpsimd.tensor_tensor(newton[:], newton[:], three_halves[:], ALU.add).then_inc(nt3, 1)
                wait(pool, nt3, T + 1, turn, 8)
                nc.gpsimd.tensor_tensor(inv[:, par], inv[:, par], newton[:], ALU.mult).then_inc(inv_made, 1)
                wait(pool, inv_made, T + 1, turn, 8)
                nc.gpsimd.tensor_tensor(q_gain[:, T % 4], inv[:, par, 0:LH], eight[:],
                                        ALU.mult).then_inc(q_gain_made, 1)

            def slot(n, turn):
                T = n - 1
                if 0 <= T < NT:
                    for side in range(2):
                        wait(pool, raw_made, 2 * T + side + 1, turn, 16)
                        nc.gpsimd.tensor_tensor(
                            plain[:, side].rearrange("p (h f) -> p h f", f=LD),
                            raw[:, T % 2, side].rearrange("p (h f) -> p h f", f=LD),
                            rot[:, T % TPB, side, 0, :].unsqueeze(1).to_broadcast([P, LH, LD]),
                            ALU.mult).then_inc(plain_made, 1)
                    for side in range(2):
                        wait(pool, plain_made, 2 * T + side + 1, turn, 16)
                        wait(pool, rot_read, 2 * T + side + 1, turn, 16)
                        r = ring_index(T - 2, 3 + side)
                        if T >= 2:
                            wait(pool, ring_filled, r + 1 - missing(r), turn, RING)
                        nc.gpsimd.tensor_tensor(turned[:, T % 2, side], plain[:, side], swapped[:, side],
                                                ALU.add).then_inc(added_rot, 1)
                    polish(T, turn)
                    wait(pool, added_rot, 2 * T + 2, turn, 16)
                    k = turned[:, T % 2, 1].rearrange("p (h f) -> p h f", f=LD)
                    nc.gpsimd.tensor_tensor(k, k, inv[:, T % 2, LH:2 * LH].unsqueeze(2).to_broadcast([P, LH, LD]),
                                            ALU.mult).then_inc(k_scaled, 1)

            over(pool, slot, 0, 15, 2, 8, NT + 1)


HID = D * 4 * 2 // 3
HC = [(c, min(P, HID - c)) for c in range(0, HID, P)]


def gated_ffn(nc, a, layer, XT, C, VAR):
    tag = f"ff{layer}_"
    NC = len(HC)
    with ExitStack() as ctx:
        def sb(name, shape, dt=F32):
            return ctx.enter_context(nc.sbuf_tensor(tag + name, shape, dt))

        def ps(name, shape, dt=F32):
            return ctx.enter_context(nc.psum_tensor(tag + name, shape, dt))

        def sem(name):
            return a["layer_semaphores"](tag + name)

        w1 = sb("w1", [P, 2 * HID])
        w2 = sb("w2", [P, NC, D])
        b1 = sb("b1", [P, 2, NC])
        ln = sb("ln", [P, 2])
        b2 = sb("b2", [P, 1])
        eps = sb("eps", [P, 1])
        hn = sb("hn", [P, 2, S])
        gate = sb("gate", [P, 2, NC, S])
        prod = sb("prod", [P, 2, NC, S])
        a_ps = ps("a", [P, NC, S])
        g_ps = ps("g", [P, NC, S])
        o_ps = ps("o", [P, S])
        loaded, eps_set = sem("loaded"), sem("eps_set")
        dev_made, inv_made, div_made, hn_made = sem("dev"), sem("inv"), sem("div"), sem("hn")
        a_filled, g_filled = sem("a_filled"), sem("g_filled")
        gate_made, prod_made = sem("gate_made"), sem("prod_made")
        o_filled, x_added = sem("o_filled"), sem("x_added")
        loads = [(w1[:], a["fw1"][layer]), (b1[:].rearrange("p s c -> p (s c)"), a["fb1"][layer]),
                 (ln[:], a["fln"][layer]), (b2[:], a["fb2"][layer])]
        loads += [(w2[0:m, i, :], a["fw2"][layer][c:c + m, :]) for i, (c, m) in enumerate(HC)]
        all_loaded = 16 * len(loads)
        block = ctx.enter_context(nc.Block())

        def batch_at(buf, b, turn):
            return flat(buf[:, bass.ds(b if isinstance(turn, int) else turn * 2 + b, 1), :])

        def run(eng, slot):
            over(eng, slot, 0, 3, 2, 2, B + 1)

        @block.sync
        def _(sp):
            for dst, src in loads:
                sp.dma_start(dst, src).then_inc(loaded, 16)

        @block.vector
        def _(dve):
            nc.vector.memset(eps[:], 1e-5).then_inc(eps_set, 1)
            with dve.Fori(0, B) as b:
                dve.wait_ge(dev_made, b + 1)
                v = flat(VAR[:, bass.ds(b, 1), :])
                nc.vector.reciprocal(v, v).then_inc(inv_made, 1)
            dve.wait_ge(inv_made, B)
            dve.wait_ge(loaded, all_loaded)

            def slot(n, turn):
                b = n
                if b < B:
                    wait(dve, hn_made, b - 1, turn, 2)
                    c = batch_at(C, b, turn)
                    nc.vector.tensor_tensor(c, c, batch_at(VAR, b, turn), ALU.mult).then_inc(div_made, 1)
                    wait(dve, div_made, b + 1, turn, 2)
                    wait(dve, g_filled, NC * (b - 1), turn, 2 * NC)
                    nc.vector.tensor_scalar(hn[:, b % 2, :], c, ln[:, 0:1], ln[:, 1:2],
                                            ALU.mult, ALU.add).then_inc(hn_made, 1)
                    for i, (_, m) in enumerate(HC):
                        wait(dve, a_filled, NC * b + i + 1, turn, 2 * NC)
                        wait(dve, gate_made, NC * b + i + 1, turn, 2 * NC)
                        wait(dve, o_filled, b - 1, turn, 2)
                        nc.vector.scalar_tensor_tensor(out=prod[0:m, b % 2, i, :], in0=a_ps[0:m, i, :],
                                                       scalar=b1[0:m, 0, i:i + 1], in1=gate[0:m, b % 2, i, :],
                                                       op0=ALU.add, op1=ALU.mult).then_inc(prod_made, 1)
                b = n - 1
                if 0 <= b < B:
                    wait(dve, o_filled, b + 1, turn, 2)
                    x = batch_at(XT, b, turn)
                    nc.vector.scalar_tensor_tensor(out=x, in0=o_ps[:], scalar=b2[:, 0:1], in1=x,
                                                   op0=ALU.add, op1=ALU.add).then_inc(x_added, 1)

            run(dve, slot)

        @block.scalar
        def _(act):
            act.wait_ge(eps_set, 1)
            with act.Fori(0, B) as b:
                v = flat(VAR[:, bass.ds(b, 1), :])
                nc.scalar.activation(v, v, ACT.Sqrt, bias=eps[:]).then_inc(dev_made, 1)
            act.wait_ge(loaded, all_loaded)

            def slot(n, turn):
                b = n
                if b < B:
                    for i, (_, m) in enumerate(HC):
                        wait(act, g_filled, NC * b + i + 1, turn, 2 * NC)
                        wait(act, prod_made, NC * (b - 1), turn, 2 * NC)
                        nc.scalar.activation(gate[0:m, b % 2, i, :], g_ps[0:m, i, :], ACT.Gelu,
                                             bias=b1[0:m, 1, i:i + 1]).then_inc(gate_made, 1)

            run(act, slot)

        @block.tensor
        def _(pe):
            pe.wait_ge(loaded, all_loaded)

            def slot(n, turn):
                b = n
                if b < B:
                    wait(pe, hn_made, b + 1, turn, 2)
                    for i, (c, m) in enumerate(HC):
                        wait(pe, prod_made, NC * (b - 1) + i + 1, turn, 2 * NC)
                        nc.tensor.matmul(g_ps[0:m, i, :], w1[:, HID + c:HID + c + m], hn[:, b % 2, :],
                                         start=True, stop=True).then_inc(g_filled, 1)
                        nc.tensor.matmul(a_ps[0:m, i, :], w1[:, c:c + m], hn[:, b % 2, :],
                                         start=True, stop=True).then_inc(a_filled, 1)
                b = n - 1
                if 0 <= b < B:
                    wait(pe, prod_made, NC * (b + 1), turn, 2 * NC)
                    wait(pe, x_added, b, turn, 2)
                    for i, (_, m) in enumerate(HC):
                        mm = nc.tensor.matmul(o_ps[:], w2[0:m, i, :], prod[0:m, b % 2, i, :],
                                              start=(i == 0), stop=(i == NC - 1))
                    mm.then_inc(o_filled, 1)

            run(pe, slot)


def add_and_store(nc, a, X, XT):
    out_tiles = a["out"].rearrange("b (t p) d -> p b t d", p=P)
    with ExitStack() as ctx:
        def sem(name):
            return a["semaphores"].enter_context(nc.semaphore("end_" + name))

        ident = ctx.enter_context(nc.sbuf_tensor("end_ident", [P, P], F32))
        t_ps = ctx.enter_context(nc.psum_tensor("end_ps", [P, 2, S], F32))
        xt = ctx.enter_context(nc.sbuf_tensor("end_xt", [P, 2, S], F32))
        loaded, copied, turned, added, stored = (sem(x) for x in ("loaded", "copied", "turned", "added", "stored"))
        block = ctx.enter_context(nc.Block())

        def run(eng, slot):
            over(eng, slot, 0, 2, 3, 2, B)

        @block.sync
        def _(sp):
            sp.dma_start(ident[:], a["ident"]).then_inc(loaded, 16)
            for b in range(B):
                sp.wait_ge(added, b + 1)
                sp.dma_start(out_tiles[:, b], X[:, b * TPB:(b + 1) * TPB, :]).then_inc(stored, 16)
            sp.wait_ge(stored, 16 * B)

        @block.scalar
        def _(act):
            def slot(n, turn):
                wait(act, turned, n - 1, turn, 2)
                b = n if isinstance(turn, int) else turn * 2 + n
                nc.scalar.activation(xt[:, n % 2, :], flat(XT[:, bass.ds(b, 1), :]), ACT.Copy).then_inc(copied, 1)

            run(act, slot)

        @block.tensor
        def _(pe):
            pe.wait_ge(loaded, 16)

            def slot(n, turn):
                wait(pe, copied, n + 1, turn, 2)
                wait(pe, added, n - 1, turn, 2)
                for t in range(TPB):
                    mm = nc.tensor.transpose(t_ps[:, n % 2, t * P:(t + 1) * P],
                                             xt[:, n % 2, t * P:(t + 1) * P], ident[:])
                mm.then_inc(turned, 1)

            run(pe, slot)

        @block.vector
        def _(dve):
            def slot(n, turn):
                wait(dve, turned, n + 1, turn, 2)
                first = n * TPB if isinstance(turn, int) else turn * (2 * TPB) + n * TPB
                x = X[:, bass.ds(first, TPB), :]
                nc.vector.tensor_tensor(x, t_ps[:, n % 2, :].rearrange("p (t d) -> p t d", d=D), x,
                                        ALU.add).then_inc(added, 1)

            run(dve, slot)


def rotary_tables():
    half = np.arange(0, LD, 2, dtype=np.float32)
    inv_freq = (1.0 / 10000.0 ** (half / LD)).astype(np.float32)
    t = np.arange(S, dtype=np.float32)
    freqs = (t[:, None] * inv_freq[None, :]).astype(np.float32)
    base = ((half + 0.4 * LD) / (1.4 * LD)).astype(np.float32)
    power = ((t - S // 2) / float(WIN // 2)).astype(np.float32)
    scale = (base[None, :] ** power[:, None]).astype(np.float32)
    cos, sin = np.cos(freqs), np.sin(freqs)
    sides = []
    for c, s in ((cos * scale, sin * scale), (cos / scale, sin / scale)):
        sides.append(np.stack([np.concatenate([c, c], 1), np.concatenate([-s, s], 1)], 1))
    return np.ascontiguousarray(np.stack(sides, 1).astype(np.float32))


def band_mask():
    i, j = np.arange(P)[:, None], np.arange(KEYS)[None, :]
    return np.where((j <= i + WIN) & (j >= i), 0.0, NEG).astype(np.float32)




def kernel(**inputs):
    import numpy as _np
    import concourse.bacc as _bacc
    from concourse.bass_utils import run_bass_kernel_spmd as _run

    nc = _bacc.Bacc("TRN2", target_bir_lowering=False, num_devices=1)
    arrays = layouts(inputs)
    aps = {name: nc.dram_tensor(f"in_{name}", v.shape, mybir.dt.from_np(v.dtype), kind="ExternalInput").ap()
           for name, v in arrays.items()}
    aps["out"] = nc.dram_tensor("out", (B, S, D), F32, kind="ExternalOutput").ap()
    build(nc, aps)
    r = _run(nc, [{f"in_{k}": v for k, v in arrays.items()}], core_ids=[0])
    return r.results[0]["out"]
```

```python
from contextlib import ExitStack

import numpy as np

import concourse.bass as bass
from concourse import mybir

ALU = mybir.AluOpType
ACT = mybir.ActivationFunctionType
AX = mybir.AxisListType
F32 = mybir.dt.float32
F16 = mybir.dt.float16
BF16 = mybir.dt.bfloat16

P = 128
B, S, D = 8, 512, 128
DEPTH = 2
TPB = S // P
NT = B * TPB

H, DH, NB = 16, 8, 32
MLP = 512
SHIFT = 64.0

UNITS = 8
SLOTS = 4 * UNITS
PAIR = 2 * SLOTS
LEAD_SCORES = 1
LEAD_MAX = 13
LEAD_PREP = 42
FIRST_SLOT = -LEAD_PREP
LAST_SLOT = B * SLOTS + 7
LOOP_FROM = 22
LOOP_TURNS = 3
LOOP_TO = LOOP_FROM + LOOP_TURNS * PAIR
TILE_SLOTS = 5


def streams(n):
    s = {}
    x = n + LEAD_SCORES
    s["scores"] = x if 0 <= x < B * SLOTS else None
    x = n + LEAD_MAX
    s["max"] = x if 0 <= x < B * SLOTS else None
    s["exp"] = n if 0 <= n < B * SLOTS else None
    s["pv"] = n // 2 - 1 if n % 2 == 0 and 2 <= n <= B * SLOTS else None
    s["out"] = n // UNITS - 1 if n % UNITS == 0 and UNITS <= n <= B * SLOTS else None
    prep, k = (n + LEAD_PREP) // SLOTS, (n + LEAD_PREP) % SLOTS
    s["prep"] = [] if not 0 <= prep < B else [
        (prep * TPB + t, k - TILE_SLOTS * t) for t in range(TPB) if 0 <= k - TILE_SLOTS * t <= 13]
    return s


def bench_uses(n):
    s = streams(n)
    uses = []
    for step, at in (("stack_q0", 10), ("stack_q1", 11), ("stack_k0", 12), ("stack_k1", 13),
                     ("xn", 1), ("qkv", 2), ("clq", 3), ("clk", 4)):
        uses += [(step, tile) for tile, k in s["prep"] if k == at]
    x = n - UNITS - 1
    if x % UNITS == 0 and 0 <= x // UNITS < B * 4:
        uses.append(("heads_out", x // UNITS))
    x = n - SLOTS - 3
    if x % SLOTS == 0 and 0 <= x // SLOTS < B:
        uses.append(("att_t", x // SLOTS))
    x = n - SLOTS - 5
    if x % SLOTS == 0 and 0 <= x // SLOTS < B:
        uses.append(("proj", x // SLOTS))
    x = n + 5
    if x % UNITS == 0 and 0 <= x // UNITS < B * 4:
        uses.append(("shift", x // UNITS))
    return uses


STACKS = ("stack_q0", "stack_q1", "stack_k0", "stack_k1")
VECTOR_EMPTIES = ("clq", "clk", "heads_out", "proj", "shift")
BENCH_ORDER = {}
for _n in range(FIRST_SLOT, LAST_SLOT):
    for _u in bench_uses(_n):
        BENCH_ORDER[(_n, _u)] = len(BENCH_ORDER)
BENCH_LIST = list(BENCH_ORDER)
BENCH_BANKS = 3
BENCH_PER_PAIR = sum(len(bench_uses(n)) for n in range(LOOP_FROM, LOOP_FROM + PAIR))


def over_slots(eng, slot):
    for n in range(FIRST_SLOT, LOOP_FROM):
        slot(n, 0)
    with eng.Fori(0, LOOP_TURNS) as turn:
        for n in range(LOOP_FROM, LOOP_FROM + PAIR):
            slot(n, turn)
    for n in range(LOOP_TO, LAST_SLOT):
        slot(n, 0)


def before(n, use):
    order = BENCH_ORDER[(n, use)] - BENCH_BANKS
    return BENCH_LIST[order][1] if order >= 0 else None


def bank_of(n, use):
    return BENCH_ORDER[(n, use)] % BENCH_BANKS


def due(count, turn, per_pair):
    return count if isinstance(turn, int) else turn * per_pair + count


def tile_at(turn, tile):
    return tile if isinstance(turn, int) else turn * (2 * TPB) + tile


def build(nc, a, debug=None):
    with ExitStack() as ctx:
        a["semaphores"] = ctx

        def sb(name, shape, dt=F32, c=ctx):
            return c.enter_context(nc.sbuf_tensor(name, shape, dt))

        X = sb("X", [P, NT, D])
        Z = sb("Z", [P, NT, D])
        R1 = sb("R1", [P, NT])
        stats = sb("stats", [P, NT, 6])
        mlp_w = mlp_weights(nc, a, ctx)
        clustered_attention(nc, a, X, Z, R1, stats, mlp_w["loads"])
        if debug == "A":
            store_tokens(nc, a, Z)
            return
        mean = sb("mean", [P, NT])
        inv_dev = sb("inv_dev", [P, NT])
        XT = sb("XT", [P, B, S])
        VAR = sb("VAR", [P, B, S])
        layer_w = layer_weights(nc, a, ctx)
        layer_w["ident"] = mlp_w["ident"]
        token_moments(nc, a, stats, mean, inv_dev, 1e-6, "m2_")
        attention_mlp(nc, a, X, Z, mean, inv_dev, stats, mlp_w,
                      layer_w["table_loads"] + layer_w["attention_loads"](0))
        if debug == "M":
            store_tokens(nc, a, X)
            return
        token_moments(nc, a, stats, mean, inv_dev, 1e-5, "m3_")
        turn_tokens(nc, a, X, mean, inv_dev, XT)
        for layer in range(DEPTH):
            taken = []

            def take(name):
                taken.append(nc.alloc_semaphore(name=name))
                return taken[-1]

            a["layer_semaphores"] = take
            local_attention(nc, a, layer, XT, Z[:].rearrange("p (b t) d -> p b (t d)", b=B), VAR, layer_w)
            gated_ffn(nc, a, layer, XT, Z[:].rearrange("p (b t) d -> p b (t d)", b=B), VAR, layer_w)
            clear(nc, taken)
            if debug == "L%d" % layer:
                break
        add_and_store(nc, a, X, XT)


def _np_of(dtype):
    return mybir.dt.np(dtype)


def layouts(inputs):
    i = {k: np.ascontiguousarray(v) for k, v in inputs.items()}
    eye = np.zeros((P, P), np.float32)
    eye[np.arange(P), np.arange(P)] = 1

    def hash_blocks(w):
        out = np.zeros((H, DH, H, NB), np.float32)
        for h in range(H):
            out[h, :, h, :] = w[h]
        return out.reshape(P, H * NB)

    a = {
        "x": i["L0_attn_inputs"], "ident": eye, "ident16": eye.astype(np.float16),
        "wq": i["L0_attn_Wq"].reshape(P, P), "wk": i["L0_attn_Wk"].reshape(P, P),
        "wv": i["L0_attn_Wv"].reshape(P, P),
        "wqT": np.ascontiguousarray(i["L0_attn_Wq"].reshape(P, P).T),
        "wkT": np.ascontiguousarray(i["L0_attn_Wk"].reshape(P, P).T),
        "whq": hash_blocks(i["L0_attn_Whq"]), "whk": hash_blocks(i["L0_attn_Whk"]),
        "wo": i["L0_attn_Wo"].reshape(P, P),
        "ln1_g": i["L0_attn_ln1_g"].reshape(P, 1), "ln1_b": i["L0_attn_ln1_b"].reshape(P, 1),
    }
    swap = np.r_[LD // 2:LD, 0:LD // 2]
    gains = np.stack([np.stack([g, g[:, swap]], 1) for g in (i["L0_ffn_q_scale"], i["L0_ffn_k_scale"])], 1)

    def chunks(v):
        out = np.zeros((DEPTH, P, 2, len(HC)), np.float32)
        for side in range(2):
            for n, (c, m) in enumerate(HC):
                out[:, :m, side, n] = v[:, side * HID + c:side * HID + c + m]
        return out.reshape(DEPTH, P, -1)

    a |= {
        "mlp_w1": i["L0_attn_W1"], "mlp_w2": i["L0_attn_W2"],
        "mlp_b1": np.ascontiguousarray(i["L0_attn_b1"].reshape(MLP // P, P).T),
        "ln2_g": i["L0_attn_ln2_g"].reshape(P, 1), "ln2_b": i["L0_attn_ln2_b"].reshape(P, 1),
        "mlp_b2_rows": np.ascontiguousarray(np.broadcast_to(i["L0_attn_b2"], (P, D))),
        "identb": eye.astype(_np_of(BF16)), "band": band_mask().astype(_np_of(BF16)),
        "mean_of": np.full((P, P), 1.0 / D, np.float32),
        "wqkv": i["L0_ffn_wqkv"], "lwo": i["L0_ffn_wo"], "rot": rotary_tables(),
        "gains": np.ascontiguousarray(np.broadcast_to(gains.reshape(DEPTH, 1, -1), (DEPTH, P, 4 * LD))),
        "fw1": i["L0_ffn_w1"], "fb1": chunks(i["L0_ffn_b1"]),
        "fln": np.ascontiguousarray(np.stack([i["L0_ffn_ln_g"], i["L0_ffn_ln_b"]], 2)),
        "fb2": i["L0_ffn_b2"].reshape(DEPTH, P, 1), "fw2": i["L0_ffn_w2"],
    }
    return a


def mlp_weights(nc, a, ctx):
    def sb(name, shape):
        return ctx.enter_context(nc.sbuf_tensor("mlp_" + name, shape, F32))

    w = {"ident": sb("ident", [P, P]), "w1": sb("w1", [P, MLP]), "w2": sb("w2", [P, MLP // P, D]),
         "b1": sb("b1", [P, MLP // P]), "ln2": sb("ln2", [P, 2]), "b2_rows": sb("b2_rows", [P, D])}
    w["loads"] = [(w["ident"][:], a["ident"]), (w["w1"][:], a["mlp_w1"]),
                  (w["w2"][:], a["mlp_w2"].rearrange("(c p) d -> p c d", p=P)), (w["b1"][:], a["mlp_b1"]),
                  (w["ln2"][:, 0:1], a["ln2_g"]), (w["ln2"][:, 1:2], a["ln2_b"]),
                  (w["b2_rows"][:], a["mlp_b2_rows"])]
    return w


def layer_weights(nc, a, ctx):
    def sb(name, shape, dt=F32):
        return ctx.enter_context(nc.sbuf_tensor("lw_" + name, shape, dt))

    NC = len(HC)
    w = {"identb": sb("identb", [P, P], BF16), "band": sb("band", [P, KEYS], BF16),
         "mean_of": sb("mean_of", [P, P]),
         "rot": sb("rot", [P, TPB, 2, 2, LD]),
         "gains": sb("gains", [P, 2, 2, LD]),
         "wqkv": sb("wqkv", [P, 3 * INNER]), "wo": sb("wo", [P, INNER // P, D]),
         "w1": sb("w1", [P, 2 * HID]), "w2": sb("w2", [P, NC, D]),
         "b1": sb("b1", [P, 2, NC]), "ln": sb("ln", [P, 2]), "b2": sb("b2", [P, 1])}
    w["table_loads"] = [(w["identb"][:], a["identb"]), (w["band"][:], a["band"]), (w["mean_of"][:], a["mean_of"]),
                        (w["rot"][:].rearrange("p t s w f -> p t (s w f)"),
                         a["rot"].rearrange("(t p) s w f -> p t (s w f)", p=P))]

    def attention_loads(layer):
        return [(w["wqkv"][:], a["wqkv"][layer]), (w["wo"][:], a["lwo"][layer].rearrange("(c p) d -> p c d", p=P)),
                (w["gains"][:].rearrange("p s w f -> p (s w f)"), a["gains"][layer])]

    def ffn_loads(layer):
        return [(w["w1"][:], a["fw1"][layer]), (w["b1"][:].rearrange("p s c -> p (s c)"), a["fb1"][layer]),
                (w["ln"][:], a["fln"][layer]), (w["b2"][:], a["fb2"][layer])
                ] + [(w["w2"][0:m, i, :], a["fw2"][layer][c:c + m, :]) for i, (c, m) in enumerate(HC)]

    w["attention_loads"], w["ffn_loads"] = attention_loads, ffn_loads
    return w


def store_tokens(nc, a, src):
    with nc.semaphore("stored") as stored, nc.Block() as block:
        @block.sync
        def _(sp):
            sp.dma_start(a["out"].rearrange("b (t p) d -> p (b t) d", p=P), src[:]).then_inc(stored, 16)
            sp.wait_ge(stored, 16)


def normalise_input(nc, a, X, Z, R1, weights, weights_loaded):
    x_tiles = a["x"].rearrange("b (t p) d -> p b t d", p=P)
    with ExitStack() as ctx:
        def sb(name, shape, dt=F32):
            return ctx.enter_context(nc.sbuf_tensor(name, shape, dt))

        def sem(name):
            return a["semaphores"].enter_context(nc.semaphore(name))

        stats = sb("in_stats", [P, NT, 6])
        moments = sb("in_moments", [P, NT, 2])
        dev = sb("in_dev", [P, NT])
        r0 = sb("in_r0", [P, NT])
        var1 = sb("in_var1", [P, NT])
        dev1 = sb("in_dev1", [P, NT])
        eps = sb("in_eps", [P, 2])
        loaded = [sem(f"in_loaded{b}") for b in range(B)]
        stats_done = sem("in_stats_done")
        moments_done = sem("in_moments_done")
        eps_set = sem("in_eps_set")
        dev_done = sem("in_dev_done")
        r0_done = sem("in_r0_done")
        r0_sq_done = sem("in_r0_sq_done")
        var1_done = sem("in_var1_done")
        block = ctx.enter_context(nc.Block())

        @block.sync
        def _(sp):
            for b in range(B):
                sp.dma_start(X[:, b * TPB:(b + 1) * TPB, :], x_tiles[:, b]).then_inc(loaded[b], 16)
            for dst, src in weights:
                sp.dma_start(dst, src).then_inc(weights_loaded, 16)

        @block.vector
        def _(dve):
            nc.vector.memset(eps[:, 0:1], 1e-5)
            nc.vector.memset(eps[:, 1:2], 1e-6).then_inc(eps_set, 1)
            for b in range(B):
                dve.wait_ge(loaded[b], 16)
                for t in range(b * TPB, (b + 1) * TPB):
                    nc.vector.bn_stats(stats[:, t, :], X[:, t, :]).then_inc(stats_done, 1)
                    if t:
                        dve.wait_ge(stats_done, t)
                        nc.vector.bn_aggr(moments[:, t - 1, :], stats[:, t - 1, :])
            dve.wait_ge(stats_done, NT)
            nc.vector.bn_aggr(moments[:, NT - 1, :], stats[:, NT - 1, :]).then_inc(moments_done, 1)
            dve.wait_ge(moments_done, 1)
            dve.wait_ge(dev_done, 1)
            nc.vector.reciprocal(r0[:], dev[:]).then_inc(r0_done, 1)
            dve.wait_ge(r0_done, 1)
            nc.vector.tensor_tensor(var1[:], r0[:], r0[:], ALU.mult).then_inc(r0_sq_done, 1)
            dve.wait_ge(r0_sq_done, 1)
            nc.vector.tensor_tensor(var1[:], var1[:], moments[:, :, 1], ALU.mult).then_inc(var1_done, 1)
            for t in range(NT):
                nc.vector.tensor_scalar(Z[:, t, :], X[:, t, :], moments[:, t, 0:1], r0[:, t:t + 1],
                                        ALU.subtract, ALU.mult)
            dve.wait_ge(dev_done, 2)
            nc.vector.reciprocal(R1[:], dev1[:])

        @block.scalar
        def _(act):
            act.wait_ge(eps_set, 1)
            act.wait_ge(moments_done, 1)
            nc.scalar.activation(dev[:], moments[:, :, 1], ACT.Sqrt, bias=eps[:, 0:1]).then_inc(dev_done, 1)
            act.wait_ge(var1_done, 1)
            nc.scalar.activation(dev1[:], var1[:], ACT.Sqrt, bias=eps[:, 1:2]).then_inc(dev_done, 1)


def clustered_attention(nc, a, X, Z, R1, stats, mlp_loads):
    with ExitStack() as ctx:
        def sb(name, shape, dt=F32):
            return ctx.enter_context(nc.sbuf_tensor(name, shape, dt))

        def ps(name, shape, dt=F32):
            return ctx.enter_context(nc.psum_tensor(name, shape, dt))

        def sem(name):
            return a["semaphores"].enter_context(nc.semaphore(name))

        ident = sb("ident", [P, P])
        ident16 = sb("ident16", [P, P], F16)
        w_qkv = sb("w_qkv", [P, 3, D])
        w_qT = sb("w_qT", [P, 2, D])
        w_hash = sb("w_hash", [P, 2, H * NB])
        w_cl = sb("w_cl", [P, 2, H * NB])
        w_o = sb("w_o", [P, D])
        ln1 = sb("ln1", [P, 2])
        xn = sb("xn", [P, 2, D])
        xnT = sb("xnT", [P, 2, P])
        qkv = sb("qkv", [P, 2, 3, D])
        cl = sb("cl", [P, 2, 2, H * NB])
        cl_max = sb("cl_max", [P, 2, 2, H])
        cl_sum = sb("cl_sum", [P, 2, 2, H])
        cl_inv = sb("cl_inv", [P, 2, 2, H])
        stack_tok = sb("stack_tok", [P, 2, H, P], F16)
        stack = sb("stack", [P, 2, 2, H, S], F16)
        v_pad = sb("v_pad", [P, 2, TPB, H, 32])
        row_max = sb("row_max", [P, 2, TPB, 4])
        shift_tok = sb("shift_tok", [P, TPB, 2, 4], F16)
        shift_row = sb("shift_row", [8, S], F16)
        prob = sb("prob", [P, 4, 4, S])
        heads_raw = sb("heads_raw", [P, S])
        inv_sum = sb("inv_sum", [P, TPB, 4])
        att_tok = sb("att_tok", [P, TPB, H, DH])
        att_T = sb("att_T", [P, S])

        scores_ps = ps("scores_ps", [P, 2, S])
        max_ps = ps("max_ps", [P, 2, S])
        heads_ps = ps("heads_ps", [P, S])
        bench_ps = ps("bench", [P, BENCH_BANKS, S])

        w_loaded = sem("w_loaded")
        folded = sem("folded")
        with ExitStack() as setup:
            loads = [(ident[:], a["ident"]), (ident16[:], a["ident16"]),
                     (w_qkv[:, 0, :], a["wq"]), (w_qkv[:, 1, :], a["wk"]), (w_qkv[:, 2, :], a["wv"]),
                     (w_qT[:, 0, :], a["wqT"]), (w_qT[:, 1, :], a["wkT"]),
                     (w_hash[:, 0, :], a["whq"]), (w_hash[:, 1, :], a["whk"]),
                     (w_o[:], a["wo"]), (ln1[:, 0:1], a["ln1_g"]), (ln1[:, 1:2], a["ln1_b"])] + mlp_loads
            normalise_input(nc, a, X, Z, R1, loads, w_loaded)
            block = setup.enter_context(nc.Block())

            @block.tensor
            def _(pe):
                pe.wait_ge(w_loaded, 16 * len(loads))
                for i in range(2):
                    nc.tensor.matmul(max_ps[:, i, :], w_qT[:, i, :], w_hash[:, i, :],
                                     start=True, stop=True).then_inc(folded, 1)

            @block.vector
            def _(dve):
                nc.vector.memset(stack_tok[:], 0.0).then_inc(folded, 1)
                nc.vector.memset(v_pad[:], 0.0).then_inc(folded, 1)
                dve.wait_ge(folded, 4)
                nc.vector.memset(stack_tok[:, 1, :, 120:122], -SHIFT)
                nc.vector.memset(v_pad[:, :, :, :, DH:DH + 1], 1.0)
                for i in range(2):
                    nc.vector.tensor_copy(w_cl[:, i, :], max_ps[:, i, :])
                dve.wait_ge(w_loaded, 16 * len(loads))
                nc.vector.tensor_scalar(w_qkv[:, 0, :], w_qkv[:, 0, :], float(DH) ** -0.5, None, ALU.mult)

        bench_filled = sem("bench_filled")
        proj_added = sem("proj_added")
        xn_made = sem("xn_made")
        xnT_made = sem("xnT_made")
        qkv_made = sem("qkv_made")
        cl_max_made = sem("cl_max_made")
        cl_sub_made = sem("cl_sub_made")
        cl_exp_made = sem("cl_exp_made")
        cl_sum_made = sem("cl_sum_made")
        cl_inv_made = sem("cl_inv_made")
        cl_scaled = sem("cl_scaled")
        cl_share_made = sem("cl_share_made")
        hi_made = sem("hi_made")
        lo_made = sem("lo_made")
        v_made = sem("v_made")
        stack_made = sem("stack_made")
        max_scored = sem("max_scored")
        max_made = sem("max_made")
        shift_hi_made = sem("shift_hi_made")
        shift_made = sem("shift_made")
        shift_row_made = sem("shift_row_made")
        shift_placed = sem("shift_placed")
        scored = sem("scored")
        exp_made = sem("exp_made")
        pv_made = sem("pv_made")
        heads_moved = sem("heads_moved")
        inv_made = sem("inv_made")
        att_made = sem("att_made")
        att_T_made = sem("att_T_made")
        block = ctx.enter_context(nc.Block())

        def uses_up_to(n, use):
            return BENCH_ORDER[(n, use)] + 1

        @block.tensor
        def _(pe):
            def bench_is_free(n, turn, use):
                if before(n, use) is None:
                    return
                step, x = before(n, use)
                if step == "xn":
                    pe.wait_ge(xnT_made, due(x + 1, turn, 2 * TPB))
                elif step == "qkv":
                    pe.wait_ge(qkv_made, due(x + 1, turn, 2 * TPB))
                elif step in ("clq", "clk"):
                    pe.wait_ge(cl_sub_made, due(2 * x + (step == "clk") + 1, turn, 4 * TPB))
                elif step[:5] == "stack":
                    pe.wait_ge(stack_made, due(4 * x + STACKS.index(step) + 1, turn, 8 * TPB))
                elif step == "heads_out":
                    pe.wait_ge(att_made, due(x + 1, turn, 8))
                elif step == "att_t":
                    pe.wait_ge(att_T_made, due(x + 1, turn, 2))
                elif step == "proj":
                    pe.wait_ge(proj_added, due(x + 1, turn, 2))
                elif step == "shift":
                    pe.wait_ge(shift_row_made, due(x + 1, turn, 8))

            def make_scores(u, i, turn):
                par, g, kt, pr = u // SLOTS % 2, u // UNITS % 4, u % UNITS // 2, u % 2
                if u % UNITS == 0 and i == 0:
                    pe.wait_ge(shift_placed, due(32 * (u // UNITS + 1), turn, 32 * 8))
                if 2 * u + i - 1 > 0:
                    pe.wait_ge(exp_made, due(2 * u + i - 1, turn, 2 * PAIR))
                h = 4 * g + 2 * pr + i
                nc.tensor.matmul(scores_ps[:, i, :], stack[:, par, 1, h, kt * P:(kt + 1) * P],
                                 stack[:, par, 0, h, :], start=True, stop=True).then_inc(scored, 1)

            def make_max_scores(u, i, turn):
                par, g, w = u // SLOTS % 2, u // UNITS % 4, u % UNITS
                h = 4 * g + w // 2
                if u % SLOTS == 0 and i == 0:
                    pe.wait_ge(stack_made, due(16 * (u // SLOTS + 1), turn, 16 * 2))
                qt = 2 * (w % 2) + i
                if 2 * u + i - 1 > 0:
                    pe.wait_ge(max_made, due(2 * u + i - 1, turn, 2 * PAIR))
                nc.tensor.matmul(max_ps[:, i, :], stack[:, par, 0, h, qt * P:(qt + 1) * P],
                                 stack[:, par, 1, h, :], start=True, stop=True).then_inc(max_scored, 1)

            def weight_values(c, turn):
                par, g, kt = c // 16 % 2, c // 4 % 4, c % 4
                pe.wait_ge(exp_made, due(4 * c + 4, turn, 2 * PAIR))
                if kt == 0:
                    if c // 4 > 0:
                        pe.wait_ge(heads_moved, due(c // 4, turn, 8))
                    if g == 0:
                        pe.wait_ge(v_made, due(TPB * (c // 16 + 1), turn, 2 * TPB))
                for j in range(4):
                    mm = nc.tensor.matmul(heads_ps[32 * j:32 * j + 32, :],
                                          v_pad[:, par, kt, 4 * g + j, :],
                                          prob[:, c % 4, j, :],
                                          start=(kt == 0), stop=(kt == 3))
                mm.then_inc(pv_made, 1)

            def fill_bench(n, turn, use):
                bench = bench_ps[:, bank_of(n, use), :]
                bench16 = bench.bitcast(F16)
                bench_is_free(n, turn, use)
                step, x = use
                if step == "xn":
                    pe.wait_ge(xn_made, due(x + 1, turn, 2 * TPB))
                    mm = nc.tensor.transpose(bench[:, 0:P], xn[:, x % 2, :], ident[:])
                elif step == "qkv":
                    pe.wait_ge(xnT_made, due(x + 1, turn, 2 * TPB))
                    mm = nc.tensor.matmul(bench[:, 0:3 * D], xnT[:, x % 2, :],
                                          w_qkv[:].rearrange("p a b -> p (a b)"), start=True, stop=True)
                elif step in ("clq", "clk"):
                    mm = nc.tensor.matmul(bench, xnT[:, x % 2, :], w_cl[:, step == "clk", :],
                                          start=True, stop=True)
                elif step[:5] == "stack":
                    side, half = int(step[6] == "k"), int(step[7])
                    pe.wait_ge(hi_made, due(2 * x + side + 1, turn, 4 * TPB))
                    pe.wait_ge(lo_made, due(2 * x + side + 1, turn, 4 * TPB))
                    for i in range(8):
                        mm = nc.tensor.transpose(bench16[:, i * P:(i + 1) * P],
                                                 stack_tok[:, side, 8 * half + i, :], ident16[:])
                elif step == "heads_out":
                    pe.wait_ge(heads_moved, due(x + 1, turn, 8))
                    for qt in range(TPB):
                        mm = nc.tensor.transpose(bench[:, qt * P:(qt + 1) * P],
                                                 heads_raw[:, qt * P:(qt + 1) * P], ident[:])
                elif step == "att_t":
                    pe.wait_ge(att_made, due(4 * (x + 1), turn, 8))
                    for qt in range(TPB):
                        mm = nc.tensor.transpose(bench[:, qt * P:(qt + 1) * P],
                                                 att_tok[:, qt].rearrange("p h f -> p (h f)"), ident[:])
                elif step == "proj":
                    pe.wait_ge(att_T_made, due(x + 1, turn, 2))
                    for qt in range(TPB):
                        mm = nc.tensor.matmul(bench[:, qt * D:(qt + 1) * D],
                                              att_T[:, qt * P:(qt + 1) * P], w_o[:],
                                              start=True, stop=True)
                elif step == "shift":
                    pe.wait_ge(shift_made, due(x + 1, turn, 8))
                    for qt in range(TPB):
                        mm = nc.tensor.transpose(bench16[0:8, qt * P:(qt + 1) * P],
                                                 shift_tok[:, qt].rearrange("p s j -> p (s j)"), ident16[:])
                mm.then_inc(bench_filled, 1)

            def slot(n, turn):
                s, uses = streams(n), bench_uses(n)
                if s["max"] is not None:
                    make_max_scores(s["max"], 0, turn)
                for use in uses[0:1]:
                    fill_bench(n, turn, use)
                if s["scores"] is not None:
                    make_scores(s["scores"], 0, turn)
                if s["max"] is not None:
                    make_max_scores(s["max"], 1, turn)
                for use in uses[1:2]:
                    fill_bench(n, turn, use)
                if s["pv"] is not None:
                    weight_values(s["pv"], turn)
                if s["scores"] is not None:
                    make_scores(s["scores"], 1, turn)
                for use in uses[2:9]:
                    fill_bench(n, turn, use)

            over_slots(pe, slot)

        @block.vector
        def _(dve):
            def empty_bench(n, turn, use):
                step, x = use
                bench = bench_ps[:, bank_of(n, use), :]
                dve.wait_ge(bench_filled, due(uses_up_to(n, use), turn, BENCH_PER_PAIR))
                if step in ("clq", "clk"):
                    side = int(step == "clk")
                    c = 2 * x + side
                    scores = bench.rearrange("p (h n) -> p h n", n=NB)
                    nc.vector.tensor_reduce(cl_max[:, x % 2, side, :], scores, AX.X,
                                            ALU.max).then_inc(cl_max_made, 1)
                    dve.wait_ge(cl_max_made, due(c + 1, turn, 4 * TPB))
                    if c - 3 > 0:
                        dve.wait_ge(lo_made, due(c - 3, turn, 4 * TPB))
                    nc.vector.tensor_tensor(
                        cl[:, x % 2, side].rearrange("p (h n) -> p h n", n=NB), scores,
                        cl_max[:, x % 2, side, :].unsqueeze(2).to_broadcast([P, H, NB]),
                        ALU.subtract).then_inc(cl_sub_made, 1)
                elif step == "heads_out":
                    v = bench.rearrange("p (q j f) -> p q j f", q=TPB, j=4)
                    nc.vector.reciprocal(inv_sum[:], v[:, :, :, DH]).then_inc(inv_made, 1)
                    dve.wait_ge(inv_made, due(x + 1, turn, 8))
                    if x % 4 == 0:
                        if x // 4 > 0:
                            dve.wait_ge(att_T_made, due(x // 4, turn, 2))
                    nc.vector.tensor_tensor(att_tok[:, :, 4 * (x % 4):4 * (x % 4) + 4, :],
                                            v[:, :, :, 0:DH],
                                            inv_sum[:].unsqueeze(3).to_broadcast([P, TPB, 4, DH]),
                                            ALU.mult).then_inc(att_made, 1)
                elif step == "proj":
                    first = x * TPB if isinstance(turn, int) else turn * (2 * TPB) + x * TPB
                    zz = Z[:, bass.ds(first, TPB), :]
                    nc.vector.tensor_tensor(zz, bench.rearrange("p (t d) -> p t d", d=D), zz,
                                            ALU.add).then_inc(proj_added, 1)
                elif step == "shift":
                    if 32 * x > 0:
                        dve.wait_ge(shift_placed, due(32 * x, turn, 32 * 8))
                    nc.vector.tensor_copy(shift_row[:], bench.bitcast(F16)[0:8, 0:S]).then_inc(shift_row_made, 1)

            def slot(n, turn):
                s = streams(n)
                for tile, k in s["prep"]:
                    if k == 0:
                        if tile - 1 > 0:
                            dve.wait_ge(xnT_made, due(tile - 1, turn, 2 * TPB))
                        T = tile_at(turn, tile)
                        nc.vector.tensor_scalar(xn[:, tile % 2, :],
                                                Z[:, bass.ds(T, 1), :].rearrange("p t d -> p (t d)"),
                                                R1[:, bass.ds(T, 1)], None, ALU.mult).then_inc(xn_made, 1)
                uses = [use for use in bench_uses(n) if use[0] in VECTOR_EMPTIES]
                added = (n - SLOTS - 6) // SLOTS if (n - SLOTS - 6) % SLOTS == 0 and n > SLOTS else None
                if added is not None:
                    dve.wait_ge(proj_added, due(added + 1, turn, 2))
                summed = [(tile, k - 6) for tile, k in s["prep"] if k in (6, 7)]
                for tile, side in summed:
                    dve.wait_ge(cl_exp_made, due(2 * tile + side + 1, turn, 4 * TPB))
                    nc.vector.tensor_reduce(cl_sum[:, tile % 2, side, :],
                                            cl[:, tile % 2, side].rearrange("p (h n) -> p h n", n=NB),
                                            AX.X, ALU.add).then_inc(cl_sum_made, 1)
                for i in range(2):
                    if s["max"] is not None:
                        u = s["max"]
                        w, grp = u % UNITS, u // UNITS
                        dve.wait_ge(max_scored, due(2 * u + i + 1, turn, 2 * PAIR))
                        qt = 2 * (w % 2) + i
                        nc.vector.tensor_reduce(row_max[:, grp % 2, qt, w // 2:w // 2 + 1],
                                                max_ps[:, i, :], AX.X, ALU.max).then_inc(max_made, 1)
                    if added is not None and i == 0:
                        for t in range(TPB):
                            T = tile_at(turn, added * TPB + t)
                            nc.vector.bn_stats(flat(stats[:, bass.ds(T, 1), :]), flat(Z[:, bass.ds(T, 1), :]))
                    for tile, side in summed:
                        c, inv = 2 * tile + side, cl_inv[:, tile % 2, side, :]
                        if i == 0:
                            dve.wait_ge(cl_sum_made, due(c + 1, turn, 4 * TPB))
                            nc.vector.reciprocal(inv, cl_sum[:, tile % 2, side, :]).then_inc(cl_inv_made, 1)
                        elif side == 0:
                            dve.wait_ge(cl_inv_made, due(c + 1, turn, 4 * TPB))
                            nc.vector.tensor_scalar(inv, inv, 0.1, None, ALU.mult).then_inc(cl_scaled, 1)
                for use in uses:
                    empty_bench(n, turn, use)
                if s["max"] is not None and s["max"] % UNITS == UNITS - 1:
                    grp = s["max"] // UNITS
                    dve.wait_ge(max_made, due(16 * (grp + 1), turn, 16 * 8))
                    if grp > 0:
                        dve.wait_ge(shift_row_made, due(grp, turn, 8))
                    nc.vector.tensor_scalar(shift_tok[:, :, 0, :], row_max[:, grp % 2], 1.0 / SHIFT,
                                            None, ALU.mult).then_inc(shift_hi_made, 1)
                    dve.wait_ge(shift_hi_made, due(grp + 1, turn, 8))
                    nc.vector.scalar_tensor_tensor(out=shift_tok[:, :, 1, :], in0=row_max[:, grp % 2],
                                                   scalar=1.0 / SHIFT, in1=shift_tok[:, :, 0, :],
                                                   op0=ALU.mult, op1=ALU.subtract).then_inc(shift_made, 1)
                for tile, k in s["prep"]:
                    par = tile % 2
                    for side in range(2):
                        c = 2 * tile + side
                        if k == 8 + side:
                            dve.wait_ge(cl_share_made, due(c + 1, turn, 4 * TPB))
                            if 4 * (tile - 1) + 2 * side + 2 > 0:
                                dve.wait_ge(stack_made, due(4 * (tile - 1) + 2 * side + 2, turn, 8 * TPB))
                            share = cl[:, par, side].rearrange("p (h n) -> p h n", n=NB)
                            for dst in ((0, 2 * NB) if side == 0 else (0, NB)):
                                nc.vector.tensor_copy(stack_tok[:, side, :, dst:dst + NB], share)
                            feat = qkv[:, par, side].rearrange("p (h f) -> p h f", f=DH)
                            for dst in ((96, 112) if side == 0 else (96, 104)):
                                ins = nc.vector.tensor_copy(stack_tok[:, side, :, dst:dst + DH], feat)
                            ins.then_inc(hi_made, 1)

            over_slots(dve, slot)

        @block.scalar
        def _(act):
            def exponentiate(u, i, turn):
                kt_all, pr = u // 2, u % 2
                act.wait_ge(scored, due(2 * u + i + 1, turn, 2 * PAIR))
                if kt_all - 3 > 0:
                    act.wait_ge(pv_made, due(kt_all - 3, turn, PAIR // 2))
                nc.scalar.activation(prob[:, kt_all % 4, 2 * pr + i, :], scores_ps[:, i, :],
                                     ACT.Exp).then_inc(exp_made, 1)

            def empty_bench(n, turn, use):
                step, x = use
                bench = bench_ps[:, bank_of(n, use), :]
                act.wait_ge(bench_filled, due(uses_up_to(n, use), turn, BENCH_PER_PAIR))
                if step == "xn":
                    nc.scalar.activation(xnT[:, x % 2, :], bench[:, 0:P], ACT.Identity,
                                         bias=ln1[:, 1:2], scale=ln1[:, 0:1]).then_inc(xnT_made, 1)
                elif step == "qkv":
                    if x - 1 > 0:
                        act.wait_ge(v_made, due(x - 1, turn, 2 * TPB))
                    if 2 * x - 2 > 0:
                        act.wait_ge(lo_made, due(2 * x - 2, turn, 4 * TPB))
                    nc.scalar.activation(qkv[:, x % 2].rearrange("p a b -> p (a b)"), bench[:, 0:3 * D],
                                         ACT.Copy).then_inc(qkv_made, 1)
                elif step == "att_t":
                    nc.scalar.activation(att_T[:], bench, ACT.Copy).then_inc(att_T_made, 1)
                else:
                    side, half = int(step[6] == "k"), int(step[7])
                    if x % TPB == 0 and side == 0 and half == 0:
                        if 2 * SLOTS * (x // TPB - 1) > 0:
                            act.wait_ge(scored, due(2 * SLOTS * (x // TPB - 1), turn, 2 * PAIR))
                    nc.scalar.activation(
                        stack[:, x // TPB % 2, side, 8 * half:8 * half + 8, x % TPB * P:(x % TPB + 1) * P],
                        bench.bitcast(F16).rearrange("p (h t) -> p h t", h=8),
                        ACT.Copy).then_inc(stack_made, 1)

            def slot(n, turn):
                s = streams(n)
                uses = [use for use in bench_uses(n) if use[0] not in VECTOR_EMPTIES]
                if s["exp"] is not None:
                    for i in range(2):
                        exponentiate(s["exp"], i, turn)
                for tile, k in s["prep"]:
                    if k == 10:
                        act.wait_ge(qkv_made, due(tile + 1, turn, 2 * TPB))
                        if 16 * (tile // TPB - 1) > 0:
                            act.wait_ge(pv_made, due(16 * (tile // TPB - 1), turn, PAIR // 2))
                        nc.scalar.activation(v_pad[:, tile // TPB % 2, tile % TPB, :, 0:DH],
                                             qkv[:, tile % 2, 2].rearrange("p (h f) -> p h f", f=DH),
                                             ACT.Copy).then_inc(v_made, 1)
                for use in uses:
                    empty_bench(n, turn, use)
                if s["out"] is not None:
                    g = s["out"]
                    act.wait_ge(pv_made, due(4 * (g + 1), turn, PAIR // 2))
                    if g > 0:
                        act.wait_ge(att_made, due(g, turn, 8))
                    nc.scalar.activation(heads_raw[:], heads_ps[:], ACT.Copy).then_inc(heads_moved, 1)
                for tile, k in s["prep"]:
                    for side in range(2):
                        if k == 4 + side:
                            act.wait_ge(cl_sub_made, due(2 * tile + side + 1, turn, 4 * TPB))
                            e = cl[:, tile % 2, side]
                            nc.scalar.activation(e, e, ACT.Exp).then_inc(cl_exp_made, 1)

            over_slots(act, slot)

        @block.gpsimd
        def _(pool):
            def slot(n, turn):
                for tile, k in streams(n)["prep"]:
                    par = tile % 2
                    for side in range(2):
                        c = 2 * tile + side
                        share = cl[:, par, side].rearrange("p (h n) -> p h n", n=NB)
                        feat = qkv[:, par, side].rearrange("p (h f) -> p h f", f=DH)
                        if k == 6 + side:
                            if side == 0:
                                pool.wait_ge(cl_scaled, due(tile + 1, turn, 2 * TPB))
                            else:
                                pool.wait_ge(cl_inv_made, due(c + 1, turn, 4 * TPB))
                            nc.gpsimd.tensor_tensor(
                                share, share, cl_inv[:, par, side, :].unsqueeze(2).to_broadcast([P, H, NB]),
                                ALU.mult).then_inc(cl_share_made, 1)
                        if k == 8 + side:
                            pool.wait_ge(hi_made, due(c + 1, turn, 4 * TPB))
                            lo = NB if side == 0 else 2 * NB
                            nc.gpsimd.tensor_tensor(stack_tok[:, side, :, lo:lo + NB], share,
                                                    stack_tok[:, side, :, 0:NB], ALU.subtract)
                            lo = 104 if side == 0 else 112
                            nc.gpsimd.tensor_tensor(stack_tok[:, side, :, lo:lo + DH], feat,
                                                    stack_tok[:, side, :, 96:96 + DH],
                                                    ALU.subtract).then_inc(lo_made, 1)

            over_slots(pool, slot)

        @block.sync
        def _(sp):
            def slot(n, turn):
                for step, g in bench_uses(n):
                    if step == "shift":
                        sp.wait_ge(shift_row_made, due(g + 1, turn, 8))
                        heads = slice(4 * (g % 4), 4 * (g % 4) + 4)
                        for part in range(2):
                            sp.dma_start(stack[120 + part:121 + part, g // 4 % 2, 0, heads, :],
                                         shift_row[4 * part:4 * part + 4, :]).then_inc(shift_placed, 16)

            over_slots(sp, slot)


def over(eng, slot, first, loop_from, turns, period, last):
    for n in range(first, loop_from):
        slot(n, 0)
    with eng.Fori(0, turns) as turn:
        for n in range(loop_from, loop_from + period):
            slot(n, turn)
    for n in range(loop_from + turns * period, last):
        slot(n, 0)


def flat(ap):
    return ap.rearrange("p a b -> p (a b)")


def clear(nc, semaphores):
    with nc.Block() as block:
        @block.gpsimd
        def _(pool):
            for s in semaphores:
                pool.sem_clear(s)
    for s in semaphores:
        nc.release_semaphore(s)


def token_moments(nc, a, stats, mean, inv_dev, eps, tag):
    with ExitStack() as ctx:
        def sb(name, shape, dt=F32):
            return ctx.enter_context(nc.sbuf_tensor(tag + name, shape, dt))

        def sem(name):
            return a["semaphores"].enter_context(nc.semaphore(tag + name))

        moments = sb("moments", [P, NT, 2])
        dev = sb("dev", [P, NT])
        eps_col = sb("eps", [P, 1])
        moments_done = sem("moments_done")
        dev_done = sem("dev_done")
        block = ctx.enter_context(nc.Block())

        @block.vector
        def _(dve):
            nc.vector.memset(eps_col[:], eps)
            for t in range(NT):
                nc.vector.bn_aggr(moments[:, t, :], stats[:, t, :]).then_inc(moments_done, 1)
            dve.wait_ge(moments_done, NT)
            nc.vector.tensor_copy(mean[:], moments[:, :, 0])
            dve.wait_ge(dev_done, 1)
            nc.vector.reciprocal(inv_dev[:], dev[:])

        @block.scalar
        def _(act):
            act.wait_ge(moments_done, NT)
            nc.scalar.activation(dev[:], moments[:, :, 1], ACT.Sqrt, bias=eps_col[:]).then_inc(dev_done, 1)


def attention_mlp(nc, a, X, Z, mean, inv_dev, stats, weights, next_loads):
    MC = MLP // P
    with ExitStack() as ctx:
        def sb(name, shape, dt=F32):
            return ctx.enter_context(nc.sbuf_tensor("mlp_" + name, shape, dt))

        def ps(name, shape, dt=F32):
            return ctx.enter_context(nc.psum_tensor("mlp_" + name, shape, dt))

        def sem(name):
            return a["semaphores"].enter_context(nc.semaphore("mlp_" + name))

        ident, w1, w2, b1, ln2, b2_rows = (weights[x] for x in ("ident", "w1", "w2", "b1", "ln2", "b2_rows"))
        y = sb("y", [P, 2, TPB, D])
        yT = sb("yT", [P, 2, S])
        hid = sb("hid", [P, 2, MC, S])
        base = sb("base", [P, 2, TPB, D])
        t_ps = ps("t_ps", [P, S])
        h_ps = ps("h_ps", [P, MC, S])
        o_ps = ps("o_ps", [P, S])
        loaded = sem("loaded")
        y_made = sem("y_made")
        turned = sem("turned")
        yT_made = sem("yT_made")
        h_filled = sem("h_filled")
        h_made = sem("h_made")
        o_filled = sem("o_filled")
        added = sem("added")
        base_half = sem("base_half")
        base_made = sem("base_made")
        block = ctx.enter_context(nc.Block())

        def tiles(buf, b, turn):
            first = b * TPB if isinstance(turn, int) else turn * (2 * TPB) + b * TPB
            return buf[:, bass.ds(first, TPB), :]

        def run(eng, slot):
            over(eng, slot, 0, 4, 2, 2, B + 2)

        @block.sync
        def _(sp):
            for dst, src in next_loads:
                sp.dma_start(dst, src).then_inc(loaded, 16)
            sp.wait_ge(loaded, 16 * len(next_loads))

        @block.vector
        def _(dve):
            def centre(b, turn):
                if b - 1 > 0:
                    dve.wait_ge(turned, due(b - 1, turn, 2))
                for t in range(TPB):
                    T = b * TPB + t if isinstance(turn, int) else turn * (2 * TPB) + b * TPB + t
                    ins = nc.vector.tensor_scalar(y[:, b % 2, t, :], flat(Z[:, bass.ds(T, 1), :]),
                                                  mean[:, bass.ds(T, 1)], inv_dev[:, bass.ds(T, 1)],
                                                  ALU.subtract, ALU.mult)
                ins.then_inc(y_made, 1)

            centre(0, 0)

            def slot(n, turn):
                summed = n - 3
                if 0 <= summed < B:
                    dve.wait_ge(added, due(summed + 1, turn, 2))
                if 0 <= summed < B:
                    for t in range(TPB):
                        T = tile_at(turn, summed * TPB + t)
                        nc.vector.bn_stats(flat(stats[:, bass.ds(T, 1), :]), flat(X[:, bass.ds(T, 1), :]))
                b = n - 2
                if 0 <= b < B:
                    dve.wait_ge(o_filled, due(b + 1, turn, 2))
                    dve.wait_ge(base_made, due(b + 1, turn, 2))
                    nc.vector.tensor_tensor(tiles(X, b, turn), o_ps[:].rearrange("p (t d) -> p t d", d=D),
                                            base[:, b % 2], ALU.add).then_inc(added, 1)
                if n + 1 < B:
                    centre(n + 1, turn)

            over(dve, slot, 0, 3, 2, 2, B + 3)

        @block.gpsimd
        def _(pool):
            def slot(n, turn):
                b = n - 1
                if 0 <= b < B:
                    if b - 1 > 0:
                        pool.wait_ge(added, due(b - 1, turn, 2))
                    nc.gpsimd.tensor_tensor(base[:, b % 2], tiles(X, b, turn), tiles(Z, b, turn),
                                            ALU.add).then_inc(base_half, 1)
                    pool.wait_ge(base_half, due(b + 1, turn, 2))
                    nc.gpsimd.tensor_tensor(base[:, b % 2], base[:, b % 2],
                                            b2_rows[:].unsqueeze(1).to_broadcast([P, TPB, D]),
                                            ALU.add).then_inc(base_made, 1)

            run(pool, slot)

        @block.scalar
        def _(act):
            def slot(n, turn):
                b = n
                if b < B:
                    act.wait_ge(turned, due(b + 1, turn, 2))
                    if MC * (b - 1) > 0:
                        act.wait_ge(h_filled, due(MC * (b - 1), turn, 2 * MC))
                    nc.scalar.activation(yT[:, b % 2, :], t_ps[:], ACT.Identity, bias=ln2[:, 1:2],
                                         scale=ln2[:, 0:1]).then_inc(yT_made, 1)
                b = n - 1
                if 0 <= b < B:
                    for c in range(MC):
                        act.wait_ge(h_filled, due(MC * b + c + 1, turn, 2 * MC))
                        if b - 1 > 0:
                            act.wait_ge(o_filled, due(b - 1, turn, 2))
                        nc.scalar.activation(hid[:, b % 2, c, :], h_ps[:, c, :], ACT.Relu,
                                             bias=b1[:, c:c + 1]).then_inc(h_made, 1)

            run(act, slot)

        @block.tensor
        def _(pe):
            def slot(n, turn):
                b = n
                if b < B:
                    pe.wait_ge(y_made, due(b + 1, turn, 2))
                    if b > 0:
                        pe.wait_ge(yT_made, due(b, turn, 2))
                    for t in range(TPB):
                        mm = nc.tensor.transpose(t_ps[:, t * P:(t + 1) * P], y[:, b % 2, t, :], ident[:])
                    mm.then_inc(turned, 1)
                b = n - 1
                if 0 <= b < B:
                    pe.wait_ge(yT_made, due(b + 1, turn, 2))
                    for c in range(MC):
                        if MC * (b - 1) + c + 1 > 0:
                            pe.wait_ge(h_made, due(MC * (b - 1) + c + 1, turn, 2 * MC))
                        nc.tensor.matmul(h_ps[:, c, :], w1[:, c * P:(c + 1) * P], yT[:, b % 2, :],
                                         start=True, stop=True).then_inc(h_filled, 1)
                b = n - 2
                if 0 <= b < B:
                    pe.wait_ge(h_made, due(MC * (b + 1), turn, 2 * MC))
                    if b > 0:
                        pe.wait_ge(added, due(b, turn, 2))
                    for t in range(TPB):
                        for c in range(MC):
                            mm = nc.tensor.matmul(o_ps[:, t * D:(t + 1) * D],
                                                  hid[:, b % 2, c, t * P:(t + 1) * P], w2[:, c, :],
                                                  start=(c == 0), stop=(c == MC - 1))
                    mm.then_inc(o_filled, 1)

            run(pe, slot)


def turn_tokens(nc, a, X, mean, inv_dev, XT):
    with ExitStack() as ctx:
        def sem(name):
            return a["semaphores"].enter_context(nc.semaphore("turn_" + name))

        ident = ctx.enter_context(nc.sbuf_tensor("turn_ident", [P, P], F32))
        w = ctx.enter_context(nc.sbuf_tensor("turn_w", [P, 2, TPB, D], F32))
        t_ps = ctx.enter_context(nc.psum_tensor("turn_ps", [P, 2, S], F32))
        loaded, made, turned, moved = sem("loaded"), sem("made"), sem("turned"), sem("moved")
        block = ctx.enter_context(nc.Block())

        def run(eng, slot):
            for n in range(B):
                slot(n, 0)

        @block.sync
        def _(sp):
            sp.dma_start(ident[:], a["ident"]).then_inc(loaded, 16)

        @block.vector
        def _(dve):
            def slot(n, turn):
                if n - 1 > 0:
                    dve.wait_ge(turned, due(n - 1, turn, 2))
                for t in range(TPB):
                    T = n * TPB + t if isinstance(turn, int) else turn * (2 * TPB) + n * TPB + t
                    ins = nc.vector.tensor_scalar(w[:, n % 2, t, :], flat(X[:, bass.ds(T, 1), :]),
                                                  mean[:, bass.ds(T, 1)], inv_dev[:, bass.ds(T, 1)],
                                                  ALU.subtract, ALU.mult)
                ins.then_inc(made, 1)

            run(dve, slot)

        @block.tensor
        def _(pe):
            pe.wait_ge(loaded, 16)

            def slot(n, turn):
                pe.wait_ge(made, due(n + 1, turn, 2))
                if n - 1 > 0:
                    pe.wait_ge(moved, due(n - 1, turn, 2))
                for t in range(TPB):
                    mm = nc.tensor.transpose(t_ps[:, n % 2, t * P:(t + 1) * P], w[:, n % 2, t, :], ident[:])
                mm.then_inc(turned, 1)

            run(pe, slot)

        @block.scalar
        def _(act):
            def slot(n, turn):
                act.wait_ge(turned, due(n + 1, turn, 2))
                b = n if isinstance(turn, int) else turn * 2 + n
                nc.scalar.activation(flat(XT[:, bass.ds(b, 1), :]), t_ps[:, n % 2, :], ACT.Copy).then_inc(moved, 1)

            run(act, slot)


LH, LD, WIN = 8, 64, 64
INNER = LH * LD
KEYS = P + WIN
NEG = -1e30
LN_SCALE = 2.0 ** 20


def local_attention(nc, a, layer, XT, C, VAR, weights):
    tag = f"la{layer}_"
    with ExitStack() as ctx:
        def sb(name, shape, dt=F32):
            return ctx.enter_context(nc.sbuf_tensor(tag + name, shape, dt))

        def ps(name, shape, dt=F32):
            return ctx.enter_context(nc.psum_tensor(tag + name, shape, dt))

        def sem(name):
            return a["layer_semaphores"](tag + name)

        ident, identb, band = weights["ident"], weights["identb"], weights["band"]
        mean_of = weights["mean_of"]
        wqkv, wo = weights["wqkv"], weights["wo"]
        rot = sb("rot", [P, TPB, 2, 2, LD])
        hT = sb("hT", [P, 2, S])
        raw = sb("raw", [P, 2, 2, INNER])
        plain = sb("plain", [P, 2, INNER])
        swapped = sb("swapped", [P, 2, INNER])
        turned = sb("turned", [P, 2, 2, INNER])
        squares = sb("squares", [P, 2, 2, INNER])
        sumsq = sb("sumsq", [P, 2, 2 * LH])
        lnsq = sb("lnsq", [P, 2, 2 * LH])
        inv = sb("inv", [P, 2, 2 * LH])
        newton = sb("newton", [P, 2 * LH])
        q_gain = sb("q_gain", [P, 4, LH])
        half_ln = sb("half_ln", [P, 1])
        three_halves = sb("three_halves", [P, 2 * LH])
        eight = sb("eight", [P, LH])
        qT = sb("qT", [P, 2, 4, P])
        kT = sb("kT", [P, 2, 4, S])
        v1 = sb("v1", [P, 2, TPB, LH, LD + 1])
        s_max = sb("s_max", [P, 2, 4])
        s_bias = sb("s_bias", [P, 2, 4])
        prob = sb("prob", [P, 2, 4, 2 * P])
        probT = sb("probT", [P, 2, 8, P])
        o_inv = sb("o_inv", [P, 4])
        o_tok = sb("o_tok", [P, 2, INNER])
        oT = sb("oT", [P, 2, 4, S])
        shifted = sb("shifted", [P, S])
        csq = sb("csq", [P, S])
        ring_ps = ps("ring", [P, 2, S])
        s_ps = ps("s", [P, 4, 2 * P])
        pT_ps = ps("pT", [P, 8, P])
        o_ps = ps("o", [P, 4, P])
        m_ps = ps("m", [P, S])
        loaded = sem("loaded")
        ready = sem("ready")
        gained = sem("gained")
        h_made = sem("h_made")
        ring_filled = sem("ring_filled")
        raw_made = sem("raw_made")
        rot_read = sem("rot_read")
        plain_made = sem("plain_made")
        sq_made = sem("sq_made")
        v_made = sem("v_made")
        qT_made = sem("qT_made")
        kT_made = sem("kT_made")
        added_rot = sem("added_rot")
        k_scaled = sem("k_scaled")
        sum_made = sem("sum_made")
        clip_made = sem("clip_made")
        ln_made = sem("ln_made")
        seed_made = sem("seed_made")
        nt1, nt2, nt3, inv_made = sem("newton1"), sem("newton2"), sem("newton3"), sem("inv_made")
        q_gain_made = sem("q_gain_made")
        s_filled = sem("s_filled")
        max_made = sem("max_made")
        bias_made = sem("bias_made")
        exp_made = sem("exp_made")
        pT_filled = sem("pT_filled")
        pT_made = sem("pT_made")
        o_filled = sem("o_filled")
        o_inv_made = sem("o_inv_made")
        o_made = sem("o_made")
        m_filled = sem("m_filled")
        oT_made = sem("oT_made")
        x_added = sem("x_added")
        sh_made = sem("sh_made")
        c_made = sem("c_made")
        csq_made = sem("csq_made")
        var_made = sem("var_made")

        T_LAST = NT + 6
        block = ctx.enter_context(nc.Block())

        def batch_at(buf, b, turn):
            return flat(buf[:, bass.ds(b if isinstance(turn, int) else turn * 2 + b, 1), :])

        def run(eng, slot):
            over(eng, slot, 0, 15, 2, 8, T_LAST)

        RING = 5 * 8

        def ring_index(T, use):
            return 5 * T + use if use < 3 else 5 * (T + 2) + use

        def ring_used(r):
            return 0 <= r // 5 - 2 * (r % 5 >= 3) < NT

        def missing(r):
            return sum(not ring_used(x) for x in range(r))

        def m_count(T):
            if T < 0:
                return 0
            return T + 1 + 3 * (T // TPB) - (T % TPB == 0 and T > 0)

        def m_square_count(b):
            return m_count((b + 1) * TPB - 1) + (4 if b < B - 1 else 3)

        def ended(T):
            return T // TPB if 0 <= T < NT and T % TPB == TPB - 1 else None

        def place(j):
            return 2 * (j % 2) + j // 2

        def attn_tile(n):
            return n - 3 if 0 <= n - 3 < NT else None

        @block.sync
        def _(sp):
            loads = weights["ffn_loads"](layer)
            for dst, src in loads:
                sp.dma_start(dst, src).then_inc(loaded, 16)
            sp.wait_ge(loaded, 16 * len(loads))

        @block.tensor
        def _(pe):
            pe.wait_ge(ready, 1)

            def ring_free(r, turn):
                p = r - 2
                while p >= 0 and not ring_used(p):
                    p -= 2
                if p < 0:
                    return
                T, use = p // 5 - 2 * (p % 5 >= 3), p % 5
                if use < 2:
                    pe.wait_ge(raw_made, due(2 * T + use + 1, turn, 16))
                else:
                    pe.wait_ge((v_made, qT_made, kT_made)[use - 2], due(T + 1, turn, 8))

            def project(T, use, turn):
                b, t = T // TPB, T % TPB
                if t == 0 and use == 0:
                    pe.wait_ge(h_made, due(2 * (b + 1), turn, 4))
                r = ring_index(T, use)
                ring_free(r, turn)
                nc.tensor.matmul(ring_ps[:, r % 2, :], hT[:, b % 2, t * P:(t + 1) * P],
                                 wqkv[:, use * INNER:(use + 1) * INNER], start=True, stop=True
                                 ).then_inc(ring_filled, 1)

            def transpose(T, use, turn):
                r = ring_index(T, use)
                ring_free(r, turn)
                if use == 3:
                    pe.wait_ge(added_rot, due(2 * T + 1, turn, 16))
                else:
                    pe.wait_ge(k_scaled, due(T + 1, turn, 8))
                for c in range(4):
                    mm = nc.tensor.transpose(ring_ps[:, r % 2, c * P:(c + 1) * P],
                                             turned[:, T % 2, use - 3, c * P:(c + 1) * P], ident[:])
                mm.then_inc(ring_filled, 1)

            def scores(T, half, turn):
                b, t = T // TPB, T % TPB
                if half == 0:
                    pe.wait_ge(qT_made, due(T + 1, turn, 8))
                    pe.wait_ge(kT_made, due(T + 1, turn, 8))
                if 2 * T + half > 0:
                    pe.wait_ge(exp_made, due(2 * T + half, turn, 16))
                lo = WIN if t == 0 else 0
                for j in range(4):
                    h = 4 * half + j
                    e = 64 * (h % 2)
                    nc.tensor.matmul(s_ps[:, place(j), lo:KEYS], qT[e:e + 64, T % 2, h // 2, :],
                                     kT[e:e + 64, b % 2, h // 2, t * P - WIN + lo:(t + 1) * P],
                                     start=(j < 2), stop=False, skip_group_check=True)
                for j in range(4):
                    mm = nc.tensor.matmul(s_ps[:, place(j), lo:KEYS], identb[:], band[:, lo:KEYS],
                                          start=False, stop=True, skip_group_check=True)
                mm.then_inc(s_filled, 1)

            def prob_turn(T, half, turn):
                t = T % TPB
                pe.wait_ge(exp_made, due(2 * T + half + 1, turn, 16))
                if 2 * T + half > 0:
                    pe.wait_ge(pT_made, due(2 * T + half, turn, 16))
                for j in range(4):
                    for blk in range(t == 0, 2):
                        mm = nc.tensor.transpose(pT_ps[:, 2 * j + blk, :],
                                                 prob[:, half, j, blk * P:(blk + 1) * P], ident[:])
                mm.then_inc(pT_filled, 1)

            def weigh(T, half, turn):
                b, t = T // TPB, T % TPB
                pe.wait_ge(pT_made, due(2 * T + half + 1, turn, 16))
                if 2 * T + half > 0:
                    pe.wait_ge(o_made, due(2 * T + half, turn, 16))
                for j in range(4):
                    for blk in range(t == 0, 2):
                        mm = nc.tensor.matmul(o_ps[:, j, 0:LD + 1], probT[:, half, 2 * j + blk, :],
                                              v1[:, b % 2, t - 1 + blk, 4 * half + j, :],
                                              start=(blk == (t == 0)), stop=(blk == 1))
                mm.then_inc(o_filled, 1)

            def slot(n, turn):
                T = n if n < NT else None
                U, R, O = attn_tile(n), n - 2, n - 4
                if U is not None:
                    scores(U, 0, turn)
                if 0 <= O < NT:
                    prob_turn(O, 1, turn)
                if ended(n - 6) is not None:
                    b = ended(n - 6)
                    pe.wait_ge(csq_made, due(b + 1, turn, 2))
                    if b < B - 1:
                        pe.wait_ge(oT_made, due((b + 1) * TPB + 1, turn, 8))
                    nc.tensor.matmul(m_ps[:], mean_of[:], csq[:], start=True, stop=True
                                     ).then_inc(m_filled, 1)
                if T is not None:
                    project(T, 0, turn)
                    project(T, 1, turn)
                if ended(n - 5) is not None:
                    b = ended(n - 5)
                    pe.wait_ge(oT_made, due((b + 1) * TPB, turn, 8))
                    for c in range(4):
                        mm = nc.tensor.matmul(m_ps[:], wo[:, c, :], oT[:, b % 2, c, :],
                                              start=(c == 0), stop=(c == 3))
                    mm.then_inc(m_filled, 1)
                if 0 <= O < NT:
                    weigh(O, 1, turn)
                if U is not None:
                    scores(U, 1, turn)
                    prob_turn(U, 0, turn)
                if T is not None:
                    project(T, 2, turn)
                if 0 <= R < NT:
                    transpose(R, 3, turn)
                if U is not None:
                    weigh(U, 0, turn)
                if 0 <= R < NT:
                    transpose(R, 4, turn)
                if ended(n - 5) is not None:
                    pe.wait_ge(sh_made, due(2 * (ended(n - 5) + 1), turn, 4))
                    nc.tensor.matmul(m_ps[:], mean_of[:], shifted[:], start=True, stop=True
                                     ).then_inc(m_filled, 1)
                if 0 <= O < NT:
                    t, b = O % TPB, O // TPB
                    pe.wait_ge(o_made, due(2 * (O + 1), turn, 16))
                    if t == 0:
                        if b > 0:
                            pe.wait_ge(c_made, due(b, turn, 2))
                    elif t == 1 and b > 0:
                        pe.wait_ge(var_made, due(b, turn, 2))
                    else:
                        pe.wait_ge(oT_made, due(O, turn, 8))
                    for c in range(4):
                        mm = nc.tensor.transpose(m_ps[:, c * P:(c + 1) * P],
                                                 o_tok[:, O % 2, c * P:(c + 1) * P], ident[:])
                    mm.then_inc(m_filled, 1)

            run(pe, slot)

        def shift(dve, dst, src, done):
            nc.vector.tensor_scalar(dst[0:64, :], src[0:64, :], 1.0, None, ALU.mult).then_inc(done, 1)
            nc.vector.tensor_scalar(dst[64:P, 1:S], src[64:P, 0:S - 1], 1.0, None, ALU.mult).then_inc(done, 1)

        @block.vector
        def _(dve):
            nc.vector.memset(three_halves[:], 1.5)
            nc.vector.memset(eight[:], 8.0)
            nc.vector.memset(half_ln[:], 0.5 * float(np.log(LN_SCALE)))
            nc.vector.memset(hT[64:P, :, 0:1], 0.0)
            nc.vector.memset(shifted[64:P, 0:1], 0.0)
            nc.vector.memset(prob[:, :, :, 0:WIN], 0.0)
            nc.vector.memset(v1[:, :, :, :, LD:LD + 1], 1.0).then_inc(ready, 1)
            for t in range(TPB):
                nc.vector.tensor_tensor(rot[:, t], weights["rot"][:, t], weights["gains"][:],
                                        ALU.mult).then_inc(gained, 1)
            dve.wait_ge(gained, TPB)

            def halves(ap):
                return ap.rearrange("p (h w f) -> p h w f", w=2, f=LD // 2)

            def rotate(T, side, turn):
                t = T % TPB
                dve.wait_ge(raw_made, due(2 * T + side + 1, turn, 16))
                if side == 0:
                    if 2 * T - 1 > 0:
                        dve.wait_ge(added_rot, due(2 * T - 1, turn, 16))
                else:
                    if 2 * T > 0:
                        dve.wait_ge(added_rot, due(2 * T, turn, 16))
                src = raw[:, T % 2, side]
                for w in range(2):
                    ins = nc.vector.tensor_tensor(
                        halves(swapped[:, side])[:, :, w, :], halves(src)[:, :, 1 - w, :],
                        rot[:, t, side, 1, w * 32:(w + 1) * 32].unsqueeze(1).to_broadcast([P, LH, 32]), ALU.mult)
                ins.then_inc(rot_read, 1)

            def norms(T, turn):
                par = T % 2
                for side in range(2):
                    dve.wait_ge(sq_made, due(2 * T + side + 1, turn, 16))
                    nc.vector.tensor_reduce(sumsq[:, par, side * LH:(side + 1) * LH],
                                            squares[:, par, side].rearrange("p (h f) -> p h f", f=LD),
                                            AX.X, ALU.add).then_inc(sum_made, 1)
                dve.wait_ge(sum_made, due(2 * T + 2, turn, 16))
                nc.vector.tensor_scalar(sumsq[:, par], sumsq[:, par], 1e-24, -0.5, ALU.max,
                                        ALU.mult).then_inc(clip_made, 1)

            def maxima(T, half, turn):
                lo = WIN if T % TPB == 0 else 0
                dve.wait_ge(s_filled, due(2 * T + half + 1, turn, 16))
                if 2 * T + half - 1 > 0:
                    dve.wait_ge(exp_made, due(2 * T + half - 1, turn, 16))
                nc.vector.tensor_reduce(s_max[:, half], s_ps[:, :, lo:KEYS], AX.X, ALU.max).then_inc(max_made, 1)
                dve.wait_ge(max_made, due(2 * T + half + 1, turn, 16))
                if half == 0:
                    dve.wait_ge(q_gain_made, due(T + 1, turn, 8))
                by_place = q_gain[:, T % 4, 4 * half:4 * half + 4].rearrange("p (b a) -> p a b", a=2)
                nc.vector.scalar_tensor_tensor(out=s_bias[:, half].rearrange("p (a b) -> p a b", a=2),
                                               in0=s_max[:, half].rearrange("p (a b) -> p a b", a=2),
                                               scalar=-1.0, in1=by_place,
                                               op0=ALU.mult, op1=ALU.mult).then_inc(bias_made, 1)

            def take_probT(T, half, turn):
                dve.wait_ge(pT_filled, due(2 * T + half + 1, turn, 16))
                if 2 * T + half - 1 > 0:
                    dve.wait_ge(o_filled, due(2 * T + half - 1, turn, 16))
                first = T % TPB == 0
                v = pT_ps[:].rearrange("p (j s) q -> p j s q", s=2)
                o = probT[:, half].rearrange("p (j s) q -> p j s q", s=2)
                nc.vector.tensor_copy(o[:, :, first:2, :], v[:, :, first:2, :]).then_inc(pT_made, 1)

            def take_out(T, half, turn):
                dve.wait_ge(o_filled, due(2 * T + half + 1, turn, 16))
                nc.vector.reciprocal(o_inv[:], o_ps[:, :, LD]).then_inc(o_inv_made, 1)
                dve.wait_ge(o_inv_made, due(2 * T + half + 1, turn, 16))
                if half == 0:
                    if m_count(T - 2) > 0:
                        dve.wait_ge(m_filled, due(m_count(T - 2), turn, 14))
                nc.vector.tensor_tensor(
                    o_tok[:, T % 2, half * 256:(half + 1) * 256].rearrange("p (j f) -> p j f", f=LD),
                    o_ps[:, :, 0:LD], o_inv[:].unsqueeze(2).to_broadcast([P, 4, LD]),
                    ALU.mult).then_inc(o_made, 1)

            def slot(n, turn):
                U, N, R, O = attn_tile(n), n - 1, n - 2, n - 4
                if n == 0:
                    shift(dve, hT[:, 0, :], batch_at(XT, 0, turn), h_made)
                if U is not None:
                    maxima(U, 0, turn)
                if 0 <= O < NT:
                    take_probT(O, 1, turn)
                if 0 <= N < NT:
                    rotate(N, 0, turn)
                if 0 <= O < NT:
                    take_out(O, 1, turn)
                if 0 <= N < NT:
                    rotate(N, 1, turn)
                if U is not None:
                    maxima(U, 1, turn)
                    take_probT(U, 0, turn)
                b = ended(n - 5)
                if b is not None:
                    x = batch_at(XT, b, turn)
                    dve.wait_ge(m_filled, due(m_count(n - 5) + 1, turn, 14))
                    nc.vector.tensor_tensor(x, m_ps[:], x, ALU.add).then_inc(x_added, 1)
                if 0 <= N < NT:
                    norms(N, turn)
                if b is not None:
                    dve.wait_ge(x_added, due(b + 1, turn, 2))
                    shift(dve, shifted, x, sh_made)
                if 0 <= R < NT:
                    r = ring_index(R, 3)
                    dve.wait_ge(ring_filled, due(r + 1 - missing(r), turn, RING))
                    if 2 * R - 2 > 0:
                        dve.wait_ge(s_filled, due(2 * R - 2, turn, 16))
                    nc.vector.tensor_copy(qT[:, R % 2].rearrange("p c q -> p (c q)"),
                                          ring_ps[:, r % 2, :]).then_inc(qT_made, 1)
                if U is not None:
                    take_out(U, 0, turn)
                if b is not None:
                    dve.wait_ge(sh_made, due(2 * (b + 1), turn, 4))
                    dve.wait_ge(m_filled, due(m_count(n - 5) + 2, turn, 14))
                    nc.vector.tensor_tensor(batch_at(C, b, turn), shifted[:], m_ps[:],
                                            ALU.subtract).then_inc(c_made, 1)
                if n % TPB == TPB - 1 and n + 1 < NT:
                    b = (n + 1) // TPB
                    if b >= 2:
                        r = ring_index((b - 1) * TPB - 1, 2)
                        dve.wait_ge(ring_filled, due(r + 1 - missing(r), turn, RING))
                    shift(dve, hT[:, b % 2, :], batch_at(XT, b, turn), h_made)

            run(dve, slot)

        @block.scalar
        def _(act):
            nc.scalar.preload_act_table_set("natural_log_exp_and_others")
            act.wait_ge(ready, 1)

            def exps(T, half, turn):
                lo = WIN if T % TPB == 0 else 0
                act.wait_ge(bias_made, due(2 * T + half + 1, turn, 16))
                if 2 * T + half - 1 > 0:
                    act.wait_ge(pT_filled, due(2 * T + half - 1, turn, 16))
                for j in range(4):
                    ins = nc.scalar.activation(prob[:, half, j, WIN + lo:WIN + KEYS],
                                               s_ps[:, place(j), lo:KEYS], ACT.Exp,
                                               bias=s_bias[:, half, place(j):place(j) + 1],
                                               scale=q_gain[:, T % 4, 4 * half + j:4 * half + j + 1])
                ins.then_inc(exp_made, 1)

            def slot(n, turn):
                T = n if n < NT else None
                U = attn_tile(n)
                if U is not None:
                    exps(U, 0, turn)
                if T is not None:
                    for side in range(2):
                        r = ring_index(T, side)
                        act.wait_ge(ring_filled, due(r + 1 - missing(r), turn, RING))
                        if 2 * T + side - 3 > 0:
                            act.wait_ge(sum_made, due(2 * T + side - 3, turn, 16))
                        if 2 * T + side - 3 > 0:
                            act.wait_ge(rot_read, due(2 * T + side - 3, turn, 16))
                        if 2 * T + side - 3 > 0:
                            act.wait_ge(added_rot, due(2 * T + side - 3, turn, 16))
                        nc.scalar.activation(raw[:, T % 2, side], ring_ps[:, r % 2, :], ACT.Copy
                                             ).then_inc(raw_made, 1)
                        act.wait_ge(raw_made, due(2 * T + side + 1, turn, 16))
                        nc.scalar.activation(squares[:, T % 2, side], raw[:, T % 2, side], ACT.Square
                                             ).then_inc(sq_made, 1)
                if T is not None:
                    b, t = T // TPB, T % TPB
                    r = ring_index(T, 2)
                    act.wait_ge(ring_filled, due(r + 1 - missing(r), turn, RING))
                    if 8 * (b - 1) > 0:
                        act.wait_ge(o_filled, due(8 * (b - 1), turn, 16))
                    nc.scalar.activation(v1[:, b % 2, t, :, 0:LD],
                                         ring_ps[:, r % 2, :].rearrange("p (h f) -> p h f", f=LD),
                                         ACT.Copy).then_inc(v_made, 1)
                if ended(n - 6) is not None:
                    b = ended(n - 6)
                    act.wait_ge(m_filled, due(m_square_count(b), turn, 14))
                    nc.scalar.activation(batch_at(VAR, b, turn), m_ps[:], ACT.Copy).then_inc(var_made, 1)
                if U is not None:
                    exps(U, 1, turn)
                if 0 <= n - 1 < NT:
                    T = n - 1
                    act.wait_ge(clip_made, due(T + 1, turn, 8))
                    if T - 1 > 0:
                        act.wait_ge(q_gain_made, due(T - 1, turn, 8))
                    if T - 1 > 0:
                        act.wait_ge(k_scaled, due(T - 1, turn, 8))
                    nc.scalar.activation(lnsq[:, T % 2], sumsq[:, T % 2], ACT.Ln, scale=-2.0 * LN_SCALE
                                         ).then_inc(ln_made, 1)
                    act.wait_ge(ln_made, due(T + 1, turn, 8))
                    nc.scalar.activation(inv[:, T % 2], lnsq[:, T % 2], ACT.Exp, bias=half_ln[:],
                                         scale=-0.5).then_inc(seed_made, 1)
                if 0 <= n - 2 < NT:
                    T = n - 2
                    b, t = T // TPB, T % TPB
                    r = ring_index(T, 4)
                    act.wait_ge(ring_filled, due(r + 1 - missing(r), turn, RING))
                    if 8 * (b - 1) > 0:
                        act.wait_ge(s_filled, due(8 * (b - 1), turn, 16))
                    nc.scalar.activation(kT[:, b % 2, :, t * P:(t + 1) * P],
                                         ring_ps[:, r % 2, :].rearrange("p (c q) -> p c q", q=P),
                                         ACT.Copy).then_inc(kT_made, 1)
                T = n - 4
                if 0 <= T < NT:
                    b, t = T // TPB, T % TPB
                    act.wait_ge(m_filled, due(m_count(T), turn, 14))
                    nc.scalar.activation(oT[:, b % 2, :, t * P:(t + 1) * P],
                                         m_ps[:].rearrange("p (c q) -> p c q", q=P),
                                         ACT.Copy).then_inc(oT_made, 1)
                if ended(n - 5) is not None:
                    b = ended(n - 5)
                    act.wait_ge(c_made, due(b + 1, turn, 2))
                    nc.scalar.activation(csq[:], batch_at(C, b, turn), ACT.Square).then_inc(csq_made, 1)

            run(act, slot)

        @block.gpsimd
        def _(pool):
            pool.wait_ge(ready, 1)
            pool.wait_ge(gained, TPB)

            def polish(T, turn):
                par = T % 2
                pool.wait_ge(seed_made, due(T + 1, turn, 8))
                if 2 * T - 6 > 0:
                    pool.wait_ge(bias_made, due(2 * T - 6, turn, 16))
                if 2 * T - 6 > 0:
                    pool.wait_ge(exp_made, due(2 * T - 6, turn, 16))
                nc.gpsimd.tensor_tensor(newton[:], inv[:, par], inv[:, par], ALU.mult).then_inc(nt1, 1)
                pool.wait_ge(nt1, due(T + 1, turn, 8))
                nc.gpsimd.tensor_tensor(newton[:], newton[:], sumsq[:, par], ALU.mult).then_inc(nt2, 1)
                pool.wait_ge(nt2, due(T + 1, turn, 8))
                nc.gpsimd.tensor_tensor(newton[:], newton[:], three_halves[:], ALU.add).then_inc(nt3, 1)
                pool.wait_ge(nt3, due(T + 1, turn, 8))
                nc.gpsimd.tensor_tensor(inv[:, par], inv[:, par], newton[:], ALU.mult).then_inc(inv_made, 1)
                pool.wait_ge(inv_made, due(T + 1, turn, 8))
                nc.gpsimd.tensor_tensor(q_gain[:, T % 4], inv[:, par, 0:LH], eight[:],
                                        ALU.mult).then_inc(q_gain_made, 1)

            def slot(n, turn):
                T = n - 1
                if 0 <= T < NT:
                    for side in range(2):
                        pool.wait_ge(raw_made, due(2 * T + side + 1, turn, 16))
                        nc.gpsimd.tensor_tensor(
                            plain[:, side].rearrange("p (h f) -> p h f", f=LD),
                            raw[:, T % 2, side].rearrange("p (h f) -> p h f", f=LD),
                            rot[:, T % TPB, side, 0, :].unsqueeze(1).to_broadcast([P, LH, LD]),
                            ALU.mult).then_inc(plain_made, 1)
                    for side in range(2):
                        pool.wait_ge(plain_made, due(2 * T + side + 1, turn, 16))
                        pool.wait_ge(rot_read, due(2 * T + side + 1, turn, 16))
                        r = ring_index(T - 2, 3 + side)
                        if T >= 2:
                            pool.wait_ge(ring_filled, due(r + 1 - missing(r), turn, RING))
                        nc.gpsimd.tensor_tensor(turned[:, T % 2, side], plain[:, side], swapped[:, side],
                                                ALU.add).then_inc(added_rot, 1)
                    polish(T, turn)
                    pool.wait_ge(added_rot, due(2 * T + 2, turn, 16))
                    k = turned[:, T % 2, 1].rearrange("p (h f) -> p h f", f=LD)
                    nc.gpsimd.tensor_tensor(k, k, inv[:, T % 2, LH:2 * LH].unsqueeze(2).to_broadcast([P, LH, LD]),
                                            ALU.mult).then_inc(k_scaled, 1)

            over(pool, slot, 0, 15, 2, 8, NT + 1)


HID = D * 4 * 2 // 3
HC = [(c, min(P, HID - c)) for c in range(0, HID, P)]


def gated_ffn(nc, a, layer, XT, C, VAR, weights):
    tag = f"ff{layer}_"
    NC = len(HC)
    with ExitStack() as ctx:
        def sb(name, shape, dt=F32):
            return ctx.enter_context(nc.sbuf_tensor(tag + name, shape, dt))

        def ps(name, shape, dt=F32):
            return ctx.enter_context(nc.psum_tensor(tag + name, shape, dt))

        def sem(name):
            return a["layer_semaphores"](tag + name)

        w1, w2, b1, ln, b2 = (weights[x] for x in ("w1", "w2", "b1", "ln", "b2"))
        eps = sb("eps", [P, 1])
        hn = sb("hn", [P, 2, S])
        gate = sb("gate", [P, 2, NC, S])
        prod = sb("prod", [P, 2, NC, S])
        a_ps = ps("a", [P, NC, S])
        g_ps = ps("g", [P, NC, S])
        o_ps = ps("o", [P, S])
        loaded, eps_set = sem("loaded"), sem("eps_set")
        dev_made, inv_made, div_made, hn_made = sem("dev"), sem("inv"), sem("div"), sem("hn")
        a_filled, g_filled = sem("a_filled"), sem("g_filled")
        gate_made, prod_made = sem("gate_made"), sem("prod_made")
        o_filled, x_added = sem("o_filled"), sem("x_added")
        block = ctx.enter_context(nc.Block())

        def batch_at(buf, b, turn):
            return flat(buf[:, bass.ds(b if isinstance(turn, int) else turn * 2 + b, 1), :])

        def run(eng, slot):
            over(eng, slot, 0, 3, 2, 2, B + 1)

        @block.sync
        def _(sp):
            loads = weights["attention_loads"](layer + 1) if layer + 1 < DEPTH else []
            for dst, src in loads:
                sp.dma_start(dst, src).then_inc(loaded, 16)
            if loads:
                sp.wait_ge(loaded, 16 * len(loads))

        @block.vector
        def _(dve):
            nc.vector.memset(eps[:], 1e-5).then_inc(eps_set, 1)

            def invert(b, turn):
                dve.wait_ge(dev_made, due(b + 1, turn, 2))
                v = batch_at(VAR, b, turn)
                nc.vector.reciprocal(v, v).then_inc(inv_made, 1)

            def normalise(b, turn):
                c = batch_at(C, b, turn)
                dve.wait_ge(inv_made, due(b + 1, turn, 2))
                nc.vector.tensor_tensor(c, c, batch_at(VAR, b, turn), ALU.mult).then_inc(div_made, 1)
                dve.wait_ge(div_made, due(b + 1, turn, 2))
                if NC * (b - 1) > 0:
                    dve.wait_ge(a_filled, due(NC * (b - 1), turn, 2 * NC))
                nc.vector.tensor_scalar(hn[:, b % 2, :], c, ln[:, 0:1], ln[:, 1:2],
                                        ALU.mult, ALU.add).then_inc(hn_made, 1)

            def multiply(b, i, turn):
                m = HC[i][1]
                dve.wait_ge(a_filled, due(NC * b + i + 1, turn, 2 * NC))
                dve.wait_ge(gate_made, due(NC * b + i + 1, turn, 2 * NC))
                if b - 1 > 0:
                    dve.wait_ge(o_filled, due(b - 1, turn, 2))
                nc.vector.scalar_tensor_tensor(out=prod[0:m, b % 2, i, :], in0=a_ps[0:m, i, :],
                                               scalar=b1[0:m, 0, i:i + 1], in1=gate[0:m, b % 2, i, :],
                                               op0=ALU.add, op1=ALU.mult).then_inc(prod_made, 1)

            invert(0, 0)
            normalise(0, 0)
            invert(1, 0)

            def slot(n, turn):
                b = n - 2
                if 0 <= b < B:
                    dve.wait_ge(o_filled, due(b + 1, turn, 2))
                    x = batch_at(XT, b, turn)
                    nc.vector.scalar_tensor_tensor(out=x, in0=o_ps[:], scalar=b2[:, 0:1], in1=x,
                                                   op0=ALU.add, op1=ALU.add).then_inc(x_added, 1)
                if n + 2 < B:
                    invert(n + 2, turn)
                if n < B:
                    for i in range(NC - 1):
                        multiply(n, i, turn)
                if n + 1 < B:
                    normalise(n + 1, turn)
                if n < B:
                    multiply(n, NC - 1, turn)

            over(dve, slot, 0, 2, 2, 2, B + 2)

        @block.scalar
        def _(act):
            act.wait_ge(eps_set, 1)
            with act.Fori(0, B) as b:
                v = flat(VAR[:, bass.ds(b, 1), :])
                nc.scalar.activation(v, v, ACT.Sqrt, bias=eps[:]).then_inc(dev_made, 1)

            def slot(n, turn):
                b = n
                if b < B:
                    for i, (_, m) in enumerate(HC):
                        act.wait_ge(g_filled, due(NC * b + i + 1, turn, 2 * NC))
                        if NC * (b - 1) > 0:
                            act.wait_ge(prod_made, due(NC * (b - 1), turn, 2 * NC))
                        nc.scalar.activation(gate[0:m, b % 2, i, :], g_ps[0:m, i, :], ACT.Gelu,
                                             bias=b1[0:m, 1, i:i + 1]).then_inc(gate_made, 1)

            run(act, slot)

        @block.tensor
        def _(pe):

            def slot(n, turn):
                b = n
                if b < B:
                    pe.wait_ge(hn_made, due(b + 1, turn, 2))
                    for i, (c, m) in enumerate(HC):
                        if NC * (b - 1) + i + 1 > 0:
                            pe.wait_ge(prod_made, due(NC * (b - 1) + i + 1, turn, 2 * NC))
                        nc.tensor.matmul(g_ps[0:m, i, :], w1[:, HID + c:HID + c + m], hn[:, b % 2, :],
                                         start=True, stop=True).then_inc(g_filled, 1)
                        nc.tensor.matmul(a_ps[0:m, i, :], w1[:, c:c + m], hn[:, b % 2, :],
                                         start=True, stop=True).then_inc(a_filled, 1)
                b = n - 1
                if 0 <= b < B:
                    pe.wait_ge(prod_made, due(NC * (b + 1), turn, 2 * NC))
                    if b > 0:
                        pe.wait_ge(x_added, due(b, turn, 2))
                    for i, (_, m) in enumerate(HC):
                        mm = nc.tensor.matmul(o_ps[:], w2[0:m, i, :], prod[0:m, b % 2, i, :],
                                              start=(i == 0), stop=(i == NC - 1))
                    mm.then_inc(o_filled, 1)

            run(pe, slot)


def add_and_store(nc, a, X, XT):
    out_tiles = a["out"].rearrange("b (t p) d -> p b t d", p=P)
    with ExitStack() as ctx:
        def sem(name):
            return a["semaphores"].enter_context(nc.semaphore("end_" + name))

        ident = ctx.enter_context(nc.sbuf_tensor("end_ident", [P, P], F32))
        t_ps = ctx.enter_context(nc.psum_tensor("end_ps", [P, 2, S], F32))
        xt = ctx.enter_context(nc.sbuf_tensor("end_xt", [P, 2, S], F32))
        loaded, copied, turned, added, stored = (sem(x) for x in ("loaded", "copied", "turned", "added", "stored"))
        block = ctx.enter_context(nc.Block())

        def run(eng, slot):
            over(eng, slot, 0, 2, 3, 2, B)

        @block.sync
        def _(sp):
            sp.dma_start(ident[:], a["ident"]).then_inc(loaded, 16)
            for b in range(B):
                sp.wait_ge(added, b + 1)
                sp.dma_start(out_tiles[:, b], X[:, b * TPB:(b + 1) * TPB, :]).then_inc(stored, 16)
            sp.wait_ge(stored, 16 * B)

        @block.scalar
        def _(act):
            def slot(n, turn):
                if n - 1 > 0:
                    act.wait_ge(turned, due(n - 1, turn, 2))
                b = n if isinstance(turn, int) else turn * 2 + n
                nc.scalar.activation(xt[:, n % 2, :], flat(XT[:, bass.ds(b, 1), :]), ACT.Copy).then_inc(copied, 1)

            run(act, slot)

        @block.tensor
        def _(pe):
            pe.wait_ge(loaded, 16)

            def slot(n, turn):
                pe.wait_ge(copied, due(n + 1, turn, 2))
                if n - 1 > 0:
                    pe.wait_ge(added, due(n - 1, turn, 2))
                for t in range(TPB):
                    mm = nc.tensor.transpose(t_ps[:, n % 2, t * P:(t + 1) * P],
                                             xt[:, n % 2, t * P:(t + 1) * P], ident[:])
                mm.then_inc(turned, 1)

            run(pe, slot)

        @block.vector
        def _(dve):
            def slot(n, turn):
                dve.wait_ge(turned, due(n + 1, turn, 2))
                first = n * TPB if isinstance(turn, int) else turn * (2 * TPB) + n * TPB
                x = X[:, bass.ds(first, TPB), :]
                nc.vector.tensor_tensor(x, t_ps[:, n % 2, :].rearrange("p (t d) -> p t d", d=D), x,
                                        ALU.add).then_inc(added, 1)

            run(dve, slot)


def rotary_tables():
    half = np.arange(0, LD, 2, dtype=np.float32)
    inv_freq = (1.0 / 10000.0 ** (half / LD)).astype(np.float32)
    t = np.arange(S, dtype=np.float32)
    freqs = (t[:, None] * inv_freq[None, :]).astype(np.float32)
    base = ((half + 0.4 * LD) / (1.4 * LD)).astype(np.float32)
    power = ((t - S // 2) / float(WIN // 2)).astype(np.float32)
    scale = (base[None, :] ** power[:, None]).astype(np.float32)
    cos, sin = np.cos(freqs), np.sin(freqs)
    sides = []
    for c, s in ((cos * scale, sin * scale), (cos / scale, sin / scale)):
        sides.append(np.stack([np.concatenate([c, c], 1), np.concatenate([-s, s], 1)], 1))
    return np.ascontiguousarray(np.stack(sides, 1).astype(np.float32))


def band_mask():
    i, j = np.arange(P)[:, None], np.arange(KEYS)[None, :]
    return np.where((j <= i + WIN) & (j >= i), 0.0, NEG).astype(np.float32)




def kernel(**inputs):
    import numpy as _np
    import concourse.bacc as _bacc
    from concourse.bass_utils import run_bass_kernel_spmd as _run

    nc = _bacc.Bacc("TRN2", target_bir_lowering=False, num_devices=1)
    arrays = layouts(inputs)
    aps = {name: nc.dram_tensor(f"in_{name}", v.shape, mybir.dt.from_np(v.dtype), kind="ExternalInput").ap()
           for name, v in arrays.items()}
    aps["out"] = nc.dram_tensor("out", (B, S, D), F32, kind="ExternalOutput").ap()
    build(nc, aps)
    r = _run(nc, [{f"in_{k}": v for k, v in arrays.items()}], core_ids=[0])
    return r.results[0]["out"]
```
